# Optimizing a Trainium2 kernel written in Bass

```python
import numpy as np
import jax
import jax.numpy as jnp

def _softmax(x, axis=-1):
    return jax.nn.softmax(x, axis=axis)

def _gelu(x):
    return jax.nn.gelu(x, approximate=True)

def _silu(x):
    return jax.nn.silu(x)

def _sigmoid(x):
    return jax.nn.sigmoid(x)

def _layernorm(x, axis=-1, eps=1e-05):
    m = jnp.mean(x, axis=axis, keepdims=True)
    v = jnp.var(x, axis=axis, keepdims=True)
    return (x - m) / jnp.sqrt(v + eps)

def _scatter_add(tgt, idx, src, axis=0):
    return tgt.at[idx].add(src)

def _segment_sum(src, seg, n):
    return jax.ops.segment_sum(src, seg, n)
kernel_name = 'mk_xattn_ffn_d2_seqx_r8_9cecba'

def setup_inputs(seed: int=0):
    np.random.seed(seed)
    _w = jnp.asarray

    def _rec_inputs():
        import jax
        import jax.numpy as jnp
        _rk = jax.random.key(seed)
        x = 7.22e-05 + 1 * jax.random.normal(jax.random.fold_in(_rk, 1), (16, 64, 512), jnp.float32)
        _lenS = 64 - jax.random.randint(jax.random.fold_in(_rk, 7), (16,), 0, max(1, 64 // 4) + 1, jnp.int32)
        _lenS2 = 64 - jax.random.randint(jax.random.fold_in(_rk, 8), (16,), 0, max(1, 64 // 4) + 1, jnp.int32)
        _ctx_4096P = jax.random.normal(jax.random.fold_in(_rk, 11), (16, 16, 512), jnp.float32)
        _ctx_4096c = jax.random.dirichlet(jax.random.fold_in(_rk, 511), 0.3 * jnp.ones((16,), jnp.float32), (16, 64))
        _ctx_4096t = jnp.einsum('bsk,bkd->bsd', _ctx_4096c, _ctx_4096P)
        _ctx_4096t = _ctx_4096t * jax.lax.rsqrt(jnp.mean(jnp.square(_ctx_4096t)) + 1e-12) * 0.953939
        ctx_4096 = 4.13588e-05 + 0.999923 * (_ctx_4096t + 0.3 * jax.random.normal(jax.random.fold_in(_rk, 611), (16, 64, 512), jnp.float32))
        pos_BxS2 = jnp.broadcast_to(jnp.arange(64, dtype=jnp.int32), (16, 64))
        _validS = jnp.arange(64)[None, :] < _lenS[:, None]
        _validS2 = jnp.arange(64)[None, :] < _lenS2[:, None]
        _causal = jnp.tril(jnp.ones((64, 64), dtype=bool))
        mask_BxSxS2_ik0 = jnp.where(jnp.broadcast_to(_validS2[:, None, :], (16, 64, 64)), 0, 1).astype(jnp.int32)
        return (x, ctx_4096, pos_BxS2, mask_BxSxS2_ik0)
    x, ctx_4096, pos_BxS2, mask_BxSxS2_ik0 = _rec_inputs()

    def _L0_xattn_setup():
        import jax, jax.numpy as jnp
        import numpy as np
        HEADS = 8
        WINDOW = 16

        def _pointwise(W, b, t):
            return jnp.einsum('oc,bct->bot', W, t) + b[None, :, None]
        key = jax.random.key(seed)
        ks = jax.random.split(key, 10)
        B, C, T = (4, 64, 512)
        s = 0.02
        return {'x': jax.random.normal(ks[0], (B, C, T), jnp.float32), 'cond': jax.random.normal(ks[1], (B, C, T), jnp.float32), 'Wq': jax.random.normal(ks[2], (C, C), jnp.float32) * s, 'bq': jnp.zeros((C,), jnp.float32), 'Wk': jax.random.normal(ks[3], (C, C), jnp.float32) * s, 'bk': jnp.zeros((C,), jnp.float32), 'Wv': jax.random.normal(ks[4], (C, C), jnp.float32) * s, 'bv': jnp.zeros((C,), jnp.float32), 'Wo': jax.random.normal(ks[5], (C, C), jnp.float32) * s, 'bo': jnp.zeros((C,), jnp.float32)}
    _L0_xattn_all = _L0_xattn_setup()
    _L0_xattn_in = {k: v for k, v in _L0_xattn_all.items() if k in ('Wq', 'bq', 'Wk', 'bk', 'Wv', 'bv', 'Wo', 'bo')}
    del _L0_xattn_all

    def _L0_ffn_setup():
        import jax, jax.numpy as jnp
        import numpy as np
        HIDDEN = 512
        INTER = 1376
        SPARSITY = 0.5

        def _ternary_weight(key, out_dim, in_dim, sparsity):
            k_mask, k_sign = jax.random.split(key)
            nonzero = jax.random.bernoulli(k_mask, 1.0 - sparsity, (out_dim, in_dim))
            sign = jnp.where(jax.random.bernoulli(k_sign, 0.5, (out_dim, in_dim)), 1.0, -1.0)
            return (nonzero * sign).astype(jnp.float32)
        key = jax.random.key(seed)
        kx, kg, ku, kd, ksg, ksu, ksd = jax.random.split(key, 7)
        x = jax.random.normal(kx, (4, 256, HIDDEN), dtype=jnp.float32)
        Wg = _ternary_weight(kg, INTER, HIDDEN, SPARSITY)
        Wu = _ternary_weight(ku, INTER, HIDDEN, SPARSITY)
        Wd = _ternary_weight(kd, HIDDEN, INTER, SPARSITY)
        ag = jax.random.uniform(ksg, (INTER,), dtype=jnp.float32, minval=0.5, maxval=1.5) / np.sqrt(HIDDEN)
        au = jax.random.uniform(ksu, (INTER,), dtype=jnp.float32, minval=0.5, maxval=1.5) / np.sqrt(HIDDEN)
        ad = jax.random.uniform(ksd, (HIDDEN,), dtype=jnp.float32, minval=0.5, maxval=1.5) / np.sqrt(INTER)
        return {'x': x, 'Wg': Wg, 'Wu': Wu, 'Wd': Wd, 'ag': ag, 'au': au, 'ad': ad}
    _L0_ffn_all = _L0_ffn_setup()
    _L0_ffn_in = {k: v for k, v in _L0_ffn_all.items() if k in ('Wg', 'Wu', 'Wd', 'ag', 'au', 'ad')}
    del _L0_ffn_all

    def _L1_xattn_setup():
        import jax, jax.numpy as jnp
        import numpy as np
        B, S, E = (2, 256, 512)
        H, KVH, D = (32, 8, 128)
        GROUPS = H // KVH
        MAX_POS = 512
        ROPE_THETA = 10000.0

        def _rope_tables(max_pos, dim, theta):
            inv_freq = 1.0 / theta ** (jnp.arange(0, dim, 2, dtype=jnp.float32) / dim)
            t = jnp.arange(max_pos, dtype=jnp.float32)
            freqs = jnp.einsum('i,j->ij', t, inv_freq)
            emb = jnp.concatenate([freqs, freqs], axis=-1)
            return (jnp.cos(emb), jnp.sin(emb))

        def _rotate_half(x):
            x1, x2 = (x[..., :x.shape[-1] // 2], x[..., x.shape[-1] // 2:])
            return jnp.concatenate([-x2, x1], axis=-1)
        key = jax.random.key(seed)
        ks = jax.random.split(key, 8)
        scale_w = 1.0 / np.sqrt(E)
        query = jax.random.normal(ks[0], (B, S, E), dtype=jnp.float32)
        k_in = jax.random.normal(ks[1], (B, S, E), dtype=jnp.float32)
        v_in = jax.random.normal(ks[2], (B, S, E), dtype=jnp.float32)
        position_ids = jnp.broadcast_to(jnp.arange(S, dtype=jnp.int64), (B, S))
        src_mask = jnp.tril(jnp.ones((S, S), dtype=jnp.int32))
        src_mask = jnp.broadcast_to(src_mask, (B, S, S))
        Wq = jax.random.normal(ks[3], (E, H * D), dtype=jnp.float32) * scale_w
        Wk = jax.random.normal(ks[4], (E, KVH * D), dtype=jnp.float32) * scale_w
        Wv = jax.random.normal(ks[5], (E, KVH * D), dtype=jnp.float32) * scale_w
        Wo = jax.random.normal(ks[6], (H * D, E), dtype=jnp.float32) * scale_w
        return {'query': query, 'key': k_in, 'value': v_in, 'position_ids': position_ids, 'src_mask': src_mask, 'Wq': Wq, 'Wk': Wk, 'Wv': Wv, 'Wo': Wo}
    _L1_xattn_all = _L1_xattn_setup()
    _L1_xattn_in = {k: v for k, v in _L1_xattn_all.items() if k in ('Wq', 'Wk', 'Wv', 'Wo')}
    del _L1_xattn_all

    def _L1_ffn_setup():
        import jax, jax.numpy as jnp
        import numpy as np
        TOP_K = 2
        key = jax.random.key(seed)
        k1, k2, k3 = jax.random.split(key, 3)
        B, S, H, O, E = (1024, 1, 512, 512, 8)
        x = jax.random.normal(k1, (B, S, H), dtype=jnp.float32)
        gate_w = jax.random.normal(k2, (H, E), dtype=jnp.float32) * 0.02
        expert_w = jax.random.normal(k3, (E, H, O), dtype=jnp.float32) * 0.02
        return {'x': x, 'gate_w': gate_w, 'expert_w': expert_w}
    _L1_ffn_all = _L1_ffn_setup()
    _L1_ffn_in = {k: v for k, v in _L1_ffn_all.items() if k in ('gate_w', 'expert_w')}
    del _L1_ffn_all
    return {'x': x, 'ctx_4096': ctx_4096, 'pos_BxS2': pos_BxS2, 'mask_BxSxS2_ik0': mask_BxSxS2_ik0, 'L0_xattn_Wq': _L0_xattn_in['Wq'], 'L0_xattn_bq': _L0_xattn_in['bq'], 'L0_xattn_Wk': _L0_xattn_in['Wk'], 'L0_xattn_bk': _L0_xattn_in['bk'], 'L0_xattn_Wv': _L0_xattn_in['Wv'], 'L0_xattn_bv': _L0_xattn_in['bv'], 'L0_xattn_Wo': _L0_xattn_in['Wo'], 'L0_xattn_bo': _L0_xattn_in['bo'], 'L0_ffn_Wg': _L0_ffn_in['Wg'], 'L0_ffn_Wu': _L0_ffn_in['Wu'], 'L0_ffn_Wd': _L0_ffn_in['Wd'], 'L0_ffn_ag': _L0_ffn_in['ag'], 'L0_ffn_au': _L0_ffn_in['au'], 'L0_ffn_ad': _L0_ffn_in['ad'], 'L1_xattn_Wq': _L1_xattn_in['Wq'], 'L1_xattn_Wk': _L1_xattn_in['Wk'], 'L1_xattn_Wv': _L1_xattn_in['Wv'], 'L1_xattn_Wo': _L1_xattn_in['Wo'], 'L1_ffn_gate_w': _L1_ffn_in['gate_w'], 'L1_ffn_expert_w': _L1_ffn_in['expert_w']}

def reference(x, ctx_4096, pos_BxS2, mask_BxSxS2_ik0, L0_xattn_Wq, L0_xattn_bq, L0_xattn_Wk, L0_xattn_bk, L0_xattn_Wv, L0_xattn_bv, L0_xattn_Wo, L0_xattn_bo, L0_ffn_Wg, L0_ffn_Wu, L0_ffn_Wd, L0_ffn_ag, L0_ffn_au, L0_ffn_ad, L1_xattn_Wq, L1_xattn_Wk, L1_xattn_Wv, L1_xattn_Wo, L1_ffn_gate_w, L1_ffn_expert_w):
    import jax
    import jax.numpy as jnp

    def _L0_xattn_ref(x, cond, Wq, bq, Wk, bk, Wv, bv, Wo, bo):
        import jax, jax.numpy as jnp
        import numpy as np
        HEADS = 8
        WINDOW = 16

        def _pointwise(W, b, t):
            return jnp.einsum('oc,bct->bot', W, t) + b[None, :, None]
        B, C, T = x.shape
        H, W = (HEADS, WINDOW)
        hd = C // H
        scale = hd ** (-0.5)
        pad_left = W // 2
        pad_right = W - pad_left - 1
        q = _pointwise(Wq, bq, x)
        k = _pointwise(Wk, bk, cond)
        v = _pointwise(Wv, bv, cond)
        k = jnp.pad(k, ((0, 0), (0, 0), (pad_left, pad_right)))
        v = jnp.pad(v, ((0, 0), (0, 0), (pad_left, pad_right)))
        idx = jnp.arange(T)[:, None] + jnp.arange(W)[None, :]
        k_win = k[:, :, idx].reshape(B, H, hd, T, W)
        v_win = v[:, :, idx].reshape(B, H, hd, T, W)
        qh = q.reshape(B, H, hd, T)
        dots = jnp.einsum('bhdt,bhdtw->bhtw', qh, k_win) * scale
        attn = jax.nn.softmax(dots, axis=-1)
        out = jnp.einsum('bhtw,bhdtw->bhdt', attn, v_win)
        out = out.reshape(B, C, T)
        return _pointwise(Wo, bo, out)

    def _L0_ffn_ref(x, Wg, Wu, Wd, ag, au, ad):
        import jax, jax.numpy as jnp
        import numpy as np
        HIDDEN = 512
        INTER = 1376
        SPARSITY = 0.5

        def _ternary_weight(key, out_dim, in_dim, sparsity):
            k_mask, k_sign = jax.random.split(key)
            nonzero = jax.random.bernoulli(k_mask, 1.0 - sparsity, (out_dim, in_dim))
            sign = jnp.where(jax.random.bernoulli(k_sign, 0.5, (out_dim, in_dim)), 1.0, -1.0)
            return (nonzero * sign).astype(jnp.float32)
        gate = jnp.einsum('bsh,ih->bsi', x, Wg) * ag
        up = jnp.einsum('bsh,ih->bsi', x, Wu) * au
        h = jax.nn.silu(gate) * up
        out = jnp.einsum('bsi,hi->bsh', h, Wd) * ad
        return out

    def _L1_xattn_ref(query, key, value, position_ids, src_mask, Wq, Wk, Wv, Wo):
        import jax, jax.numpy as jnp
        import numpy as np
        B, S, E = (2, 256, 512)
        H, KVH, D = (32, 8, 128)
        GROUPS = H // KVH
        MAX_POS = 512
        ROPE_THETA = 10000.0

        def _rope_tables(max_pos, dim, theta):
            inv_freq = 1.0 / theta ** (jnp.arange(0, dim, 2, dtype=jnp.float32) / dim)
            t = jnp.arange(max_pos, dtype=jnp.float32)
            freqs = jnp.einsum('i,j->ij', t, inv_freq)
            emb = jnp.concatenate([freqs, freqs], axis=-1)
            return (jnp.cos(emb), jnp.sin(emb))

        def _rotate_half(x):
            x1, x2 = (x[..., :x.shape[-1] // 2], x[..., x.shape[-1] // 2:])
            return jnp.concatenate([-x2, x1], axis=-1)
        nb, q_len, _ = query.shape
        q = (query @ Wq).reshape(nb, q_len, H, D).transpose(0, 2, 1, 3)
        k = (key @ Wk).reshape(nb, q_len, KVH, D).transpose(0, 2, 1, 3)
        v = (value @ Wv).reshape(nb, q_len, KVH, D).transpose(0, 2, 1, 3)
        cos_t, sin_t = _rope_tables(MAX_POS, D, ROPE_THETA)
        cos = cos_t[position_ids][:, None]
        sin = sin_t[position_ids][:, None]
        q = q * cos + _rotate_half(q) * sin
        k = k * cos + _rotate_half(k) * sin
        k = jnp.repeat(k, GROUPS, axis=1)
        v = jnp.repeat(v, GROUPS, axis=1)
        scores = jnp.einsum('bhqd,bhkd->bhqk', q, k) / jnp.sqrt(jnp.float32(D))
        mask = src_mask[:, None]
        scores = jnp.where(mask == 0, jnp.float32(-1000000000.0), scores)
        attn = jax.nn.softmax(scores, axis=-1)
        x = jnp.einsum('bhqk,bhkd->bhqd', attn, v)
        x = x.transpose(0, 2, 1, 3).reshape(nb, q_len, H * D)
        return x @ Wo

    def _L1_ffn_ref(x, gate_w, expert_w):
        import jax, jax.numpy as jnp
        import numpy as np
        TOP_K = 2
        E = gate_w.shape[-1]
        logits = jnp.einsum('bsh,he->bse', x, gate_w)
        topv, topi = jax.lax.top_k(logits, TOP_K)
        w = jax.nn.softmax(topv, axis=-1)
        onehot = jax.nn.one_hot(topi, E, dtype=x.dtype)
        w_e = jnp.einsum('bske,bsk->bse', onehot, w)
        out = jnp.einsum('bsh,eho,bse->bso', x, expert_w, w_e)
        return out
    x = x + _L0_xattn_ref(_layernorm(x, axis=-1), ctx_4096, L0_xattn_Wq, L0_xattn_bq, L0_xattn_Wk, L0_xattn_bk, L0_xattn_Wv, L0_xattn_bv, L0_xattn_Wo, L0_xattn_bo)
    x = x + _L0_ffn_ref(_layernorm(x, axis=-1), L0_ffn_Wg, L0_ffn_Wu, L0_ffn_Wd, L0_ffn_ag, L0_ffn_au, L0_ffn_ad)
    x = x + _L1_xattn_ref(_layernorm(x, axis=-1), ctx_4096, ctx_4096, pos_BxS2, mask_BxSxS2_ik0, L1_xattn_Wq, L1_xattn_Wk, L1_xattn_Wv, L1_xattn_Wo)
    x = x + _L1_ffn_ref(_layernorm(x, axis=-1), L1_ffn_gate_w, L1_ffn_expert_w)
    return x

_drawn_inputs = setup_inputs


def setup_inputs(seed=0):
    import zlib

    import numpy as np

    out = dict(_drawn_inputs(seed))
    spreads = {'L0_xattn_bq': (0.0, 0.8),
     'L0_xattn_bk': (0.0, 0.8),
     'L0_xattn_bv': (0.0, 0.8),
     'L0_xattn_bo': (0.0, 0.1)}
    factors = {'L0_xattn_Wq': 8.0, 'L0_xattn_Wk': 8.0, 'L0_xattn_Wv': 5.51, 'L0_xattn_Wo': 4.605}
    for name, (base, spread) in spreads.items():
        noise = np.random.default_rng([zlib.crc32(name.encode()), seed]).standard_normal(out[name].shape)
        drawn = base * np.exp(spread * noise) if base else spread * noise
        out[name] = jnp.asarray(drawn.astype(out[name].dtype))
    for name, factor in factors.items():
        out[name] = (out[name] * factor).astype(out[name].dtype)
    return out
```

```python
from contextlib import ExitStack

import concourse.bass as bass
import numpy as np
from concourse import mybir

F32 = mybir.dt.float32
F32R = mybir.dt.float32r
I32 = mybir.dt.int32
U32 = mybir.dt.uint32
ALU = mybir.AluOpType
ACT = mybir.ActivationFunctionType
AX_X = mybir.AxisListType.X

P = 128
BATCH, SEQ, E = 16, 64, 512
TT = BATCH * SEQ // P
EC = E // P
EPS = 1e-5

WH, WD, WIN = 8, 8, 16
BLK = 16
KEYS = 2 * BLK
PAD = WIN // 2
UNIT_T = 128
UNITS_PER_TILE = E // UNIT_T

INTER = 1376
IT = -(-INTER // P)

HEADS, KVH, HD = 32, 8, 128
GRP = HEADS // KVH
MAX_POS, THETA = 512, 10000.0
MASKED = -1e9

EXPERTS = 8

C_ID, C_HM, C_HH, C_BAND, C_IOTA, C_END = np.cumsum([0, P, WH, WH // 2, KEYS, EXPERTS]).tolist()


def shape_constants():
    c = np.zeros((P, C_END), np.float32)
    p = np.arange(P)
    c[:, C_ID:C_HM] = np.eye(P)
    c[:, C_HM:C_HH] = (p[:, None] % SEQ) // WD == np.arange(WH)
    c[:, C_HH:C_BAND] = (p[:, None] % (SEQ // 2)) // WD == np.arange(WH // 2)
    j, t = np.arange(KEYS), p % BLK
    inside = (j[None] >= t[:, None]) & (j[None] < t[:, None] + WIN)
    c[:, C_BAND:C_IOTA] = np.where(inside, 0.0, -1e30)
    c[:, C_IOTA:C_END] = np.arange(EXPERTS)
    return c


def rotary_table():
    inv = (1.0 / np.float32(THETA) ** (np.arange(0, HD, 2, dtype=np.float32) / np.float32(HD))).astype(np.float32)
    f = np.arange(MAX_POS, dtype=np.float32)[:, None] * inv[None]
    return np.concatenate([np.cos(f), np.sin(f)], -1).astype(np.float32)


def live(n, total):
    return not isinstance(n, int) or 0 <= n < total


def pipeline(eng, step, begin, loop_begin, loop_end, end, body, per):
    assert (loop_end - loop_begin) % body == 0
    for n in range(begin, loop_begin):
        step(n, n % body, n // per)
    with eng.Fori(0, (loop_end - loop_begin) // body) as i:
        for u in range(body):
            step(i * body + (loop_begin + u), (loop_begin + u) % body, i * (body // per) + (loop_begin + u) // per)
    for n in range(loop_end, end):
        step(n, n % body, n // per)


def mm3(nc, out, l_hi, l_lo, r_hi, r_lo, first, last):
    nc.tensor.matmul(out, l_hi, r_hi, start=first, stop=False)
    nc.tensor.matmul(out, l_hi, r_lo, start=False, stop=False)
    return nc.tensor.matmul(out, l_lo, r_hi, start=False, stop=last)


class Shared:
    pass


def allocator(nc, stack):
    def sb(name, shape, dt=F32):
        return stack.enter_context(nc.sbuf_tensor(name, shape, dt))

    def sem(name):
        return stack.enter_context(nc.semaphore(name))

    return sb, sem


def norm_stats(nc, vec, src, tiles, stats, mv, veps, sem_stats, sem_aggr, sem_veps, loaded=None):
    for t in tiles:
        if loaded:
            vec.wait_ge(loaded[t], 16)
        nc.vector.bn_stats(stats[:, t, :], src[:, t, :]).then_inc(sem_stats, 1)
    for t in tiles:
        vec.wait_ge(sem_stats, t + 1)
        nc.vector.bn_aggr(mv[:, t, :], stats[:, t, :]).then_inc(sem_aggr, 1)
    vec.wait_ge(sem_aggr, tiles[-1] + 1)
    some = slice(tiles[0], tiles[-1] + 1)
    nc.vector.tensor_scalar(veps[:, some], mv[:, some, 1], EPS, None, ALU.add).then_inc(sem_veps, 1)


def transpose_rows(nc, sh, name, src, hi, lo, norm):
    with ExitStack() as st:
        sb, sem = allocator(nc, st)
        stats = sb(name + "_stats", [P, TT, 6])
        mv = sb(name + "_mv", [P, TT, 2])
        veps = sb(name + "_veps", [P, TT])
        std = sb(name + "_std", [P, TT])
        rstd = sb(name + "_rstd", [P, TT])
        xn = sb(name + "_xn", [P, 2, E])
        s_stats, s_aggr, s_veps, s_std, s_rstd = (sem(name + x) for x in ("_s", "_a", "_v", "_d", "_r"))
        normed, transposed, hi_done, lo_done = (sem(name + x) for x in ("_normed", "_tr", "_hi", "_lo"))
        ident = sh.const[:, C_ID:C_HM]

        with nc.Block() as block:
            @block.vector
            def _(vec):
                if norm:
                    norm_stats(nc, vec, src, range(TT), stats, mv, veps, s_stats, s_aggr, s_veps)
                    vec.wait_ge(s_std, 1)
                    nc.vector.reciprocal(rstd[:], std[:]).then_inc(s_rstd, 1)
                    vec.wait_ge(s_rstd, 1)

                def normalise(t):
                    if t >= 2:
                        vec.wait_ge(transposed, t - 1)
                    nc.vector.tensor_scalar(xn[:, t % 2, :], src[:, t, :], mv[:, t, 0:1], rstd[:, t:t + 1],
                                            ALU.subtract, ALU.mult).then_inc(normed, 1)

                if norm:
                    normalise(0)
                for t in range(TT):
                    if norm and t + 1 < TT:
                        normalise(t + 1)
                    vec.wait_ge(hi_done, t + 1)
                    tok = slice(t * P, (t + 1) * P)
                    nc.vector.tensor_tensor(lo[:, :, tok],
                                            sh.PS[:, t % 2, :].rearrange("p (c n) -> p c n", c=EC),
                                            hi[:, :, tok].bitcast(F32), ALU.subtract).then_inc(lo_done, 1)

            @block.scalar
            def _(act):
                if norm:
                    act.wait_ge(s_veps, 1)
                    nc.scalar.activation(std[:], veps[:], ACT.Sqrt).then_inc(s_std, 1)
                for t in range(TT):
                    act.wait_ge(transposed, t + 1)
                    nc.scalar.activation(hi[:, :, t * P:(t + 1) * P],
                                         sh.PS[:, t % 2, :].rearrange("p (c n) -> p c n", c=EC),
                                         ACT.Copy).then_inc(hi_done, 1)

            @block.tensor
            def _(pe):
                for t in range(TT):
                    if norm:
                        pe.wait_ge(normed, t + 1)
                    if t >= 2:
                        pe.wait_ge(lo_done, t - 1)
                    for c in range(EC):
                        rows = (xn[:, t % 2, :] if norm else src[:, t, :])[:, c * P:(c + 1) * P]
                        last = nc.tensor.transpose(sh.PS[:, t % 2, c * P:(c + 1) * P], rows, ident)
                    last.then_inc(transposed, 1)


def window_attention(nc, sh, d):
    UNITS = TT * UNITS_PER_TILE
    STEPS = (-4, 8, 24, UNITS + 6, 8, UNITS_PER_TILE)
    HH = WH // 2
    FIRST = 2
    with ExitStack() as st:
        sb, sem = allocator(nc, st)
        ident = sh.const[:, C_ID:C_HM]
        hm = sh.const[:, C_HM:C_HH]
        hh4 = sh.const[:, C_HH:C_BAND]
        band = sh.const[:, C_BAND:C_IOTA]

        stats, mv = sb("wa_stats", [P, TT, 6]), sb("wa_mv", [P, TT, 2])
        veps, std, rstd = sb("wa_veps", [P, TT]), sb("wa_std", [P, TT]), sb("wa_rstd", [P, TT])
        wrow = sb("wa_wrow", [P, 4, P])
        wT = sb("wa_wT", [P, 4, P])
        bias = sb("wa_bias", [P, 4])
        xn = sb("wa_xn", [P, 2, E])
        qp = sb("wa_qp", [P, E])
        qx = sb("wa_qx", [P, 2, E // BLK, WH, BLK])
        kp = sb("wa_kp", [P, 2, PAD + E + PAD])
        vp = sb("wa_vp", [P, 2, PAD + E + PAD])
        sm = sb("wa_sm", [P, 4, 2 * 2 * 4, KEYS])
        mx, su, rc = (sb("wa_" + x, [P, 4, 16]) for x in ("mx", "su", "rc"))
        pt = sb("wa_pt", [P, 2, 2, 2, P])
        vt = sb("wa_vt", [P, 2, 2, P])
        oh = sb("wa_oh", [P, 2, UNIT_T])

        SC = sh.PS[:, 0:2, 0:256]
        OH = sh.PS[:, 2:6, 0:2 * HH * BLK]
        CT = [sh.PS[:, 2, :], sh.PS[:, 3, :]]
        VT = sh.PS[:, 6, 0:256]
        AO = sh.PS[:, 6, 256:256 + UNIT_T]
        PJ = sh.PS[:, 7, :]

        x_loaded = [sem(f"wa_x{t}") for t in range(TT)]
        ctx_loaded = [sem(f"wa_ctx{t}") for t in range(TT)]
        names = ("const_loaded loaded zeroed padded ct_tr ct_hi ct_lo w_tr w_ready stats aggr veps std rstd normed "
                 "q_mm k_mm v_mm q_biased q_ready k_ready v_ready sc_mm keyed banded maxed subbed exped summed recip probs "
                 "rowed vt_mm vt_copied oh_mm selected oh_copied ao_mm x_added").split()
        S = {x: sem("wa_" + x) for x in names}

        with nc.Block() as block:
            @block.sync
            def _(sp):
                for t in range(TT):
                    for dst, name, done in ((sh.X, "x", x_loaded), (sh.CTX, "ctx", ctx_loaded)):
                        sp.dma_start(dst[:, t, :],
                                     d[name][2 * t:2 * t + 2, :, :].rearrange("b s e -> (b s) e")).then_inc(done[t], 16)

            @block.tensor
            def _(pe):
                pe.wait_ge(S["const_loaded"], 16)
                pe.wait_ge(S["loaded"], 256)
                for i in range(4):
                    last = nc.tensor.transpose(PJ[:, i * P:(i + 1) * P], wrow[:, i, :], ident)
                last.then_inc(S["w_tr"], 1)
                pe.wait_ge(S["w_ready"], 1)

                def project_context(t, which, done):
                    ctx = sh.CTX[:, bass.ds(t, 1), :].rearrange("p a e -> p (a e)")
                    nc.tensor.matmul(PJ, wT[:, which, :], ctx, start=True, stop=True).then_inc(done, 1)

                def step(n, u, t):
                    q = u % 4
                    if live(t + 1, TT):
                        if q == 0:
                            if not isinstance(t, int) or t >= 0:
                                pe.wait_ge(S["v_ready"], t + 1)
                            pe.wait_ge(S["normed"], t + 2)
                            nc.tensor.matmul(PJ, wT[:, 0, :], xn[:, (u // 4 + 1) % 2, :],
                                             start=True, stop=True).then_inc(S["q_mm"], 1)
                        if q == 1:
                            pe.wait_ge(S["q_biased"], t + 2)
                            project_context(t + 1, 1, S["k_mm"])
                        if q == 2:
                            pe.wait_ge(S["k_ready"], t + 2)
                            project_context(t + 1, 2, S["v_mm"])
                    c = n + 4
                    if isinstance(n, int) and c < TT:
                        pe.wait_ge(ctx_loaded[c], 16)
                        if c >= 2:
                            pe.wait_ge(S["ct_lo"], c - 1)
                        for k in range(EC):
                            last = nc.tensor.transpose(CT[c % 2][:, k * P:(k + 1) * P], sh.CTX[:, c, k * P:(k + 1) * P], ident)
                        last.then_inc(S["ct_tr"], 1)
                    if live(n, UNITS):
                        pe.wait_ge(S["q_ready"], t + 1)
                        pe.wait_ge(S["k_ready"], t + 1)
                        if not isinstance(n, int) or n >= 1:
                            pe.wait_ge(S["keyed"], n)
                    m, w = n - 3, (u - 3) % 8
                    if live(m, UNITS):
                        slot, qm = w // 4, w % 4
                        pe.wait_ge(S["v_ready"], t + 1 if q >= 3 else t)
                        if not isinstance(n, int) or m >= 1:
                            pe.wait_ge(S["vt_copied"], m)
                        if not isinstance(n, int) or m >= 3:
                            pe.wait_ge(S["x_added"], m - 2)
                        for g in range(2):
                            t0 = qm * UNIT_T + g * BLK
                            last = nc.tensor.transpose(VT[:, g * P:(g + 1) * P], vp[:, slot, t0:t0 + P], ident)
                        last.then_inc(S["vt_mm"], 1)
                    if live(n, UNITS):
                        for g in range(2):
                            for i in range(4):
                                for b2 in range(2):
                                    rows = slice(b2 * SEQ, (b2 + 1) * SEQ)
                                    blk = 8 * q + 2 * i + g
                                    last = nc.tensor.matmul(
                                        SC[i * KEYS:(i + 1) * KEYS, b2, g * P:(g + 1) * P],
                                        kp[rows, u // 4, blk * BLK:blk * BLK + KEYS],
                                        qx[rows, u // 4, blk, :, :].rearrange("p h t -> p (h t)"),
                                        start=True, stop=True)
                        last.then_inc(S["sc_mm"], 1)
                    m = n - 4
                    if live(m, UNITS):
                        pe.wait_ge(S["rowed"], m + 1)
                        pe.wait_ge(S["vt_copied"], m + 1)
                        if not isinstance(n, int) or m >= 1:
                            pe.wait_ge(S["oh_copied"], m)
                        else:
                            pe.wait_ge(S["ct_lo"], TT)
                    m = n - 5
                    if live(m, UNITS):
                        pe.wait_ge(S["oh_copied"], m + 1)
                        pe.wait_ge(S["vt_copied"], m + 3 if live(m + 2, UNITS) else UNITS)
                        if not isinstance(n, int) or m >= 1:
                            pe.wait_ge(S["x_added"], m)
                        nc.tensor.matmul(AO, wT[:, 3, :], oh[:, (u - 5) % 2, :], start=True, stop=True).then_inc(S["ao_mm"], 1)
                    m = n - 4
                    if live(m, UNITS):
                        for g in range(2):
                            for quarter in range(4):
                                for i in range(4):
                                    rows = slice(i * KEYS, (i + 1) * KEYS)
                                    chan = slice(quarter * 32, (quarter + 1) * 32)
                                    b2, half = quarter // 2, quarter % 2
                                    out = OH[chan, i, :].rearrange("p (h g t) -> p h g t", h=HH, g=2)[:, :, g, :]
                                    last = nc.tensor.matmul(out, vt[rows, u % 2, g, chan],
                                                            pt[rows, u % 2, b2, g, half * HH * BLK:(half + 1) * HH * BLK],
                                                            start=True, stop=True)
                        last.then_inc(S["oh_mm"], 1)

                pipeline(pe, step, *STEPS)

            @block.vector
            def _(vec):
                def statistics(k, tiles):
                    norm_stats(nc, vec, sh.X, tiles, stats, mv, veps, S["stats"], S["aggr"], S["veps"], x_loaded)
                    some = slice(tiles[0], tiles[-1] + 1)
                    vec.wait_ge(S["std"], k)
                    nc.vector.reciprocal(rstd[:, some], std[:, some]).then_inc(S["rstd"], 1)
                    vec.wait_ge(S["rstd"], k)

                statistics(1, range(FIRST))
                vec.wait_ge(S["const_loaded"], 16)
                vec.wait_ge(S["loaded"], 256)
                vec.wait_ge(S["w_tr"], 1)
                nc.vector.tensor_copy(wT[:].rearrange("p a b -> p (a b)"), PJ).then_inc(S["w_ready"], 1)

                def normalise(t, slot):
                    if not isinstance(t, int) or t >= 2:
                        vec.wait_ge(S["q_mm"], t - 1)
                    one = bass.ds(t, 1)
                    nc.vector.tensor_scalar(xn[:, slot:slot + 1, :], sh.X[:, one, :], mv[:, one, 0], rstd[:, one],
                                            ALU.subtract, ALU.mult).then_inc(S["normed"], 1)

                def add_bias(t, which, mm, dst, ready):
                    vec.wait_ge(S[mm], t + 1)
                    nc.vector.tensor_scalar(dst, PJ, bias[:, which:which + 1], None, ALU.add).then_inc(S[ready], 1)

                normalise(0, 0)
                vec.wait_ge(S["padded"], 4)

                def step(n, u, t):
                    q, slot = u % 4, u // 4
                    c = n + 4
                    if isinstance(n, int) and n == 0:
                        statistics(2, range(FIRST, TT))
                    if isinstance(n, int) and c < TT:
                        vec.wait_ge(S["ct_hi"], c + 1)
                        tok = slice(c * P, (c + 1) * P)
                        nc.vector.tensor_tensor(sh.CTl[:, :, tok], CT[c % 2].rearrange("p (c n) -> p c n", c=EC),
                                                sh.CTh[:, :, tok].bitcast(F32), ALU.subtract).then_inc(S["ct_lo"], 1)
                    m, w = n - 1, (u - 1) % 4
                    if live(m, UNITS):
                        vec.wait_ge(S["banded"], m + 1)
                        nc.vector.reduce_max(mx[:, w, :], sm[:, w, :, :], AX_X).then_inc(S["maxed"], 1)
                    if live(t + 1, TT):
                        if q == 0:
                            if not isinstance(t, int) or t >= 0:
                                vec.wait_ge(S["q_ready"], t + 1)
                            add_bias(t + 1, 0, "q_mm", qp[:], "q_biased")
                        if q == 1:
                            add_bias(t + 1, 1, "k_mm", kp[:, 1 - slot, PAD:PAD + E], "k_ready")
                        if q == 2:
                            if not isinstance(t, int) or t >= 1:
                                vec.wait_ge(S["vt_mm"], 4 * t)
                            add_bias(t + 1, 2, "v_mm", vp[:, 1 - slot, PAD:PAD + E], "v_ready")
                    if q == 3 and live(t + 2, TT) and (not isinstance(t, int) or t >= -1):
                        normalise(t + 2, slot)
                    m, w = n - 2, (u - 2) % 4
                    if live(m, UNITS):
                        vec.wait_ge(S["exped"], m + 1)
                        nc.vector.reduce_sum(su[:, w, :], sm[:, w, :, :], AX_X).then_inc(S["summed"], 1)
                        vec.wait_ge(S["summed"], m + 1)
                        nc.vector.reciprocal(rc[:, w, :], su[:, w, :]).then_inc(S["recip"], 1)
                    m, w = n - 3, (u - 3) % 4
                    if live(m, UNITS):
                        vec.wait_ge(S["probs"], m + 1)
                        if not isinstance(n, int) or m >= 2:
                            vec.wait_ge(S["oh_mm"], m - 1)
                        nc.vector.transpose(pt[:, w % 2, :, :, :].rearrange("p b g x -> p (b g x)"),
                                            sm[:, w, :, :].rearrange("p a k -> p (a k)")).then_inc(S["rowed"], 1)
                    if live(n, UNITS):
                        vec.wait_ge(S["sc_mm"], n + 1)
                        if not isinstance(n, int) or n >= 4:
                            vec.wait_ge(S["rowed"], n - 3)
                        nc.vector.transpose(sm[:, u % 4, :, :].rearrange("p (b x) k -> p b (x k)", b=2),
                                            SC).then_inc(S["keyed"], 1)
                    m, w = n - 5, (u - 5) % 4
                    if live(m, UNITS):
                        vec.wait_ge(S["ao_mm"], m + 1)
                        x = sh.X[:, bass.ds(t - 1 if q >= 1 else t - 2, 1),
                                 w * UNIT_T:(w + 1) * UNIT_T]
                        nc.vector.scalar_tensor_tensor(x, AO.rearrange("p (a e) -> p a e", a=1), bias[:, 3:4], x,
                                                       ALU.add, ALU.add).then_inc(S["x_added"], 1)
                    m = n - 4
                    if live(m, UNITS):
                        vec.wait_ge(S["oh_mm"], m + 1)
                        if not isinstance(n, int) or m >= 2:
                            vec.wait_ge(S["ao_mm"], m - 1)
                        own = oh[:, u % 2, :].rearrange("p (i x) -> p i x", i=4)
                        for h in range(HH):
                            part = OH[:, :, h * 2 * BLK:(h + 1) * 2 * BLK]
                            if h == 0:
                                nc.vector.tensor_scalar(own, part, hh4[:, h:h + 1], None, ALU.mult).then_inc(S["selected"], 1)
                            else:
                                vec.wait_ge(S["selected"], (HH - 1) * m + h)
                                nc.vector.scalar_tensor_tensor(own, part, hh4[:, h:h + 1], own, ALU.mult,
                                                               ALU.add).then_inc(S["selected" if h < HH - 1 else "oh_copied"], 1)

                pipeline(vec, step, *STEPS)

            @block.gpsimd
            def _(gp):
                nc.gpsimd.memset(wrow[:], 0.0).then_inc(S["zeroed"], 1)
                for padded in (kp, vp):
                    nc.gpsimd.memset(padded[:, :, 0:PAD], 0.0).then_inc(S["padded"], 1)
                    nc.gpsimd.memset(padded[:, :, PAD + E:], 0.0).then_inc(S["padded"], 1)
                gp.wait_ge(S["const_loaded"], 16)

                def step(n, u, t):
                    m, w = n - 1, (u - 1) % 4
                    if live(m, UNITS):
                        gp.wait_ge(S["maxed"], m + 1)
                        s = sm[:, w, :, :]
                        nc.gpsimd.tensor_tensor(s, s, mx[:, w, :].unsqueeze(2).broadcast_to([P, 16, KEYS]),
                                                ALU.subtract).then_inc(S["subbed"], 1)
                    m, w = n - 2, (u - 2) % 4
                    if live(m, UNITS):
                        gp.wait_ge(S["recip"], m + 1)
                        s = sm[:, w, :, :]
                        nc.gpsimd.tensor_tensor(s, s, rc[:, w, :].unsqueeze(2).broadcast_to([P, 16, KEYS]),
                                                ALU.mult).then_inc(S["probs"], 1)
                    if live(n, UNITS):
                        gp.wait_ge(S["keyed"], n + 1)
                        s = sm[:, u % 4, :, :]
                        nc.gpsimd.tensor_tensor(s, s, band.unsqueeze(1).broadcast_to([P, 16, KEYS]),
                                                ALU.add).then_inc(S["banded"], 1)

                pipeline(gp, step, *STEPS)

            @block.scalar
            def _(act):
                act.dma_start(sh.const[:], d["consts"]).then_inc(S["const_loaded"], 16)
                act.wait_ge(S["zeroed"], 1)
                for i, w in enumerate(("Wq", "Wk", "Wv", "Wo")):
                    for b in range(2):
                        half = slice(b * SEQ, (b + 1) * SEQ)
                        act.dma_start(wrow[half, i, half], d["L0_" + w]).then_inc(S["loaded"], 16)
                        act.dma_start(bias[half, i:i + 1],
                                      d["L0_b" + w[1]].rearrange("(p a) -> p a", a=1)).then_inc(S["loaded"], 16)

                def deviations(k, tiles):
                    some = slice(tiles[0], tiles[-1] + 1)
                    act.wait_ge(S["veps"], k)
                    nc.scalar.activation(std[:, some], veps[:, some], ACT.Sqrt).then_inc(S["std"], 1)

                deviations(1, range(FIRST))
                act.wait_ge(S["const_loaded"], 16)

                def step(n, u, t):
                    q, slot = u % 4, u // 4
                    c = n + 4
                    if isinstance(n, int) and c < TT:
                        act.wait_ge(S["ct_tr"], c + 1)
                        nc.scalar.activation(sh.CTh[:, :, c * P:(c + 1) * P], CT[c % 2].rearrange("p (c n) -> p c n", c=EC),
                                             ACT.Copy).then_inc(S["ct_hi"], 1)
                    if isinstance(n, int) and n == 0:
                        deviations(2, range(FIRST, TT))
                    m = n - 3
                    if live(m, UNITS):
                        act.wait_ge(S["vt_mm"], m + 1)
                        if not isinstance(n, int) or m >= 2:
                            act.wait_ge(S["oh_mm"], m - 1)
                        nc.scalar.activation(vt[:, (u - 3) % 2, :, :].rearrange("p g x -> p (g x)"), VT,
                                             ACT.Copy).then_inc(S["vt_copied"], 1)
                    m, w = n - 1, (u - 1) % 4
                    if live(m, UNITS):
                        act.wait_ge(S["subbed"], m + 1)
                        nc.scalar.activation(sm[:, w, :, :], sm[:, w, :, :], ACT.Exp, scale=WD ** -0.5).then_inc(S["exped"], 1)
                    if q >= 1 and live(t + 1, TT):
                        if q == 1:
                            act.wait_ge(S["q_biased"], t + 2)
                            if not isinstance(t, int) or t >= 1:
                                act.wait_ge(S["sc_mm"], 4 * t)
                        for h in range(3 * q - 3, min(3 * q, WH)):
                            last = nc.scalar.activation(qx[:, 1 - slot, :, h, :], qp[:].rearrange("p (k t) -> p k t", t=BLK),
                                                        ACT.Copy, scale=hm[:, h:h + 1])
                        if q == 3:
                            last.then_inc(S["q_ready"], 1)

                pipeline(act, step, *STEPS)


def gated_ffn(nc, sh, d):
    HALF = TT * P // 2
    STEPS = (0, 4, 10, IT + 2, 2, 2)
    with ExitStack() as st:
        sb, sem = allocator(nc, st)
        ident = sh.const[:, C_ID:C_HM]
        graw, uraw = (sb("ff_" + x, [P, 2, E]) for x in ("graw", "uraw"))
        draw = sb("ff_draw", [P, 2, EC, P])
        gT, uT, dT = ([sb(f"ff_{x}T{part}", [P, 2, E], F32R) for part in ("h", "l")] for x in "gud")
        agu = sb("ff_agu", [P, IT, 2])
        col = sb("ff_col", [P, 2, 2])
        ad = sb("ff_ad", [P, E])
        sg = sb("ff_sg", [P, 2, HALF])
        hf = sb("ff_hf", [P, 2, HALF])
        hh, hl = (sb("ff_h" + x, [P, 2, 2 * HALF], F32R) for x in "hl")
        F = sb("ff_F", [P, TT, E])

        T = [sh.PS[:, 0, :], sh.PS[:, 1, :]]
        G, U = sh.PS[:, 2, :], sh.PS[:, 3, :]
        D = sh.PS[:, 4:8, :]

        names = ("loaded0 loaded1 scales zeroed agu_zeroed columns g_tr u_tr d_tr g_hi u_hi d_hi g_split u_split d_split "
                 "g_mm u_mm silu gated h_hi h_split d_mm added scaled").split()
        S = {x: sem("ff_" + x) for x in names}

        def width(i):
            return INTER - (IT - 1) * P if isinstance(i, int) and i == IT - 1 else P

        with nc.Block() as block:
            @block.sync
            def _(sp):
                def load(i, slot):
                    w = width(i)
                    done = S[f"loaded{slot}"]
                    rows = bass.ds(i * P, w)
                    sp.dma_start(graw[:w, slot, :], d["L0_Wg"][rows, :]).then_inc(done, 16)
                    sp.dma_start(uraw[:w, slot, :], d["L0_Wu"][rows, :]).then_inc(done, 16)
                    sp.dma_start(draw[:, slot, :, :w],
                                 d["L0_Wd"].rearrange("(c p) i -> p c i", p=P)[:, :, rows]).then_inc(done, 16)

                load(0, 0)
                load(1, 1)
                full = IT - 1
                sp.wait_ge(S["agu_zeroed"], 1)
                for name, dst in (("L0_ag", agu[:, :, 0]), ("L0_au", agu[:, :, 1])):
                    sp.dma_start(dst[:, 0:full], d[name][0:full * P].rearrange("(i p) -> p i", p=P),
                                 allow_slow_non_contiguous=True).then_inc(S["scales"], 16)
                    sp.dma_start(dst[:width(full), full:IT],
                                 d[name][full * P:INTER].rearrange("(p a) -> p a", a=1),
                                 allow_slow_non_contiguous=True).then_inc(S["scales"], 16)
                sp.dma_start(ad[:], d["L0_ad"].partition_broadcast(P)).then_inc(S["scales"], 16)
                with sp.Fori(0, 4) as i:
                    for u in range(2):
                        sp.wait_ge(S["d_tr"], 2 * i + u + 1)
                        load(2 * i + u + 2, u)
                sp.wait_ge(S["d_tr"], IT - 2)
                load(IT - 1, (IT - 1) % 2)

            @block.tensor
            def _(pe):
                def transposes(bank, raw, slot, w, done):
                    for c in range(EC):
                        if raw is draw:
                            last = nc.tensor.transpose(bank[:w, c * P:(c + 1) * P], raw[:, slot, c, :w], ident)
                        else:
                            last = nc.tensor.transpose(bank[:, c * P:c * P + w], raw[:w, slot, c * P:(c + 1) * P],
                                                       ident[:w, :w])
                    last.then_inc(S[done], 1)

                def inner(out, wT, slot, half, w):
                    tok = slice(half * HALF, (half + 1) * HALF)
                    for c in range(EC):
                        cols = slice(c * P, c * P + w)
                        last = mm3(nc, out[:w, :], wT[0][:, slot, cols], wT[1][:, slot, cols],
                                   sh.NTh[:, c, tok], sh.NTl[:, c, tok], c == 0, c == EC - 1)
                    return last

                def down(i, slot, tiles, w):
                    for t in tiles:
                        if not isinstance(i, int) or 8 * i + t >= 4:
                            pe.wait_ge(S["added"], 8 * i + (t - 3))
                        tok = slice(t * P, (t + 1) * P)
                        mm3(nc, D[:, t % 4, :], hh[:w, slot, tok], hl[:w, slot, tok],
                            dT[0][:w, slot, :], dT[1][:w, slot, :], True, True).then_inc(S["d_mm"], 1)

                def step(s, u, j):
                    i, o = s - 1, s - 2
                    past = not isinstance(s, int)
                    if live(s, IT):
                        pe.wait_ge(S[f"loaded{u}"], 48 * j + 48)
                        if past or s >= 2:
                            pe.wait_ge(S["d_split"], s - 1)
                        elif s == 1:
                            pe.wait_ge(S["g_split"], 1)
                        transposes(T[0], graw, u, width(s), "g_tr")
                    if live(i, IT):
                        pe.wait_ge(S["g_split"], i + 1)
                        if past or i >= 1:
                            pe.wait_ge(S["silu"], 2 * i)
                        inner(G, gT, 1 - u, 0, width(i)).then_inc(S["g_mm"], 1)
                    if live(o, IT):
                        pe.wait_ge(S["h_split"], 2 * o + 2)
                        pe.wait_ge(S["d_split"], o + 1)
                        down(o, u, (0, 1), width(o))
                    if live(s, IT):
                        if past or s >= 1:
                            pe.wait_ge(S["u_split"], s)
                        transposes(T[1], uraw, u, width(s), "u_tr")
                    if live(i, IT):
                        pe.wait_ge(S["u_split"], i + 1)
                        if past or i >= 1:
                            pe.wait_ge(S["gated"], 2 * i)
                        inner(U, uT, 1 - u, 0, width(i)).then_inc(S["u_mm"], 1)
                    if live(o, IT):
                        down(o, u, (2, 3), width(o))
                    if live(i, IT):
                        pe.wait_ge(S["g_split"], min(s + 1, IT) if isinstance(s, int) else s + 1)
                        transposes(T[0], draw, 1 - u, width(i), "d_tr")
                        pe.wait_ge(S["silu"], 2 * i + 1)
                        inner(G, gT, 1 - u, 1, width(i)).then_inc(S["g_mm"], 1)
                    if live(o, IT):
                        down(o, u, (4, 5), width(o))
                    if live(i, IT):
                        pe.wait_ge(S["gated"], 2 * i + 1)
                        inner(U, uT, 1 - u, 1, width(i)).then_inc(S["u_mm"], 1)
                    if live(o, IT):
                        down(o, u, (6, 7), width(o))

                pipeline(pe, step, *STEPS)

            @block.scalar
            def _(act):
                def high(bank, wT, slot, w, tr, done, free, rows=P):
                    act.wait_ge(*tr)
                    if free:
                        act.wait_ge(*free)
                    src, dst = bank.rearrange("p (c n) -> p c n", c=EC), wT[0][:, slot, :].rearrange("p (c n) -> p c n", c=EC)
                    nc.scalar.activation(dst[:rows, :, :w], src[:rows, :, :w], ACT.Copy).then_inc(S[done], 1)

                def silu(i, half, w, column):
                    act.wait_ge(S["g_mm"], 2 * i + half + 1)
                    if not isinstance(i, int) or i >= 1:
                        act.wait_ge(S["gated"], 2 * i + half - 1)
                    act.wait_ge(S["columns"], i + 1)
                    nc.scalar.activation(sg[:w, half, :], G[:w, :], ACT.Silu, scale=column).then_inc(S["silu"], 1)

                def h_high(i, slot, half, w):
                    act.wait_ge(S["gated"], 2 * i + half + 1)
                    if not isinstance(i, int) or i >= 2:
                        act.wait_ge(S["d_mm"], 8 * i - 8)
                    nc.scalar.activation(hh[:w, slot, half * HALF:(half + 1) * HALF], hf[:w, half, :],
                                         ACT.Copy).then_inc(S["h_hi"], 1)

                def step(s, u, j):
                    i = s - 1
                    past = not isinstance(s, int)
                    if live(s, IT):
                        high(T[0], gT, u, width(s), (S["g_tr"], s + 1), "g_hi",
                             (S["g_mm"], 2 * s - 2) if past or s >= 2 else None)
                    if live(i, IT):
                        a = col[:width(i), 1 - u, 0:1]
                        silu(i, 0, width(i), a)
                    if live(s, IT):
                        high(T[1], uT, u, width(s), (S["u_tr"], s + 1), "u_hi",
                             (S["u_mm"], 2 * s - 2) if past or s >= 2 else None)
                    if live(i, IT):
                        h_high(i, 1 - u, 0, width(i))
                        high(T[0], dT, 1 - u, P, (S["d_tr"], i + 1), "d_hi",
                             (S["d_mm"], 8 * i - 8) if past or i >= 2 else None, width(i))
                        silu(i, 1, width(i), a)
                        h_high(i, 1 - u, 1, width(i))

                pipeline(act, step, *STEPS)

            @block.vector
            def _(vec):
                vec.wait_ge(S["scales"], 80)
                vec.wait_ge(S["zeroed"], 1)

                def low(bank, wT, slot, w, hi, done, rows=P):
                    vec.wait_ge(*hi)
                    src = bank.rearrange("p (c n) -> p c n", c=EC)[:rows, :, :w]
                    hi_part, dst = (x[:, slot, :].rearrange("p (c n) -> p c n", c=EC)[:rows, :, :w] for x in wT)
                    nc.vector.tensor_tensor(dst, src, hi_part.bitcast(F32), ALU.subtract).then_inc(S[done], 1)

                def gate(i, half, w, column):
                    vec.wait_ge(S["u_mm"], 2 * i + half + 1)
                    vec.wait_ge(S["silu"], 2 * i + half + 1)
                    if not isinstance(i, int) or i >= 1:
                        vec.wait_ge(S["h_split"], 2 * i + half - 1)
                    nc.vector.scalar_tensor_tensor(hf[:w, half, :], U[:w, :], column, sg[:w, half, :],
                                                   ALU.mult, ALU.mult).then_inc(S["gated"], 1)

                def add_down(o, tiles):
                    for t in tiles:
                        vec.wait_ge(S["d_mm"], 8 * o + t + 1)
                        nc.vector.tensor_tensor(F[:, t, :], F[:, t, :], D[:, t % 4, :], ALU.add).then_inc(S["added"], 1)

                def step(s, u, j):
                    i, o = s - 1, s - 2
                    past = not isinstance(s, int)
                    if live(s, IT):
                        low(T[0], gT, u, width(s), (S["g_hi"], s + 1), "g_split")
                    if live(o, IT):
                        add_down(o, (0, 1))
                    if live(s, IT):
                        low(T[1], uT, u, width(s), (S["u_hi"], s + 1), "u_split")
                    if live(i, IT):
                        a = col[:width(i), 1 - u, 1:2]
                        gate(i, 0, width(i), a)
                    if live(o, IT):
                        add_down(o, (2, 3))
                    if live(i, IT):
                        low(T[0], dT, 1 - u, P, (S["d_hi"], i + 1), "d_split", width(i))
                    if live(o, IT):
                        add_down(o, (4, 5))
                    if live(i, IT):
                        gate(i, 1, width(i), a)
                    if live(o, IT):
                        add_down(o, (6, 7))

                pipeline(vec, step, *STEPS)
                for t in range(TT):
                    vec.wait_ge(S["added"], 8 * (IT - 1) + t + 1)
                    nc.vector.tensor_tensor(F[:, t, :], F[:, t, :], ad[:], ALU.mult).then_inc(S["scaled"], 1)
                for t in range(TT):
                    vec.wait_ge(S["scaled"], t + 1)
                    nc.vector.tensor_tensor(sh.X[:, t, :], sh.X[:, t, :], F[:, t, :], ALU.add)

            @block.gpsimd
            def _(gp):
                nc.gpsimd.memset(F[:], 0.0).then_inc(S["zeroed"], 1)
                nc.gpsimd.memset(agu[:], 0.0).then_inc(S["agu_zeroed"], 1)
                gp.wait_ge(S["scales"], 80)

                def h_low(i, slot, half, w):
                    gp.wait_ge(S["h_hi"], 2 * i + half + 1)
                    tok = slice(half * HALF, (half + 1) * HALF)
                    nc.gpsimd.tensor_tensor(hl[:w, slot, tok], hf[:w, half, :], hh[:w, slot, tok].bitcast(F32),
                                            ALU.subtract).then_inc(S["h_split"], 1)

                def step(s, u, j):
                    if live(s, IT):
                        if not isinstance(s, int) or s >= 2:
                            gp.wait_ge(S["gated"], 2 * s - 2)
                        nc.gpsimd.tensor_copy(col[:, u, :], agu[:, bass.ds(s, 1), :].rearrange("p a b -> p (a b)")
                                              ).then_inc(S["columns"], 1)
                    if live(s - 1, IT):
                        h_low(s - 1, 1 - u, 0, width(s - 1))
                        h_low(s - 1, 1 - u, 1, width(s - 1))

                pipeline(gp, step, *STEPS)


def cross_attention(nc, sh, d):
    UNITS = KVH * TT
    AHEAD = 8
    STEPS = (-AHEAD, 8, UNITS - AHEAD, UNITS + 4, 16, TT)
    QC = GRP * HD
    KVC = 2 * HD
    with ExitStack() as st:
        sb, sem = allocator(nc, st)
        ident = sh.const[:, C_ID:C_HM]
        raw = sb("ca_raw", [P, EC, QC])
        kvraw = sb("ca_kvraw", [P, EC, KVC])
        wq, wo = ([sb(f"ca_{x}{part}", [P, 2, EC, QC], F32R) for part in ("h", "l")] for x in ("wq", "wo"))
        wkv = [sb(f"ca_wkv{part}", [P, 2, EC, KVC], F32R) for part in ("h", "l")]
        rot = sb("ca_rot", [P, TT, HD])
        cap = sb("ca_cap", [P, TT, P])
        qr = sb("ca_qr", [P, (GRP + 1) * HD])
        sn = sb("ca_sn", [P, (GRP + 1) * HD])
        qT = sb("ca_qT", [P, QC])
        kT = sb("ca_kT", [P, P])
        V = sb("ca_V", [P, 4, HD])
        sm = sb("ca_sm", [P, 2, 2 * 2, SEQ])
        mx, su, rc = (sb("ca_" + x, [P, 2, 4]) for x in ("mx", "su", "rc"))
        pT = sb("ca_pT", [P, 2 * P])
        aT = [sb(f"ca_aT{part}", [P, GRP, P], F32R) for part in ("h", "l")]

        QKV = sh.PS[:, 0:2, :].rearrange("p a b -> p (a b)")
        QT = sh.PS[:, 2, :]
        KP = sh.PS[:, 3, 2 * P:3 * P]
        PP = sh.PS[:, 3, 0:2 * P]
        SC = sh.PS[:, 4, 0:4 * SEQ]
        AV = sh.PS[:, 5:7, 0:2 * P]
        O = sh.PS[:, 7, :]

        names = ("raw0 raw1 raw2 raw3 kv_loaded mask_loaded pos_loaded rot_loaded masked w_hi w_split "
                 "qkv_mm cosed rope_read roped v_copied tr_mm qT_copied kT_copied "
                 "sc_mm capped maxed subbed exped summed recip probs pp_mm pp_copied av_mm av_hi av_lo o_mm added").split()
        S = {x: sem("ca_" + x) for x in names}
        mi = sb("ca_mi", [P, TT * P], I32)
        pi = sb("ca_pi", [P, TT], I32)

        def gp_of(u):
            return u // 8 % 2

        with nc.Block() as block:
            @block.sync
            def _(sp):
                def load_q(g, p):
                    sp.dma_start(raw[:, p, :], d["L1_Wq"][p * P:(p + 1) * P, bass.ds(g * QC, QC)]).then_inc(S[f"raw{p}"], 16)

                def load_o(g, p):
                    sp.dma_start(raw[:, p, :], d["L1_Wo"][bass.ds(g * QC + p * P, P), :]).then_inc(S[f"raw{p}"], 16)

                def load_kv(g):
                    for x, name in enumerate(("L1_Wk", "L1_Wv")):
                        sp.dma_start(kvraw[:, :, x * HD:(x + 1) * HD],
                                     d[name][:, bass.ds(g * HD, HD)].rearrange("(c p) n -> p c n", p=P)).then_inc(S["kv_loaded"], 16)

                for p in range(EC):
                    load_q(0, p)
                load_kv(0)
                for h2 in range(2):
                    sp.dma_start(mi[h2 * SEQ:(h2 + 1) * SEQ, :].rearrange("p (b k) -> p b k", k=SEQ),
                                 d["mask"].rearrange("b q k -> q b k")).then_inc(S["mask_loaded"], 16)
                for p in range(EC):
                    sp.wait_ge(S["w_split"], p + 1)
                    load_o(0, p)
                with sp.Fori(1, KVH) as g:
                    for p in range(EC):
                        sp.wait_ge(S["w_split"], 8 * g - 3 + p)
                        load_q(g, p)
                    load_kv(g)
                    for p in range(EC):
                        sp.wait_ge(S["w_split"], 8 * g + p + 1)
                        load_o(g, p)

            def split_source(n, u, g):
                w = (u + AHEAD) % 16
                p, par = w % 8, w // 8
                if p < EC:
                    return [(raw[:, p, :], [x[:, par, p, :] for x in wq], (S[f"raw{p}"], 32 * g + 16))]
                p -= EC
                return [(kvraw[:, p, :], [x[:, par, p, :] for x in wkv], (S["kv_loaded"], 32 * g + 32)),
                        (raw[:, p, :], [x[:, par, p, :] for x in wo], (S[f"raw{p}"], 32 * g + 32))]

            @block.tensor
            def _(pe):
                def step(n, u, g):
                    past = not isinstance(n, int)
                    t = u % TT
                    m = n - 1
                    if live(m, UNITS):
                        pe.wait_ge(S["roped"], m + 1)
                        if past or m >= 1:
                            pe.wait_ge(S["qT_copied"], m)
                        if past or m >= 2:
                            pe.wait_ge(S["pp_copied"], m - 1)
                        for h in range(GRP):
                            out = QT[:, h // 2 * 2 * P:(h // 2 + 1) * 2 * P].rearrange("p (b m q) -> p b m q", b=2, m=2)[:, :, h % 2, :]
                            nc.tensor.transpose(out, qr[:, h * HD:(h + 1) * HD], ident)
                        nc.tensor.transpose(KP, qr[:, QC:QC + HD], ident).then_inc(S["tr_mm"], 1)
                    if live(n, UNITS):
                        par = gp_of(u)
                        if t == 0:
                            pe.wait_ge(S["w_split"], 8 * g + 8)
                        if past or n >= 1:
                            pe.wait_ge(S["rope_read"], n)
                            pe.wait_ge(S["v_copied"], n)
                        tok = slice(t * P, (t + 1) * P)
                        for c in range(EC):
                            mm3(nc, QKV[:, QC:QC + KVC], sh.CTh[:, c, tok], sh.CTl[:, c, tok],
                                wkv[0][:, par, c, :], wkv[1][:, par, c, :], c == 0, c == EC - 1)
                        for c in range(EC):
                            last = mm3(nc, QKV[:, 0:QC], sh.NTh[:, c, tok], sh.NTl[:, c, tok],
                                       wq[0][:, par, c, :], wq[1][:, par, c, :], c == 0, c == EC - 1)
                        last.then_inc(S["qkv_mm"], 1)
                    if live(m, UNITS):
                        pe.wait_ge(S["qT_copied"], m + 1)
                        pe.wait_ge(S["kT_copied"], m + 1)
                        if past or m >= 1:
                            pe.wait_ge(S["capped"], m)
                        for hp in range(2):
                            for b2 in range(2):
                                c0 = (2 * hp + b2)
                                last = nc.tensor.matmul(SC[:, c0 * SEQ:(c0 + 1) * SEQ], qT[:, c0 * P:(c0 + 1) * P],
                                                        kT[:, b2 * SEQ:(b2 + 1) * SEQ], start=True, stop=True)
                        last.then_inc(S["sc_mm"], 1)
                    m = n - 2
                    if live(m, UNITS):
                        pe.wait_ge(S["probs"], m + 1)
                        pe.wait_ge(S["kT_copied"], m + 2 if live(m + 1, UNITS) else UNITS)
                        if past or m >= 1:
                            pe.wait_ge(S["pp_copied"], m)
                        for hp in range(2):
                            last = nc.tensor.transpose(PP[:, hp * P:(hp + 1) * P],
                                                       sm[:, u % 2, 2 * hp:2 * hp + 2, :].rearrange("p b k -> p (b k)"), ident)
                        last.then_inc(S["pp_mm"], 1)
                    m = n - 3
                    if live(m, UNITS):
                        par = gp_of(u - 3)
                        pe.wait_ge(S["av_lo"], m + 1)
                        if past or m >= 1:
                            pe.wait_ge(S["added"], m)
                        for h in range(GRP):
                            last = mm3(nc, O, aT[0][:, h, :], aT[1][:, h, :], wo[0][:, par, h, :], wo[1][:, par, h, :],
                                       h == 0, h == GRP - 1)
                        last.then_inc(S["o_mm"], 1)
                    m = n - 2
                    if live(m, UNITS):
                        pe.wait_ge(S["pp_copied"], m + 1)
                        if past or m >= 1:
                            pe.wait_ge(S["av_lo"], m)
                        for b2 in range(2):
                            rows = slice(b2 * SEQ, (b2 + 1) * SEQ)
                            last = nc.tensor.matmul(AV[:, b2, :], V[rows, (u - 2) % 4, :], pT[rows, :], start=True, stop=True)
                        last.then_inc(S["av_mm"], 1)

                pipeline(pe, step, *STEPS)

            @block.scalar
            def _(act):
                def step(n, u, g):
                    past = not isinstance(n, int)
                    m = n - 2
                    if live(m, UNITS):
                        act.wait_ge(S["subbed"], m + 1)
                        s = sm[:, u % 2, :, :]
                        nc.scalar.activation(s, s, ACT.Exp).then_inc(S["exped"], 1)
                    m = n - 3
                    if live(m, UNITS):
                        act.wait_ge(S["av_mm"], m + 1)
                        for b2 in range(2):
                            last = nc.scalar.activation(aT[0][:, :, b2 * SEQ:(b2 + 1) * SEQ],
                                                        AV[:, b2, :].rearrange("p (h q) -> p h q", h=GRP), ACT.Copy)
                        last.then_inc(S["av_hi"], 1)
                    m = n - 1
                    if live(m, UNITS):
                        act.wait_ge(S["tr_mm"], m + 1)
                        if past or m >= 1:
                            act.wait_ge(S["sc_mm"], m)
                        nc.scalar.activation(kT[:], KP, ACT.Copy).then_inc(S["kT_copied"], 1)
                        nc.scalar.activation(qT[:], QT, ACT.Copy).then_inc(S["qT_copied"], 1)
                    if live(n + AHEAD, UNITS):
                        if u % 8 == 0 and (past or n >= 8):
                            act.wait_ge(S["qkv_mm"], 8 * g)
                            act.wait_ge(S["o_mm"], 8 * g - 8)
                        if u % 8 == 4 and (past or n >= 8):
                            act.wait_ge(S["o_mm"], 8 * g)
                        for src, dst, loaded in split_source(n, u, g + 1):
                            act.wait_ge(*loaded)
                            last = nc.scalar.activation(dst[0], src, ACT.Copy)
                        last.then_inc(S["w_hi"], 1)
                    if live(n, UNITS):
                        act.wait_ge(S["rope_read"], n + 1)
                        if past or n >= 4:
                            act.wait_ge(S["av_mm"], n - 3)
                        nc.scalar.activation(V[:, u % 4, :], QKV[:, QC + HD:QC + KVC], ACT.Copy).then_inc(S["v_copied"], 1)
                    m = n - 2
                    if live(m, UNITS):
                        act.wait_ge(S["pp_mm"], m + 1)
                        if past or m >= 1:
                            act.wait_ge(S["av_mm"], m)
                        nc.scalar.activation(pT[:], PP, ACT.Copy).then_inc(S["pp_copied"], 1)

                pipeline(act, step, *STEPS)

            @block.vector
            def _(vec):
                vec.wait_ge(S["mask_loaded"], 32)
                flat = cap[:].rearrange("p t k -> p (t k)")
                nc.vector.tensor_scalar(flat, mi[:], 0.0, 3e38, ALU.not_equal, ALU.mult).then_inc(S["masked"], 1)
                vec.wait_ge(S["masked"], 1)
                nc.vector.tensor_scalar(flat, flat, MASKED, None, ALU.add).then_inc(S["masked"], 1)
                vec.wait_ge(S["masked"], 2)
                vec.wait_ge(S["rot_loaded"], 16 * TT)

                def step(n, u, g):
                    past = not isinstance(n, int)
                    t = u % TT
                    m = n - 2
                    if live(m, UNITS):
                        vec.wait_ge(S["exped"], m + 1)
                        nc.vector.reduce_sum(su[:, u % 2, :], sm[:, u % 2, :, :], AX_X).then_inc(S["summed"], 1)
                        vec.wait_ge(S["summed"], m + 1)
                        nc.vector.reciprocal(rc[:, u % 2, :], su[:, u % 2, :]).then_inc(S["recip"], 1)
                    m = n - 3
                    if live(m, UNITS):
                        vec.wait_ge(S["av_hi"], m + 1)
                        for b2 in range(2):
                            q = slice(b2 * SEQ, (b2 + 1) * SEQ)
                            last = nc.vector.tensor_tensor(aT[1][:, :, q], AV[:, b2, :].rearrange("p (h q) -> p h q", h=GRP),
                                                           aT[0][:, :, q].bitcast(F32), ALU.subtract)
                        last.then_inc(S["av_lo"], 1)
                    m = n - 4
                    if live(m, UNITS):
                        vec.wait_ge(S["o_mm"], m + 1)
                        x = sh.X[:, (t - 4) % TT, :]
                        nc.vector.tensor_tensor(x, x, O, ALU.add).then_inc(S["added"], 1)
                    if live(n, UNITS):
                        vec.wait_ge(S["qkv_mm"], n + 1)
                        if past or n >= 1:
                            vec.wait_ge(S["tr_mm"], n)
                            vec.wait_ge(S["roped"], n)
                        cs, sn_t = rot[:, t, 0:HD // 2], rot[:, t, HD // 2:HD]
                        x = QKV[:, 0:QC + HD].rearrange("p (h x c) -> p h x c", x=2, c=HD // 2)
                        y = sn[:].rearrange("p (h x c) -> p h x c", x=2, c=HD // 2)
                        nc.vector.tensor_tensor(qr[:].rearrange("p (h c) -> p h c", c=HD // 2),
                                                QKV[:, 0:QC + HD].rearrange("p (h c) -> p h c", c=HD // 2),
                                                cs.unsqueeze(1).broadcast_to([P, 2 * (GRP + 1), HD // 2]), ALU.mult)
                        s5 = sn_t.unsqueeze(1).broadcast_to([P, GRP + 1, HD // 2])
                        nc.vector.tensor_tensor(y[:, :, 1, :], x[:, :, 0, :], s5, ALU.mult)
                        nc.vector.scalar_tensor_tensor(y[:, :, 0, :], x[:, :, 1, :], -1.0, s5, ALU.mult,
                                                       ALU.mult).then_inc(S["rope_read"], 1)
                    m = n - 1
                    if live(m, UNITS):
                        vec.wait_ge(S["sc_mm"], m + 1)
                        if past or m >= 2:
                            vec.wait_ge(S["pp_mm"], m - 1)
                        s = sm[:, (u - 1) % 2, :, :]
                        nc.vector.scalar_tensor_tensor(
                            s.rearrange("p (h b) k -> p h (b k)", h=2), SC.rearrange("p (h k) -> p h k", h=2), HD ** -0.5,
                            cap[:, (t - 1) % TT, :].unsqueeze(1).broadcast_to([P, 2, P]),
                            ALU.mult, ALU.min).then_inc(S["capped"], 1)
                        vec.wait_ge(S["capped"], m + 1)
                        nc.vector.reduce_max(mx[:, (u - 1) % 2, :], s, AX_X).then_inc(S["maxed"], 1)

                pipeline(vec, step, *STEPS)

            @block.gpsimd
            def _(gp):
                gp.dma_start(pi[:], d["pos"].rearrange("(t b) s -> (b s) t", b=2),
                             allow_slow_non_contiguous=True).then_inc(S["pos_loaded"], 16)
                gp.wait_ge(S["pos_loaded"], 16)
                for t in range(TT):
                    gp.indirect_dma_start(rot[:, t, :], None, d["rotary"],
                                          bass.IndirectOffsetOnAxis(ap=pi[:, t:t + 1], axis=0)).then_inc(S["rot_loaded"], 16)

                def step(n, u, g):
                    m = n - 2
                    if live(m, UNITS):
                        gp.wait_ge(S["recip"], m + 1)
                        s = sm[:, u % 2, :, :]
                        nc.gpsimd.tensor_tensor(s, s, rc[:, u % 2, :].unsqueeze(2).broadcast_to([P, 4, SEQ]),
                                                ALU.mult).then_inc(S["probs"], 1)
                    if live(n + AHEAD, UNITS):
                        gp.wait_ge(S["w_hi"], n + (AHEAD + 1))
                        for src, dst, loaded in split_source(n, u, g + 1):
                            last = nc.gpsimd.tensor_tensor(dst[1], src, dst[0].bitcast(F32), ALU.subtract)
                        last.then_inc(S["w_split"], 1)
                    if live(n, UNITS):
                        gp.wait_ge(S["rope_read"], n + 1)
                        nc.gpsimd.tensor_tensor(qr[:], qr[:], sn[:], ALU.add).then_inc(S["roped"], 1)
                    m = n - 1
                    if live(m, UNITS):
                        gp.wait_ge(S["maxed"], m + 1)
                        s = sm[:, (u - 1) % 2, :, :]
                        nc.gpsimd.tensor_tensor(s, s, mx[:, (u - 1) % 2, :].unsqueeze(2).broadcast_to([P, 4, SEQ]),
                                                ALU.subtract).then_inc(S["subbed"], 1)

                pipeline(gp, step, *STEPS)


def routed_ffn(nc, sh, d):
    UNITS = EXPERTS * TT
    AHEAD = TT
    STEPS = (-AHEAD, 8, UNITS - AHEAD, UNITS, 16, TT)
    with ExitStack() as st:
        sb, sem = allocator(nc, st)
        iota = sh.const[:, C_IOTA:C_END]
        raw = sb("rf_raw", [P, 2, EC, E])
        w = [sb(f"rf_w{part}", [P, 2, EC, E], F32R) for part in ("h", "l")]
        graw = sb("rf_graw", [P, EC, EXPERTS])
        gw = [sb(f"rf_gw{part}", [P, EC, EXPERTS], F32R) for part in ("h", "l")]
        lg = sb("rf_lg", [P, TT, EXPERTS])
        top = sb("rf_top", [P, TT, EXPERTS])
        at = sb("rf_at", [P, TT, EXPERTS], U32)
        atf = sb("rf_atf", [P, 2, TT])
        wt = sb("rf_wt", [P, 2, TT])
        e2, s2 = sb("rf_e2", [P, TT]), sb("rf_s2", [P, TT])
        we = sb("rf_we", [P, TT, EXPERTS])
        we2 = sb("rf_we2", [P, TT, EXPERTS])

        LG = sh.PS[:, 3, 0:TT * EXPERTS]
        D = sh.PS[:, 4:8, :]
        names = ("loaded0 loaded1 g_loaded g_hi g_split lg_mm lg_copied top_done at_done w_hi w_split d_mm added "
                 "chain exped stored").split()
        S = {x: sem("rf_" + x) for x in names}

        with nc.Block() as block:
            @block.sync
            def _(sp):
                def load(e, slot):
                    src = d["experts"][bass.ds(e, 1), :, :].rearrange("a (c p) o -> p (a c) o", p=P)
                    sp.dma_start(raw[:, slot, :, :], src).then_inc(S[f"loaded{slot}"], 16)

                sp.dma_start(graw[:], d["gate_w"].rearrange("(c p) e -> p c e", p=P)).then_inc(S["g_loaded"], 16)
                load(0, 0)
                load(1, 1)
                with sp.Fori(1, EXPERTS // 2) as j:
                    for u in range(2):
                        sp.wait_ge(S["w_split"], 8 * j + (4 * u - 4))
                        load(2 * j + u, u)
                for t in range(TT):
                    sp.wait_ge(S["added"], UNITS - TT + t + 1)
                    sp.dma_start(d["out"][2 * t:2 * t + 2, :, :].rearrange("b s e -> (b s) e"),
                                 sh.X[:, t, :]).then_inc(S["stored"], 16)
                sp.wait_ge(S["stored"], 16 * TT)

            @block.tensor
            def _(pe):
                pe.wait_ge(S["g_split"], 1)
                for t in range(TT):
                    tok = slice(t * P, (t + 1) * P)
                    for c in range(EC):
                        last = mm3(nc, LG[:, t * EXPERTS:(t + 1) * EXPERTS], sh.NTh[:, c, tok], sh.NTl[:, c, tok],
                                   gw[0][:, c, :], gw[1][:, c, :], c == 0, c == EC - 1)
                last.then_inc(S["lg_mm"], 1)

                def step(n, u, e):
                    if live(n, UNITS):
                        t, par = u % TT, u // TT
                        if t == 0:
                            pe.wait_ge(S["w_split"], 4 * e + 4)
                        if not isinstance(n, int) or n >= 4:
                            pe.wait_ge(S["added"], n - 3)
                        tok = slice(t * P, (t + 1) * P)
                        for c in range(EC):
                            last = mm3(nc, D[:, t % 4, :], sh.NTh[:, c, tok], sh.NTl[:, c, tok],
                                       w[0][:, par, c, :], w[1][:, par, c, :], c == 0, c == EC - 1)
                        last.then_inc(S["d_mm"], 1)

                pipeline(pe, step, *STEPS)

            @block.scalar
            def _(act):
                act.wait_ge(S["g_loaded"], 16)
                nc.scalar.activation(gw[0][:], graw[:], ACT.Copy).then_inc(S["g_hi"], 1)

                def step(n, u, e):
                    p, par = u % TT, (u // TT + 1) % 2
                    if live(n + AHEAD, UNITS) and p < EC:
                        if p == 0:
                            first = 16 * ((n + AHEAD) // (2 * TT)) + 16 if isinstance(n, int) else None
                            if isinstance(n, int):
                                act.wait_ge(S[f"loaded{par}"], first)
                            else:
                                act.wait_ge(S[f"loaded{par}"], 8 * e + (24 - 8 * par))
                            if not isinstance(n, int) or n >= TT:
                                act.wait_ge(S["d_mm"], TT * e)
                        nc.scalar.activation(w[0][:, par, p, :], raw[:, par, p, :], ACT.Copy).then_inc(S["w_hi"], 1)
                    if isinstance(n, int) and n == -2:
                        act.wait_ge(S["chain"], 1)
                        nc.scalar.activation(e2[:], e2[:], ACT.Exp).then_inc(S["exped"], 1)

                pipeline(act, step, *STEPS)

            @block.gpsimd
            def _(gp):
                def step(n, u, e):
                    p, par = u % TT, (u // TT + 1) % 2
                    if live(n + AHEAD, UNITS) and p < EC:
                        gp.wait_ge(S["w_hi"], 4 * e + (p + 5))
                        nc.gpsimd.tensor_tensor(w[1][:, par, p, :], raw[:, par, p, :], w[0][:, par, p, :].bitcast(F32),
                                                ALU.subtract).then_inc(S["w_split"], 1)

                pipeline(gp, step, *STEPS)

            @block.vector
            def _(vec):
                vec.wait_ge(S["g_hi"], 1)
                nc.vector.tensor_tensor(gw[1][:], graw[:], gw[0][:].bitcast(F32), ALU.subtract).then_inc(S["g_split"], 1)
                vec.wait_ge(S["lg_mm"], 1)
                nc.vector.tensor_copy(lg[:].rearrange("p t e -> p (t e)"), LG).then_inc(S["lg_copied"], 1)
                vec.wait_ge(S["lg_copied"], 1)
                for t in range(TT):
                    nc.vector.max(top[:, t, :], lg[:, t, :]).then_inc(S["top_done"], 1)
                for t in range(TT):
                    vec.wait_ge(S["top_done"], t + 1)
                    nc.vector.max_index(at[:, t, :], top[:, t, :], lg[:, t, :]).then_inc(S["at_done"], 1)
                nc.vector.tensor_tensor(e2[:], top[:, :, 1], top[:, :, 0], ALU.subtract).then_inc(S["chain"], 1)
                vec.wait_ge(S["exped"], 1)
                nc.vector.tensor_scalar(s2[:], e2[:], 1.0, None, ALU.add).then_inc(S["chain"], 1)
                vec.wait_ge(S["chain"], 2)
                nc.vector.reciprocal(wt[:, 0, :], s2[:]).then_inc(S["chain"], 1)
                vec.wait_ge(S["chain"], 3)
                nc.vector.tensor_tensor(wt[:, 1, :], e2[:], wt[:, 0, :], ALU.mult).then_inc(S["chain"], 1)
                vec.wait_ge(S["at_done"], TT)
                nc.vector.tensor_copy(atf[:], at[:, :, 0:2].rearrange("p t k -> p k t")).then_inc(S["chain"], 1)
                vec.wait_ge(S["chain"], 5)
                for t in range(TT):
                    for k, dst in enumerate((we, we2)):
                        nc.vector.tensor_scalar(dst[:, t, :], iota, atf[:, k, t:t + 1], wt[:, k, t:t + 1],
                                                ALU.is_equal, ALU.mult).then_inc(S["chain"], 1)
                vec.wait_ge(S["chain"], 5 + 2 * TT)
                nc.vector.tensor_tensor(we[:], we[:], we2[:], ALU.add).then_inc(S["chain"], 1)
                vec.wait_ge(S["chain"], 6 + 2 * TT)

                def step(n, u, e):
                    if live(n, UNITS):
                        t = u % TT
                        vec.wait_ge(S["d_mm"], n + 1)
                        x = sh.X[:, t, :]
                        nc.vector.scalar_tensor_tensor(x, D[:, t % 4, :], we[:, t, bass.ds(e, 1)], x,
                                                       ALU.mult, ALU.add).then_inc(S["added"], 1)

                pipeline(vec, step, *STEPS)


def two_layers_kernel(nc, d):
    with ExitStack() as st:
        sh = Shared()
        sh.X = st.enter_context(nc.sbuf_tensor("X", [P, TT, E], F32))
        sh.const = st.enter_context(nc.sbuf_tensor("const", [P, C_END], F32))
        sh.PS = st.enter_context(nc.psum_tensor("PS", [P, 8, 512], F32))
        sh.NTh, sh.NTl, sh.CTh, sh.CTl = (
            st.enter_context(nc.sbuf_tensor(x, [P, EC, TT * P], F32R)) for x in ("NTh", "NTl", "CTh", "CTl"))
        with nc.sbuf_tensor("CTX", [P, TT, E], F32) as sh.CTX:
            window_attention(nc, sh, d)
            transpose_rows(nc, sh, "t1", sh.X, sh.NTh, sh.NTl, True)
        gated_ffn(nc, sh, d)
        transpose_rows(nc, sh, "t2", sh.X, sh.NTh, sh.NTl, True)
        cross_attention(nc, sh, d)
        transpose_rows(nc, sh, "t3", sh.X, sh.NTh, sh.NTl, True)
        routed_ffn(nc, sh, d)


INPUTS = {"x": "x", "ctx_4096": "ctx", "pos_BxS2": "pos", "mask_BxSxS2_ik0": "mask",
          "L0_xattn_Wq": "L0_Wq", "L0_xattn_bq": "L0_bq", "L0_xattn_Wk": "L0_Wk", "L0_xattn_bk": "L0_bk",
          "L0_xattn_Wv": "L0_Wv", "L0_xattn_bv": "L0_bv", "L0_xattn_Wo": "L0_Wo", "L0_xattn_bo": "L0_bo",
          "L0_ffn_Wg": "L0_Wg", "L0_ffn_Wu": "L0_Wu", "L0_ffn_Wd": "L0_Wd",
          "L0_ffn_ag": "L0_ag", "L0_ffn_au": "L0_au", "L0_ffn_ad": "L0_ad",
          "L1_xattn_Wq": "L1_Wq", "L1_xattn_Wk": "L1_Wk", "L1_xattn_Wv": "L1_Wv", "L1_xattn_Wo": "L1_Wo",
          "L1_ffn_gate_w": "gate_w", "L1_ffn_expert_w": "experts"}


def kernel(**inputs):
    import concourse.bacc as bacc
    from concourse.bass_utils import run_bass_kernel_spmd

    nc = bacc.Bacc("TRN2", target_bir_lowering=False, num_devices=1)
    arrays, d = {}, {}
    for name, short in INPUTS.items():
        arrays["in_" + short] = np.ascontiguousarray(inputs[name])
    arrays["in_consts"] = shape_constants()
    arrays["in_rotary"] = rotary_table()
    for name, a in arrays.items():
        d[name[3:]] = nc.dram_tensor(name, a.shape, mybir.dt.from_np(a.dtype), kind="ExternalInput").ap()
    d["out"] = nc.dram_tensor("out", (BATCH, SEQ, E), F32, kind="ExternalOutput").ap()
    two_layers_kernel(nc, d)
    r = run_bass_kernel_spmd(nc, [arrays], core_ids=[0])
    return r.results[0]["out"]
```

```python
from contextlib import ExitStack

import concourse.bass as bass
import numpy as np
from concourse import mybir

F32 = mybir.dt.float32
F32R = mybir.dt.float32r
I32 = mybir.dt.int32
U32 = mybir.dt.uint32
ALU = mybir.AluOpType
ACT = mybir.ActivationFunctionType
AX_X = mybir.AxisListType.X

P = 128
BATCH, SEQ, E = 16, 64, 512
TT = BATCH * SEQ // P
EC = E // P
EPS = 1e-5

WH, WD, WIN = 8, 8, 16
BLK = 16
KEYS = 2 * BLK
PAD = WIN // 2
UNIT_T = 128
UNITS_PER_TILE = E // UNIT_T

INTER = 1376
IT = -(-INTER // P)

HEADS, KVH, HD = 32, 8, 128
GRP = HEADS // KVH
QC = GRP * HD
KVC = 2 * HD
MAX_POS, THETA = 512, 10000.0
MASKED = -1e9

EXPERTS = 8

C_ID, C_HM, C_HH, C_BAND, C_IOTA, C_END = np.cumsum([0, P, WH, WH // 2, KEYS, EXPERTS]).tolist()


def shape_constants():
    c = np.zeros((P, C_END), np.float32)
    p = np.arange(P)
    c[:, C_ID:C_HM] = np.eye(P)
    c[:, C_HM:C_HH] = (p[:, None] % SEQ) // WD == np.arange(WH)
    c[:, C_HH:C_BAND] = (p[:, None] % (SEQ // 2)) // WD == np.arange(WH // 2)
    j, t = np.arange(KEYS), p % BLK
    inside = (j[None] >= t[:, None]) & (j[None] < t[:, None] + WIN)
    c[:, C_BAND:C_IOTA] = np.where(inside, 0.0, -1e30)
    c[:, C_IOTA:C_END] = np.arange(EXPERTS)
    return c


def rotary_table():
    inv = (1.0 / np.float32(THETA) ** (np.arange(0, HD, 2, dtype=np.float32) / np.float32(HD))).astype(np.float32)
    f = np.arange(MAX_POS, dtype=np.float32)[:, None] * inv[None]
    return np.concatenate([np.cos(f), np.sin(f)], -1).astype(np.float32)


def live(n, total):
    return not isinstance(n, int) or 0 <= n < total


def pipeline(eng, step, begin, loop_begin, loop_end, end, body, per):
    assert (loop_end - loop_begin) % body == 0
    for n in range(begin, loop_begin):
        step(n, n % body, n // per)
    with eng.Fori(0, (loop_end - loop_begin) // body) as i:
        for u in range(body):
            step(i * body + (loop_begin + u), (loop_begin + u) % body, i * (body // per) + (loop_begin + u) // per)
    for n in range(loop_end, end):
        step(n, n % body, n // per)


def mm3(nc, out, l_hi, l_lo, r_hi, r_lo, first, last):
    nc.tensor.matmul(out, l_hi, r_hi, start=first, stop=False)
    nc.tensor.matmul(out, l_hi, r_lo, start=False, stop=False)
    return nc.tensor.matmul(out, l_lo, r_hi, start=False, stop=last)


class Shared:
    pass


def views(room, *sizes):
    ends = np.cumsum(sizes).tolist()
    return [room[:, end - size:end] for end, size in zip(ends, sizes)]


def allocator(nc, stack):
    def sb(name, shape, dt=F32):
        return stack.enter_context(nc.sbuf_tensor(name, shape, dt))

    def sem(name):
        return stack.enter_context(nc.semaphore(name))

    return sb, sem


def norm_stats(nc, vec, src, tiles, stats, mv, veps, sem_stats, sem_aggr, sem_veps, loaded=None):
    for t in tiles:
        if loaded:
            vec.wait_ge(loaded[t], 16)
        nc.vector.bn_stats(stats[:, t, :], src[:, t, :]).then_inc(sem_stats, 1)
    for t in tiles:
        vec.wait_ge(sem_stats, t + 1)
        nc.vector.bn_aggr(mv[:, t, :], stats[:, t, :]).then_inc(sem_aggr, 1)
    vec.wait_ge(sem_aggr, tiles[-1] + 1)
    some = slice(tiles[0], tiles[-1] + 1)
    nc.vector.tensor_scalar(veps[:, some], mv[:, some, 1], EPS, None, ALU.add).then_inc(sem_veps, 1)


class NormedRows:

    @staticmethod
    def buffers(sb):
        return [sb("norm_" + name, [P, 2] + more) for name, more in
                (("stats", [6]), ("mv", [2]), ("veps", []), ("std", []), ("rstd", []), ("xn", [E]), ("spare", []))]

    def __init__(self, nc, sh, st, name):
        sem = allocator(nc, st)[1]
        self.nc, self.sh = nc, sh
        self.stats, self.mv, self.veps, self.std, self.rstd, self.xn, self.spare = sh.norm_buffers
        (self.counted, self.aggregated, self.eps_added, self.rooted, self.inverted, self.normed, self.transposed,
         self.high_done, self.low_done) = (sem(name + x) for x in
                                           ("_counted", "_aggregated", "_eps_added", "_rooted", "_inverted",
                                            "_normed", "_transposed", "_high", "_low"))

    def give_credits(self, gp):
        self.nc.gpsimd.memset(self.spare[:, 0:1], 0.0).then_inc(self.transposed, 2)
        self.nc.gpsimd.memset(self.spare[:, 1:2], 0.0).then_inc(self.low_done, 1)

    def await_credits(self, vec):
        vec.wait_ge(self.transposed, 2)
        vec.wait_ge(self.low_done, 1)

    def count(self, vec, t, slot):
        self.nc.vector.bn_stats(self.stats[:, slot, :], self.sh.X[:, bass.ds(t, 1), :].rearrange("p a e -> p (a e)")
                                ).then_inc(self.counted, 1)

    def await_count(self, vec, t):
        vec.wait_ge(self.counted, t + 1)
        vec.wait_ge(self.transposed, t + 1)

    def aggregate(self, vec, t, slot):
        one = slice(slot, slot + 1)
        self.nc.vector.bn_aggr(self.mv[:, slot, :], self.stats[:, slot, :]).then_inc(self.aggregated, 1)
        vec.wait_ge(self.aggregated, t + 1)
        self.nc.vector.tensor_scalar(self.veps[:, one], self.mv[:, one, 1], EPS, None, ALU.add).then_inc(self.eps_added, 1)

    def root(self, act, t, slot):
        one = slice(slot, slot + 1)
        act.wait_ge(self.eps_added, t + 1)
        self.nc.scalar.activation(self.std[:, one], self.veps[:, one], ACT.Sqrt).then_inc(self.rooted, 1)

    def normalise(self, vec, t, slot):
        one = slice(slot, slot + 1)
        vec.wait_ge(self.rooted, t + 1)
        self.nc.vector.reciprocal(self.rstd[:, one], self.std[:, one]).then_inc(self.inverted, 1)
        vec.wait_ge(self.inverted, t + 1)
        self.nc.vector.tensor_scalar(self.xn[:, one, :], self.sh.X[:, bass.ds(t, 1), :], self.mv[:, one, 0],
                                     self.rstd[:, one], ALU.subtract, ALU.mult).then_inc(self.normed, 1)

    def transpose(self, pe, t, slot, bank):
        pe.wait_ge(self.normed, t + 1)
        for c in range(EC):
            last = self.nc.tensor.transpose(bank[:, c * P:(c + 1) * P], self.xn[:, slot, c * P:(c + 1) * P],
                                            self.sh.const[:, C_ID:C_HM])
        last.then_inc(self.transposed, 1)

    def high(self, act, t, bank):
        act.wait_ge(self.transposed, t + 3)
        self.nc.scalar.activation(self.sh.NTh[:, :, t * P:(t + 1) * P], bank.rearrange("p (c n) -> p c n", c=EC),
                                  ACT.Copy).then_inc(self.high_done, 1)

    def high_by_vector(self, vec, t, bank):
        vec.wait_ge(self.transposed, t + 3)
        self.nc.vector.tensor_copy(self.sh.NTh[:, :, bass.ds(t * P, P)], bank.rearrange("p (c n) -> p c n", c=EC)
                                   ).then_inc(self.high_done, 1)

    def low(self, vec, t, bank):
        vec.wait_ge(self.high_done, t + 1)
        tok = bass.ds(t * P, P)
        self.nc.vector.tensor_tensor(self.sh.NTl[:, :, tok], bank.rearrange("p (c n) -> p c n", c=EC),
                                     self.sh.NTh[:, :, tok].bitcast(F32), ALU.subtract).then_inc(self.low_done, 1)

    def several_by_vector(self, vec, tiles, banks):
        first, end = tiles[0], tiles[-1] + 1
        for t in range(first, end + 2):
            if t < end:
                self.count(vec, t, t % 2)
            if first < t <= end:
                self.normalise(vec, t - 1, (t - 1) % 2)
            if t < end:
                self.await_count(vec, t)
                self.aggregate(vec, t, t % 2)
            if t >= first + 2:
                self.low(vec, t - 2, banks[t % 2])

    def pair_by_vector(self, vec, tiles):
        for t in tiles:
            self.count(vec, t, t % 2)
        for t in tiles:
            self.await_count(vec, t)
            self.aggregate(vec, t, t % 2)
        for t in tiles:
            self.normalise(vec, t, t % 2)

    def several_by_tensor(self, pe, tiles, banks):
        for t in tiles:
            if t >= 2:
                pe.wait_ge(self.low_done, t)
            self.transpose(pe, t, t % 2, banks[t % 2])


def window_attention(nc, sh, d, norm, ffn):
    UNITS = TT * UNITS_PER_TILE
    STEPS = (-4, 8, 24, UNITS + 6, 8, UNITS_PER_TILE)
    HH = WH // 2
    FIRST = 2
    with ExitStack() as st:
        sb, sem = allocator(nc, st)
        ident = sh.const[:, C_ID:C_HM]
        hm = sh.const[:, C_HM:C_HH]
        hh4 = sh.const[:, C_HH:C_BAND]
        band = sh.const[:, C_BAND:C_IOTA]

        stats, mv = sb("wa_stats", [P, TT, 6]), sb("wa_mv", [P, TT, 2])
        veps, std, rstd = sb("wa_veps", [P, TT]), sb("wa_std", [P, TT]), sb("wa_rstd", [P, TT])
        wrow = sb("wa_wrow", [SEQ, 4, SEQ])
        brow = sb("wa_brow", [4, SEQ])
        wT = sb("wa_wT", [P, 4, P])
        bias = sb("wa_bias", [P, 4])
        xn = sb("wa_xn", [P, 2, E])
        qp = sb("wa_qp", [P, E])
        qx = sb("wa_qx", [P, 2, E // BLK, WH, BLK])
        kp = sb("wa_kp", [P, 2, PAD + E + PAD])
        vp = sb("wa_vp", [P, 2, PAD + E + PAD])
        sm = sb("wa_sm", [P, 4, 2 * 2 * 4, KEYS])
        mx, su, rc = (sb("wa_" + x, [P, 4, 16]) for x in ("mx", "su", "rc"))
        pt = sb("wa_pt", [P, 2, 2, 2, P])
        vt = sb("wa_vt", [P, 2, 2, P])
        oh = sb("wa_oh", [P, 2, UNIT_T])

        SC = sh.PS[:, 0:2, 0:256]
        OH = sh.PS[:, 2:6, 0:2 * HH * BLK]
        CT = [sh.PS[:, 2, :], sh.PS[:, 3, :]]
        VT = sh.PS[:, 6, 0:256]
        AO = sh.PS[:, 6, 256:256 + UNIT_T]
        PJ = sh.PS[:, 7, :]

        LOADS = ((0, FIRST), (FIRST, TT))
        x_loaded, ctx_loaded = ([part for a, b in LOADS for part in [sem(f"wa_{x}{a}")] * (b - a)] for x in ("x", "ctx"))
        names = ("const_loaded loaded zeroed padded ct_tr ct_hi ct_lo w_tr w_ready stats aggr veps std rstd normed "
                 "q_mm k_mm v_mm q_biased q_ready k_ready v_ready sc_mm keyed banded maxed subbed exped summed recip probs "
                 "rowed vt_mm vt_copied oh_mm selected oh_copied ao_mm x_added").split()
        S = {x: sem("wa_" + x) for x in names}

        with nc.Block() as block:
            @block.sync
            def _(sp):
                def load(dst, name, done, a, b):
                    sp.dma_start(dst[:, a:b, :], d[name][2 * a:2 * b, :, :].rearrange("(t b) s e -> (b s) t e", b=2)
                                 ).then_inc(done[a], 16)

                load(sh.X, "x", x_loaded, *LOADS[0])
                sp.dma_start(sh.const[:], d["consts"]).then_inc(S["const_loaded"], 16)
                for i, w in enumerate(("Wq", "Wk", "Wv", "Wo")):
                    sp.dma_start(wrow[:, i, :], d["L0_" + w]).then_inc(S["loaded"], 16)
                    sp.dma_start(brow[i:i + 1, :], d["L0_b" + w[1]].rearrange("(a c) -> a c", a=1)).then_inc(S["loaded"], 16)
                load(sh.CTX, "ctx", ctx_loaded, *LOADS[0])
                load(sh.X, "x", x_loaded, *LOADS[1])
                load(sh.CTX, "ctx", ctx_loaded, *LOADS[1])
                ffn.first_loads(sp)

            @block.tensor
            def _(pe):
                pe.wait_ge(S["const_loaded"], 16)
                pe.wait_ge(S["loaded"], 128)
                for b2 in range(2):
                    half = slice(b2 * SEQ, (b2 + 1) * SEQ)
                    for i in range(4):
                        nc.tensor.matmul(PJ[half, i * SEQ:(i + 1) * SEQ], wrow[:, i, :], ident[:SEQ, :SEQ], start=True, stop=True)
                    last = nc.tensor.matmul(PJ[half, 4 * SEQ:4 * SEQ + 4], brow[:], ident[:4, :4], start=True, stop=True)
                last.then_inc(S["w_tr"], 1)
                pe.wait_ge(S["w_ready"], 1)

                def project_context(t, which, done):
                    ctx = sh.CTX[:, bass.ds(t, 1), :].rearrange("p a e -> p (a e)")
                    nc.tensor.matmul(PJ, wT[:, which, :], ctx, start=True, stop=True).then_inc(done, 1)

                def step(n, u, t):
                    q = u % 4
                    if live(t + 1, TT):
                        if q == 0:
                            if not isinstance(t, int) or t >= 0:
                                pe.wait_ge(S["v_ready"], t + 1)
                            if not isinstance(t, int) or t >= 2:
                                pe.wait_ge(norm.low_done, t - 1)
                            pe.wait_ge(S["normed"], t + 2)
                            nc.tensor.matmul(PJ, wT[:, 0, :], xn[:, (u // 4 + 1) % 2, :],
                                             start=True, stop=True).then_inc(S["q_mm"], 1)
                        if q == 1:
                            pe.wait_ge(S["q_biased"], t + 2)
                            project_context(t + 1, 1, S["k_mm"])
                        if q == 2:
                            pe.wait_ge(S["k_ready"], t + 2)
                            project_context(t + 1, 2, S["v_mm"])
                    if q == 3 and live(t - 2, TT - 1):
                        if live(t + 1, TT):
                            pe.wait_ge(S["v_ready"], t + 2)
                        else:
                            pe.wait_ge(norm.low_done, t - 1)
                        norm.transpose(pe, t - 2, u // 4, PJ)
                    c = n + 4
                    if isinstance(n, int) and c < TT:
                        pe.wait_ge(ctx_loaded[c], 16)
                        if c >= 2:
                            pe.wait_ge(S["ct_lo"], c - 1)
                        for k in range(EC):
                            last = nc.tensor.transpose(CT[c % 2][:, k * P:(k + 1) * P], sh.CTX[:, c, k * P:(k + 1) * P], ident)
                        last.then_inc(S["ct_tr"], 1)
                    if live(n, UNITS):
                        pe.wait_ge(S["q_ready"], t + 1)
                        pe.wait_ge(S["k_ready"], t + 1)
                        if not isinstance(n, int) or n >= 1:
                            pe.wait_ge(S["keyed"], n)
                    m, w = n - 3, (u - 3) % 8
                    if live(m, UNITS):
                        slot, qm = w // 4, w % 4
                        pe.wait_ge(S["v_ready"], t + 1 if q >= 3 else t)
                        if not isinstance(n, int) or m >= 1:
                            pe.wait_ge(S["vt_copied"], m)
                        if not isinstance(n, int) or m >= 3:
                            pe.wait_ge(S["x_added"], m - 2)
                        for g in range(2):
                            t0 = qm * UNIT_T + g * BLK
                            last = nc.tensor.transpose(VT[:, g * P:(g + 1) * P], vp[:, slot, t0:t0 + P], ident)
                        last.then_inc(S["vt_mm"], 1)
                    if live(n, UNITS):
                        for g in range(2):
                            for i in range(4):
                                for b2 in range(2):
                                    rows = slice(b2 * SEQ, (b2 + 1) * SEQ)
                                    blk = 8 * q + 2 * i + g
                                    last = nc.tensor.matmul(
                                        SC[i * KEYS:(i + 1) * KEYS, b2, g * P:(g + 1) * P],
                                        kp[rows, u // 4, blk * BLK:blk * BLK + KEYS],
                                        qx[rows, u // 4, blk, :, :].rearrange("p h t -> p (h t)"),
                                        start=True, stop=True)
                        last.then_inc(S["sc_mm"], 1)
                    m = n - 4
                    if live(m, UNITS):
                        pe.wait_ge(S["rowed"], m + 1)
                        pe.wait_ge(S["vt_copied"], m + 1)
                        if not isinstance(n, int) or m >= 1:
                            pe.wait_ge(S["oh_copied"], m)
                        else:
                            pe.wait_ge(S["ct_lo"], TT)
                    m = n - 5
                    if live(m, UNITS):
                        pe.wait_ge(S["oh_copied"], m + 1)
                        pe.wait_ge(S["vt_copied"], m + 3 if live(m + 2, UNITS) else UNITS)
                        if not isinstance(n, int) or m >= 1:
                            pe.wait_ge(S["x_added"], m)
                        nc.tensor.matmul(AO, wT[:, 3, :], oh[:, (u - 5) % 2, :], start=True, stop=True).then_inc(S["ao_mm"], 1)
                    m = n - 4
                    if live(m, UNITS):
                        for g in range(2):
                            for quarter in range(4):
                                for i in range(4):
                                    rows = slice(i * KEYS, (i + 1) * KEYS)
                                    chan = slice(quarter * 32, (quarter + 1) * 32)
                                    b2, half = quarter // 2, quarter % 2
                                    out = OH[chan, i, :].rearrange("p (h g t) -> p h g t", h=HH, g=2)[:, :, g, :]
                                    last = nc.tensor.matmul(out, vt[rows, u % 2, g, chan],
                                                            pt[rows, u % 2, b2, g, half * HH * BLK:(half + 1) * HH * BLK],
                                                            start=True, stop=True)
                        last.then_inc(S["oh_mm"], 1)

                pipeline(pe, step, *STEPS)

            @block.vector
            def _(vec):
                def statistics(k, tiles):
                    norm_stats(nc, vec, sh.X, tiles, stats, mv, veps, S["stats"], S["aggr"], S["veps"], x_loaded)
                    some = slice(tiles[0], tiles[-1] + 1)
                    vec.wait_ge(S["std"], k)
                    nc.vector.reciprocal(rstd[:, some], std[:, some]).then_inc(S["rstd"], 1)
                    vec.wait_ge(S["rstd"], k)

                statistics(1, range(FIRST))
                vec.wait_ge(S["const_loaded"], 16)
                vec.wait_ge(S["w_tr"], 1)
                vec.wait_ge(S["zeroed"], 1)
                for b2 in range(2):
                    half = slice(b2 * SEQ, (b2 + 1) * SEQ)
                    nc.vector.tensor_copy(wT[half, :, half], PJ[half, 0:4 * SEQ].rearrange("p (i c) -> p i c", i=4))
                nc.vector.tensor_copy(bias[:], PJ[:, 4 * SEQ:4 * SEQ + 4]).then_inc(S["w_ready"], 1)

                def normalise(t, slot):
                    if not isinstance(t, int) or t >= 2:
                        vec.wait_ge(S["q_mm"], t - 1)
                    one = bass.ds(t, 1)
                    nc.vector.tensor_scalar(xn[:, slot:slot + 1, :], sh.X[:, one, :], mv[:, one, 0], rstd[:, one],
                                            ALU.subtract, ALU.mult).then_inc(S["normed"], 1)

                def add_bias(t, which, mm, dst, ready):
                    vec.wait_ge(S[mm], t + 1)
                    nc.vector.tensor_scalar(dst, PJ, bias[:, which:which + 1], None, ALU.add).then_inc(S[ready], 1)

                normalise(0, 0)
                vec.wait_ge(S["padded"], 4)
                vec.wait_ge(S["w_ready"], 1)

                def step(n, u, t):
                    q, slot = u % 4, u // 4
                    c = n + 4
                    if isinstance(n, int) and n == 0:
                        statistics(2, range(FIRST, TT))
                    if isinstance(n, int) and c < TT:
                        vec.wait_ge(S["ct_hi"], c + 1)
                        tok = slice(c * P, (c + 1) * P)
                        nc.vector.tensor_tensor(sh.CTl[:, :, tok], CT[c % 2].rearrange("p (c n) -> p c n", c=EC),
                                                sh.CTh[:, :, tok].bitcast(F32), ALU.subtract).then_inc(S["ct_lo"], 1)
                    m, w = n - 1, (u - 1) % 4
                    if q == 1 and live(t - 2, TT - 1):
                        vec.wait_ge(S["x_added"], 4 * t - 4)
                    if live(m, UNITS):
                        vec.wait_ge(S["banded"], m + 1)
                        nc.vector.reduce_max(mx[:, w, :], sm[:, w, :, :], AX_X).then_inc(S["maxed"], 1)
                    if live(t + 1, TT):
                        if q == 0:
                            if not isinstance(t, int) or t >= 0:
                                vec.wait_ge(S["q_ready"], t + 1)
                            add_bias(t + 1, 0, "q_mm", qp[:], "q_biased")
                        if q == 1:
                            add_bias(t + 1, 1, "k_mm", kp[:, 1 - slot, PAD:PAD + E], "k_ready")
                        if q == 2:
                            if not isinstance(t, int) or t >= 1:
                                vec.wait_ge(S["vt_mm"], 4 * t)
                            add_bias(t + 1, 2, "v_mm", vp[:, 1 - slot, PAD:PAD + E], "v_ready")
                    if q == 3 and live(t + 2, TT) and (not isinstance(t, int) or t >= -1):
                        normalise(t + 2, slot)
                    if q == 1 and live(t - 2, TT - 1):
                        norm.count(vec, t - 2, slot)
                        norm.await_count(vec, t - 2)
                    if q == 2 and live(t - 2, TT - 1):
                        norm.normalise(vec, t - 2, slot)
                    if q == 3 and live(t - 2, TT - 1):
                        norm.high_by_vector(vec, t - 2, PJ)
                        norm.low(vec, t - 2, PJ)
                    m, w = n - 2, (u - 2) % 4
                    if live(m, UNITS):
                        vec.wait_ge(S["exped"], m + 1)
                        nc.vector.reduce_sum(su[:, w, :], sm[:, w, :, :], AX_X).then_inc(S["summed"], 1)
                        vec.wait_ge(S["summed"], m + 1)
                        nc.vector.reciprocal(rc[:, w, :], su[:, w, :]).then_inc(S["recip"], 1)
                    if q == 1 and live(t - 2, TT - 1):
                        norm.aggregate(vec, t - 2, slot)
                    m, w = n - 3, (u - 3) % 4
                    if live(m, UNITS):
                        vec.wait_ge(S["probs"], m + 1)
                        if not isinstance(n, int) or m >= 2:
                            vec.wait_ge(S["oh_mm"], m - 1)
                        nc.vector.transpose(pt[:, w % 2, :, :, :].rearrange("p b g x -> p (b g x)"),
                                            sm[:, w, :, :].rearrange("p a k -> p (a k)")).then_inc(S["rowed"], 1)
                    if live(n, UNITS):
                        vec.wait_ge(S["sc_mm"], n + 1)
                        if not isinstance(n, int) or n >= 4:
                            vec.wait_ge(S["rowed"], n - 3)
                        nc.vector.transpose(sm[:, u % 4, :, :].rearrange("p (b x) k -> p b (x k)", b=2),
                                            SC).then_inc(S["keyed"], 1)
                    m, w = n - 5, (u - 5) % 4
                    if live(m, UNITS):
                        vec.wait_ge(S["ao_mm"], m + 1)
                        x = sh.X[:, bass.ds(t - 1 if q >= 1 else t - 2, 1),
                                 w * UNIT_T:(w + 1) * UNIT_T]
                        nc.vector.scalar_tensor_tensor(x, AO.rearrange("p (a e) -> p a e", a=1), bias[:, 3:4], x,
                                                       ALU.add, ALU.add).then_inc(S["x_added"], 1)
                    m = n - 4
                    if live(m, UNITS):
                        vec.wait_ge(S["oh_mm"], m + 1)
                        if not isinstance(n, int) or m >= 2:
                            vec.wait_ge(S["ao_mm"], m - 1)
                        own = oh[:, u % 2, :].rearrange("p (i x) -> p i x", i=4)
                        for h in range(HH):
                            part = OH[:, :, h * 2 * BLK:(h + 1) * 2 * BLK]
                            if h == 0:
                                nc.vector.tensor_scalar(own, part, hh4[:, h:h + 1], None, ALU.mult).then_inc(S["selected"], 1)
                            else:
                                vec.wait_ge(S["selected"], (HH - 1) * m + h)
                                nc.vector.scalar_tensor_tensor(own, part, hh4[:, h:h + 1], own, ALU.mult,
                                                               ALU.add).then_inc(S["selected" if h < HH - 1 else "oh_copied"], 1)

                pipeline(vec, step, *STEPS)

            @block.gpsimd
            def _(gp):
                nc.gpsimd.memset(wT[:], 0.0).then_inc(S["zeroed"], 1)
                nc.gpsimd.memset(ffn.agu[:], 0.0).then_inc(ffn.agu_zeroed, 1)
                for padded in (kp, vp):
                    nc.gpsimd.memset(padded[:, :, 0:PAD], 0.0).then_inc(S["padded"], 1)
                    nc.gpsimd.memset(padded[:, :, PAD + E:], 0.0).then_inc(S["padded"], 1)
                norm.give_credits(gp)
                gp.wait_ge(S["const_loaded"], 16)

                def step(n, u, t):
                    m, w = n - 1, (u - 1) % 4
                    if live(m, UNITS):
                        gp.wait_ge(S["maxed"], m + 1)
                        s = sm[:, w, :, :]
                        nc.gpsimd.tensor_tensor(s, s, mx[:, w, :].unsqueeze(2).broadcast_to([P, 16, KEYS]),
                                                ALU.subtract).then_inc(S["subbed"], 1)
                    m, w = n - 2, (u - 2) % 4
                    if live(m, UNITS):
                        gp.wait_ge(S["recip"], m + 1)
                        s = sm[:, w, :, :]
                        nc.gpsimd.tensor_tensor(s, s, rc[:, w, :].unsqueeze(2).broadcast_to([P, 16, KEYS]),
                                                ALU.mult).then_inc(S["probs"], 1)
                    if live(n, UNITS):
                        gp.wait_ge(S["keyed"], n + 1)
                        s = sm[:, u % 4, :, :]
                        nc.gpsimd.tensor_tensor(s, s, band.unsqueeze(1).broadcast_to([P, 16, KEYS]),
                                                ALU.add).then_inc(S["banded"], 1)

                pipeline(gp, step, *STEPS)

            @block.scalar
            def _(act):
                def deviations(k, tiles):
                    some = slice(tiles[0], tiles[-1] + 1)
                    act.wait_ge(S["veps"], k)
                    nc.scalar.activation(std[:, some], veps[:, some], ACT.Sqrt).then_inc(S["std"], 1)

                deviations(1, range(FIRST))
                act.wait_ge(S["const_loaded"], 16)

                def step(n, u, t):
                    q, slot = u % 4, u // 4
                    c = n + 4
                    if isinstance(n, int) and c < TT:
                        act.wait_ge(S["ct_tr"], c + 1)
                        nc.scalar.activation(sh.CTh[:, :, c * P:(c + 1) * P], CT[c % 2].rearrange("p (c n) -> p c n", c=EC),
                                             ACT.Copy).then_inc(S["ct_hi"], 1)
                    if isinstance(n, int) and n == 0:
                        deviations(2, range(FIRST, TT))
                    m = n - 3
                    if live(m, UNITS):
                        act.wait_ge(S["vt_mm"], m + 1)
                        if not isinstance(n, int) or m >= 2:
                            act.wait_ge(S["oh_mm"], m - 1)
                        nc.scalar.activation(vt[:, (u - 3) % 2, :, :].rearrange("p g x -> p (g x)"), VT,
                                             ACT.Copy).then_inc(S["vt_copied"], 1)
                    m, w = n - 1, (u - 1) % 4
                    if live(m, UNITS):
                        act.wait_ge(S["subbed"], m + 1)
                        nc.scalar.activation(sm[:, w, :, :], sm[:, w, :, :], ACT.Exp, scale=WD ** -0.5).then_inc(S["exped"], 1)
                    if q == 1 and live(t - 2, TT - 1):
                        norm.root(act, t - 2, slot)
                    if q >= 1 and live(t + 1, TT):
                        if q == 1:
                            act.wait_ge(S["q_biased"], t + 2)
                            if not isinstance(t, int) or t >= 1:
                                act.wait_ge(S["sc_mm"], 4 * t)
                        for h in range(3 * q - 3, min(3 * q, WH)):
                            last = nc.scalar.activation(qx[:, 1 - slot, :, h, :], qp[:].rearrange("p (k t) -> p k t", t=BLK),
                                                        ACT.Copy, scale=hm[:, h:h + 1])
                        if q == 3:
                            last.then_inc(S["q_ready"], 1)

                pipeline(act, step, *STEPS)


def width(i):
    return INTER - (IT - 1) * P if isinstance(i, int) and i == IT - 1 else P


class GatedInputs:

    def __init__(self, nc, st, room, d):
        sb, sem = allocator(nc, st)
        self.d = d
        graw, uraw, draw = views(room, 2 * E, 2 * E, 2 * E)
        self.graw, self.uraw = (x.rearrange("p (a e) -> p a e", a=2) for x in (graw, uraw))
        self.draw = draw.rearrange("p (a c n) -> p a c n", a=2, c=EC)
        self.agu = sb("ff_agu", [P, IT, 2])
        self.ad = sb("ff_ad", [P, E])
        self.loaded = [sem("ff_loaded0"), sem("ff_loaded1")]
        self.agu_zeroed, self.scales = sem("ff_agu_zeroed"), sem("ff_scales")

    def load(self, sp, i, slot):
        w, done = width(i), self.loaded[slot]
        rows = bass.ds(i * P, w)
        sp.dma_start(self.graw[:w, slot, :], self.d["L0_Wg"][rows, :]).then_inc(done, 16)
        sp.dma_start(self.uraw[:w, slot, :], self.d["L0_Wu"][rows, :]).then_inc(done, 16)
        sp.dma_start(self.draw[:, slot, :, :w],
                     self.d["L0_Wd"].rearrange("(c p) i -> p c i", p=P)[:, :, rows]).then_inc(done, 16)

    def first_loads(self, sp):
        full = IT - 1
        self.load(sp, 0, 0)
        self.load(sp, 1, 1)
        sp.wait_ge(self.agu_zeroed, 1)
        for name, dst in (("L0_ag", self.agu[:, :, 0]), ("L0_au", self.agu[:, :, 1])):
            sp.dma_start(dst[:, 0:full], self.d[name][0:full * P].rearrange("(i p) -> p i", p=P),
                         allow_slow_non_contiguous=True).then_inc(self.scales, 16)
            sp.dma_start(dst[:width(full), full:IT], self.d[name][full * P:INTER].rearrange("(p a) -> p a", a=1),
                         allow_slow_non_contiguous=True).then_inc(self.scales, 16)
        sp.dma_start(self.ad[:], self.d["L0_ad"].partition_broadcast(P)).then_inc(self.scales, 16)


def gated_ffn(nc, sh, d, norm, ffn, next_norm, cross):
    HALF = TT * P // 2
    STEPS = (0, 4, 10, IT + 2, 2, 2)
    with ExitStack() as st:
        sb, sem = allocator(nc, st)
        ident = sh.const[:, C_ID:C_HM]
        graw, uraw, draw = ffn.graw, ffn.uraw, ffn.draw
        gT, uT, dT = ([sb(f"ff_{x}T{part}", [P, 2, E], F32R) for part in ("h", "l")] for x in "gud")
        col = sb("ff_col", [P, 2, 2])
        mi = sb("ca_mi", [P, TT * P], I32)
        pi = sb("ca_pi", [P, TT], I32)
        dad = sb("ff_dad", [P, E])
        sg = sb("ff_sg", [P, 2, HALF])
        hf = sb("ff_hf", [P, 2, HALF])
        hh, hl = (sb("ff_h" + x, [P, 2, 2 * HALF], F32R) for x in "hl")

        T = [sh.PS[:, 0, :], sh.PS[:, 1, :]]
        G, U = sh.PS[:, 2, :], sh.PS[:, 3, :]
        D = sh.PS[:, 4:8, :]

        names = ("columns d_scaled g_tr u_tr d_tr g_hi u_hi d_hi g_split u_split d_split "
                 "g_mm u_mm silu gated h_hi h_split d_mm added").split()
        S = {x: sem("ff_" + x) for x in names}

        with nc.Block() as block:
            @block.sync
            def _(sp):
                cross.first_loads(sp, mi)
                with sp.Fori(0, 4) as i:
                    for u in range(2):
                        sp.wait_ge(S["d_tr"], 2 * i + u + 1)
                        ffn.load(sp, 2 * i + u + 2, u)
                sp.wait_ge(S["d_tr"], IT - 2)
                ffn.load(sp, IT - 1, (IT - 1) % 2)
                for p in range(EC):
                    sp.wait_ge(cross.w_split, p + 1)
                    cross.load_o(sp, 0, p)

            @block.tensor
            def _(pe):
                def transposes(bank, raw, slot, w, done):
                    for c in range(EC):
                        if raw is draw:
                            last = nc.tensor.transpose(bank[:w, c * P:(c + 1) * P], raw[:, slot, c, :w], ident)
                        else:
                            last = nc.tensor.transpose(bank[:, c * P:c * P + w], raw[:w, slot, c * P:(c + 1) * P],
                                                       ident[:w, :w])
                    last.then_inc(S[done], 1)

                def inner(out, wT, slot, half, w):
                    tok = slice(half * HALF, (half + 1) * HALF)
                    for c in range(EC):
                        cols = slice(c * P, c * P + w)
                        last = mm3(nc, out[:w, :], wT[0][:, slot, cols], wT[1][:, slot, cols],
                                   sh.NTh[:, c, tok], sh.NTl[:, c, tok], c == 0, c == EC - 1)
                    return last

                def down(i, slot, tiles, w):
                    for t in tiles:
                        if not isinstance(i, int) or 8 * i + t >= 4:
                            pe.wait_ge(S["added"], 8 * i + (t - 3))
                        tok = slice(t * P, (t + 1) * P)
                        mm3(nc, D[:, t % 4, :], hh[:w, slot, tok], hl[:w, slot, tok],
                            dT[0][:w, slot, :], dT[1][:w, slot, :], True, True).then_inc(S["d_mm"], 1)

                def step(s, u, j):
                    i, o = s - 1, s - 2
                    past = not isinstance(s, int)
                    if live(s, IT):
                        pe.wait_ge(ffn.loaded[u], 48 * j + 48)
                        if past or s >= 2:
                            pe.wait_ge(S["d_scaled"], s - 1)
                        elif s == 1:
                            pe.wait_ge(S["g_split"], 1)
                        transposes(T[0], graw, u, width(s), "g_tr")
                    if isinstance(i, int) and i == 0:
                        norm.transpose(pe, TT - 1, (TT - 1) % 2, D[:, 3, :])
                    if live(i, IT):
                        pe.wait_ge(S["g_split"], i + 1)
                        if past or i >= 1:
                            pe.wait_ge(S["silu"], 2 * i)
                        inner(G, gT, 1 - u, 0, width(i)).then_inc(S["g_mm"], 1)
                    if live(o, IT):
                        pe.wait_ge(S["h_split"], 2 * o + 2)
                        pe.wait_ge(S["d_split"], o + 1)
                        down(o, u, (0, 1), width(o))
                    if live(s, IT):
                        if past or s >= 1:
                            pe.wait_ge(S["u_split"], s)
                        transposes(T[1], uraw, u, width(s), "u_tr")
                    if live(i, IT):
                        pe.wait_ge(S["u_split"], i + 1)
                        if past or i >= 1:
                            pe.wait_ge(S["gated"], 2 * i)
                        inner(U, uT, 1 - u, 0, width(i)).then_inc(S["u_mm"], 1)
                    if live(o, IT):
                        down(o, u, (2, 3), width(o))
                    if live(i, IT):
                        pe.wait_ge(S["g_split"], min(s + 1, IT) if isinstance(s, int) else s + 1)
                        transposes(T[0], draw, 1 - u, width(i), "d_tr")
                        pe.wait_ge(S["silu"], 2 * i + 1)
                        if isinstance(i, int) and i == 0:
                            pe.wait_ge(norm.low_done, TT + 1)
                        inner(G, gT, 1 - u, 1, width(i)).then_inc(S["g_mm"], 1)
                    if live(o, IT):
                        down(o, u, (4, 5), width(o))
                    if live(i, IT):
                        pe.wait_ge(S["gated"], 2 * i + 1)
                        inner(U, uT, 1 - u, 1, width(i)).then_inc(S["u_mm"], 1)
                    if live(o, IT):
                        down(o, u, (6, 7), width(o))

                pipeline(pe, step, *STEPS)

            @block.scalar
            def _(act):
                def high(bank, wT, slot, w, tr, done, free):
                    act.wait_ge(*tr)
                    if free:
                        act.wait_ge(*free)
                    src, dst = bank.rearrange("p (c n) -> p c n", c=EC), wT[0][:, slot, :].rearrange("p (c n) -> p c n", c=EC)
                    nc.scalar.activation(dst[:, :, :w], src[:, :, :w], ACT.Copy).then_inc(S[done], 1)

                def silu(i, half, w, column):
                    act.wait_ge(S["g_mm"], 2 * i + half + 1)
                    if not isinstance(i, int) or i >= 1:
                        act.wait_ge(S["gated"], 2 * i + half - 1)
                    act.wait_ge(S["columns"], i + 1)
                    nc.scalar.activation(sg[:w, half, :], G[:w, :], ACT.Silu, scale=column).then_inc(S["silu"], 1)

                def h_high(i, slot, half, w):
                    act.wait_ge(S["gated"], 2 * i + half + 1)
                    if not isinstance(i, int) or i >= 2:
                        act.wait_ge(S["d_mm"], 8 * i - 8)
                    nc.scalar.activation(hh[:w, slot, half * HALF:(half + 1) * HALF], hf[:w, half, :],
                                         ACT.Copy).then_inc(S["h_hi"], 1)

                norm.root(act, TT - 1, (TT - 1) % 2)

                def step(s, u, j):
                    i = s - 1
                    past = not isinstance(s, int)
                    if isinstance(i, int) and i == 0:
                        norm.high(act, TT - 1, D[:, 3, :])
                    if live(s, IT):
                        high(T[0], gT, u, width(s), (S["g_tr"], s + 1), "g_hi",
                             (S["g_mm"], 2 * s - 2) if past or s >= 2 else None)
                    if live(i, IT):
                        a = col[:width(i), 1 - u, 0:1]
                        silu(i, 0, width(i), a)
                    if live(s, IT):
                        high(T[1], uT, u, width(s), (S["u_tr"], s + 1), "u_hi",
                             (S["u_mm"], 2 * s - 2) if past or s >= 2 else None)
                    if live(i, IT):
                        h_high(i, 1 - u, 0, width(i))
                        act.wait_ge(S["d_scaled"], i + 1)
                        if past or i >= 2:
                            act.wait_ge(S["d_mm"], 8 * i - 8)
                        nc.scalar.activation(dT[0][:width(i), 1 - u, :], dad[:width(i), :], ACT.Copy).then_inc(S["d_hi"], 1)
                        silu(i, 1, width(i), a)
                        h_high(i, 1 - u, 1, width(i))

                pipeline(act, step, *STEPS)
                cross.first_high(act)


            @block.vector
            def _(vec):
                vec.wait_ge(ffn.scales, 80)
                norm.count(vec, TT - 1, (TT - 1) % 2)
                norm.await_count(vec, TT - 1)
                norm.aggregate(vec, TT - 1, (TT - 1) % 2)
                norm.normalise(vec, TT - 1, (TT - 1) % 2)

                def low(bank, wT, slot, w, hi, done):
                    vec.wait_ge(*hi)
                    src = bank.rearrange("p (c n) -> p c n", c=EC)[:, :, :w]
                    hi_part, dst = (x[:, slot, :].rearrange("p (c n) -> p c n", c=EC)[:, :, :w] for x in wT)
                    nc.vector.tensor_tensor(dst, src, hi_part.bitcast(F32), ALU.subtract).then_inc(S[done], 1)

                def gate(i, half, w, column):
                    vec.wait_ge(S["u_mm"], 2 * i + half + 1)
                    vec.wait_ge(S["silu"], 2 * i + half + 1)
                    if not isinstance(i, int) or i >= 1:
                        vec.wait_ge(S["h_split"], 2 * i + half - 1)
                    nc.vector.scalar_tensor_tensor(hf[:w, half, :], U[:w, :], column, sg[:w, half, :],
                                                   ALU.mult, ALU.mult).then_inc(S["gated"], 1)

                def add_down(o, tiles):
                    for t in tiles:
                        vec.wait_ge(S["d_mm"], 8 * o + t + 1)
                        nc.vector.tensor_tensor(sh.X[:, t, :], sh.X[:, t, :], D[:, t % 4, :], ALU.add).then_inc(S["added"], 1)

                def step(s, u, j):
                    i, o = s - 1, s - 2
                    past = not isinstance(s, int)
                    if isinstance(i, int) and i == 0:
                        norm.low(vec, TT - 1, D[:, 3, :])
                    if isinstance(s, int) and s == 3:
                        cross.make_cap(vec, mi)
                    if live(s, IT):
                        low(T[0], gT, u, width(s), (S["g_hi"], s + 1), "g_split")
                    if live(o, IT):
                        add_down(o, (0, 1))
                    if live(s, IT):
                        low(T[1], uT, u, width(s), (S["u_hi"], s + 1), "u_split")
                    if live(i, IT):
                        a = col[:width(i), 1 - u, 1:2]
                        gate(i, 0, width(i), a)
                    if live(o, IT):
                        add_down(o, (2, 3))
                    if live(i, IT):
                        vec.wait_ge(S["d_tr"], i + 1)
                        if past or i >= 1:
                            vec.wait_ge(S["d_split"], i)
                        nc.vector.tensor_tensor(dad[:width(i), :], T[0][:width(i), :], ffn.ad[:width(i), :],
                                                ALU.mult).then_inc(S["d_scaled"], 1)
                    if live(o, IT):
                        add_down(o, (4, 5))
                    if live(i, IT):
                        gate(i, 1, width(i), a)
                    if live(o, IT):
                        add_down(o, (6, 7))

                pipeline(vec, step, *STEPS)
            @block.gpsimd
            def _(gp):
                next_norm.give_credits(gp)
                gp.wait_ge(ffn.scales, 80)

                def h_low(i, slot, half, w):
                    gp.wait_ge(S["h_hi"], 2 * i + half + 1)
                    tok = slice(half * HALF, (half + 1) * HALF)
                    nc.gpsimd.tensor_tensor(hl[:w, slot, tok], hf[:w, half, :], hh[:w, slot, tok].bitcast(F32),
                                            ALU.subtract).then_inc(S["h_split"], 1)

                def step(s, u, j):
                    if isinstance(s, int) and s == 3:
                        cross.gather_rotary(gp, pi)
                    if live(s, IT):
                        if not isinstance(s, int) or s >= 2:
                            gp.wait_ge(S["gated"], 2 * s - 2)
                        nc.gpsimd.tensor_copy(col[:, u, :], ffn.agu[:, bass.ds(s, 1), :].rearrange("p a b -> p (a b)")
                                              ).then_inc(S["columns"], 1)
                    if live(s - 1, IT):
                        w = width(s - 1)
                        h_low(s - 1, 1 - u, 0, w)
                        gp.wait_ge(S["d_hi"], s)
                        nc.gpsimd.tensor_tensor(dT[1][:w, 1 - u, :], dad[:w, :], dT[0][:w, 1 - u, :].bitcast(F32),
                                                ALU.subtract).then_inc(S["d_split"], 1)
                        h_low(s - 1, 1 - u, 1, w)

                pipeline(gp, step, *STEPS)
                cross.first_low(gp)



class CrossInputs:

    def __init__(self, nc, st, d):
        sb, sem = allocator(nc, st)
        self.nc, self.d = nc, d
        self.raw = sb("ca_raw", [P, EC, QC])
        self.kvraw = sb("ca_kvraw", [P, EC, KVC])
        self.wq = [sb(f"ca_wq{part}", [P, 2, EC, QC], F32R) for part in ("h", "l")]
        self.rot = sb("ca_rot", [P, TT, HD])
        self.cap = sb("ca_cap", [P, TT, P])
        self.graw = sb("rf_graw", [P, EC, EXPERTS])
        self.gw = [sb(f"rf_gw{part}", [P, EC, EXPERTS], F32R) for part in ("h", "l")]
        self.raw_loaded = [sem(f"ca_raw{p}") for p in range(EC)]
        self.kv_loaded, self.mask_loaded, self.pos_loaded, self.rot_loaded, self.gate_loaded = (
            sem("ca_" + x + "_loaded") for x in ("kv", "mask", "pos", "rot", "gate"))
        self.masked, self.w_hi, self.w_split, self.gate_hi = (sem("ca_" + x) for x in ("masked", "w_hi", "w_split", "gate_hi"))

    def load_q(self, sp, g, p):
        sp.dma_start(self.raw[:, p, :], self.d["L1_Wq"][p * P:(p + 1) * P, bass.ds(g * QC, QC)]).then_inc(self.raw_loaded[p], 16)

    def load_o(self, sp, g, p):
        sp.dma_start(self.raw[:, p, :], self.d["L1_Wo"][bass.ds(g * QC + p * P, P), :]).then_inc(self.raw_loaded[p], 16)

    def load_kv(self, sp, g):
        for x, name in enumerate(("L1_Wk", "L1_Wv")):
            sp.dma_start(self.kvraw[:, :, x * HD:(x + 1) * HD],
                         self.d[name][:, bass.ds(g * HD, HD)].rearrange("(c p) n -> p c n", p=P)).then_inc(self.kv_loaded, 16)

    def first_loads(self, sp, mi):
        for p in range(EC):
            self.load_q(sp, 0, p)
        self.load_kv(sp, 0)
        for h2 in range(2):
            sp.dma_start(mi[h2 * SEQ:(h2 + 1) * SEQ, :].rearrange("p (b k) -> p b k", k=SEQ),
                         self.d["mask"].rearrange("b q k -> q b k")).then_inc(self.mask_loaded, 16)
        sp.dma_start(self.graw[:], self.d["gate_w"].rearrange("(c p) e -> p c e", p=P)).then_inc(self.gate_loaded, 16)

    def gather_rotary(self, gp, pi):
        gp.dma_start(pi[:], self.d["pos"].rearrange("(t b) s -> (b s) t", b=2),
                     allow_slow_non_contiguous=True).then_inc(self.pos_loaded, 16)
        gp.wait_ge(self.pos_loaded, 16)
        for t in range(TT):
            gp.indirect_dma_start(self.rot[:, t, :], None, self.d["rotary"],
                                  bass.IndirectOffsetOnAxis(ap=pi[:, t:t + 1], axis=0)).then_inc(self.rot_loaded, 16)

    def make_cap(self, vec, mi):
        vec.wait_ge(self.mask_loaded, 32)
        flat = self.cap[:].rearrange("p t k -> p (t k)")
        self.nc.vector.tensor_scalar(flat, mi[:], 0.0, 3e38, ALU.not_equal, ALU.mult).then_inc(self.masked, 1)
        vec.wait_ge(self.masked, 1)
        self.nc.vector.tensor_scalar(flat, flat, MASKED, None, ALU.add).then_inc(self.masked, 1)

    def first_high(self, act):
        for p in range(EC):
            act.wait_ge(self.raw_loaded[p], 16)
            self.nc.scalar.activation(self.wq[0][:, 0, p, :], self.raw[:, p, :], ACT.Copy).then_inc(self.w_hi, 1)
        act.wait_ge(self.gate_loaded, 16)
        self.nc.scalar.activation(self.gw[0][:], self.graw[:], ACT.Copy).then_inc(self.gate_hi, 1)

    def first_low(self, gp):
        for p in range(EC):
            gp.wait_ge(self.w_hi, p + 1)
            self.nc.gpsimd.tensor_tensor(self.wq[1][:, 0, p, :], self.raw[:, p, :], self.wq[0][:, 0, p, :].bitcast(F32),
                                         ALU.subtract).then_inc(self.w_split, 1)
        gp.wait_ge(self.gate_hi, 1)
        self.nc.gpsimd.tensor_tensor(self.gw[1][:], self.graw[:], self.gw[0][:].bitcast(F32), ALU.subtract)


def cross_attention(nc, sh, d, norm, next_norm, cross):
    UNITS = KVH * TT
    AHEAD = 8
    STEPS = (-EC, 8, UNITS - AHEAD, UNITS + 4, 16, TT)
    with ExitStack() as st:
        sb, sem = allocator(nc, st)
        ident = sh.const[:, C_ID:C_HM]
        raw, kvraw, wq, rot, cap = cross.raw, cross.kvraw, cross.wq, cross.rot, cross.cap
        wo = [sb(f"ca_wo{part}", [P, 2, EC, QC], F32R) for part in ("h", "l")]
        wkv = [sb(f"ca_wkv{part}", [P, 2, EC, KVC], F32R) for part in ("h", "l")]
        qr, sn, V, sm = views(sh.room, (GRP + 1) * HD, (GRP + 1) * HD, 4 * HD, 2 * 4 * SEQ)
        V = V.rearrange("p (a c) -> p a c", a=4)
        sm = sm.rearrange("p (a x k) -> p a x k", a=2, x=4)
        qT = sb("ca_qT", [P, QC])
        kT = sb("ca_kT", [P, P])
        mx, su, rc = (sb("ca_" + x, [P, 2, 4]) for x in ("mx", "su", "rc"))
        pT = sb("ca_pT", [P, 2 * P])
        aT = [sb(f"ca_aT{part}", [P, GRP, P], F32R) for part in ("h", "l")]

        QKV = sh.PS[:, 0:2, :].rearrange("p a b -> p (a b)")
        QT = sh.PS[:, 2, :]
        KP = sh.PS[:, 3, 2 * P:3 * P]
        PP = sh.PS[:, 3, 0:2 * P]
        SC = sh.PS[:, 4, 0:4 * SEQ]
        AV = sh.PS[:, 5:7, 0:2 * P]
        O = sh.PS[:, 7, :]

        names = ("qkv_mm cosed rope_read roped v_copied tr_mm qT_copied kT_copied "
                 "sc_mm capped maxed subbed exped summed recip probs pp_mm pp_copied av_mm av_hi av_lo o_mm added").split()
        S = {x: sem("ca_" + x) for x in names}
        S["w_hi"], S["w_split"] = cross.w_hi, cross.w_split
        FIRST = range(TT // 2)

        def rows_due(n):
            if isinstance(n, int) and n in (0, 1):
                return norm, (TT // 2 + 2 * n, TT // 2 + 2 * n + 1), [sh.PS[:, 5, :], sh.PS[:, 6, :]]
            if isinstance(n, int) and UNITS <= n < UNITS + 3:
                return next_norm, (2 * (n - UNITS), 2 * (n - UNITS) + 1), [sh.PS[:, 0, :], sh.PS[:, 1, :]]
            return None, (), None

        def gp_of(u):
            return u // 8 % 2

        with nc.Block() as block:
            @block.sync
            def _(sp):
                with sp.Fori(1, KVH) as g:
                    for p in range(EC):
                        sp.wait_ge(S["w_split"], 8 * g - 3 + p)
                        cross.load_q(sp, g, p)
                    cross.load_kv(sp, g)
                    for p in range(EC):
                        sp.wait_ge(S["w_split"], 8 * g + p + 1)
                        cross.load_o(sp, g, p)
                for p in range(EC):
                    sp.wait_ge(S["w_split"], 8 * KVH - 3 + p)
                    sp.dma_start(raw[:, p, :], d["experts"][0, p * P:(p + 1) * P, :]).then_inc(cross.raw_loaded[p], 16)

            def split_source(n, u, g):
                w = (u + AHEAD) % 16
                p, par = w % 8, w // 8
                if p < EC:
                    return [(raw[:, p, :], [x[:, par, p, :] for x in wq], (cross.raw_loaded[p], 32 * g + 16))]
                p -= EC
                return [(kvraw[:, p, :], [x[:, par, p, :] for x in wkv], (cross.kv_loaded, 32 * g + 32)),
                        (raw[:, p, :], [x[:, par, p, :] for x in wo], (cross.raw_loaded[p], 32 * g + 32))]

            @block.tensor
            def _(pe):
                def step(n, u, g):
                    past = not isinstance(n, int)
                    t = u % TT
                    m = n - 1
                    if live(m, UNITS):
                        pe.wait_ge(S["roped"], m + 1)
                        if past or m >= 1:
                            pe.wait_ge(S["qT_copied"], m)
                        if past or m >= 2:
                            pe.wait_ge(S["pp_copied"], m - 1)
                        for h in range(GRP):
                            out = QT[:, h // 2 * 2 * P:(h // 2 + 1) * 2 * P].rearrange("p (b m q) -> p b m q", b=2, m=2)[:, :, h % 2, :]
                            nc.tensor.transpose(out, qr[:, h * HD:(h + 1) * HD], ident)
                        nc.tensor.transpose(KP, qr[:, QC:QC + HD], ident).then_inc(S["tr_mm"], 1)
                    if live(n, UNITS):
                        par = gp_of(u)
                        if t == 0:
                            pe.wait_ge(S["w_split"], 8 * g + 8)
                        if not past and n < TT:
                            pe.wait_ge(norm.low_done, n + 2)
                        if past or n >= 1:
                            pe.wait_ge(S["rope_read"], n)
                            pe.wait_ge(S["v_copied"], n)
                        tok = slice(t * P, (t + 1) * P)
                        for c in range(EC):
                            mm3(nc, QKV[:, QC:QC + KVC], sh.CTh[:, c, tok], sh.CTl[:, c, tok],
                                wkv[0][:, par, c, :], wkv[1][:, par, c, :], c == 0, c == EC - 1)
                        for c in range(EC):
                            last = mm3(nc, QKV[:, 0:QC], sh.NTh[:, c, tok], sh.NTl[:, c, tok],
                                       wq[0][:, par, c, :], wq[1][:, par, c, :], c == 0, c == EC - 1)
                        last.then_inc(S["qkv_mm"], 1)
                    rows, tiles, banks = rows_due(n)
                    if tiles:
                        if n == UNITS:
                            pe.wait_ge(S["rope_read"], UNITS)
                            pe.wait_ge(S["v_copied"], UNITS)
                        rows.several_by_tensor(pe, tiles, banks)
                    if live(m, UNITS):
                        pe.wait_ge(S["qT_copied"], m + 1)
                        pe.wait_ge(S["kT_copied"], m + 1)
                        if past or m >= 1:
                            pe.wait_ge(S["capped"], m)
                        for hp in range(2):
                            for b2 in range(2):
                                c0 = (2 * hp + b2)
                                last = nc.tensor.matmul(SC[:, c0 * SEQ:(c0 + 1) * SEQ], qT[:, c0 * P:(c0 + 1) * P],
                                                        kT[:, b2 * SEQ:(b2 + 1) * SEQ], start=True, stop=True)
                        last.then_inc(S["sc_mm"], 1)
                    m = n - 2
                    if live(m, UNITS):
                        pe.wait_ge(S["probs"], m + 1)
                        pe.wait_ge(S["kT_copied"], m + 2 if live(m + 1, UNITS) else UNITS)
                        if past or m >= 1:
                            pe.wait_ge(S["pp_copied"], m)
                        for hp in range(2):
                            last = nc.tensor.transpose(PP[:, hp * P:(hp + 1) * P],
                                                       sm[:, u % 2, 2 * hp:2 * hp + 2, :].rearrange("p b k -> p (b k)"), ident)
                        last.then_inc(S["pp_mm"], 1)
                    m = n - 3
                    if live(m, UNITS):
                        par = gp_of(u - 3)
                        pe.wait_ge(S["av_lo"], m + 1)
                        if past or m >= 1:
                            pe.wait_ge(S["added"], m)
                        for h in range(GRP):
                            last = mm3(nc, O, aT[0][:, h, :], aT[1][:, h, :], wo[0][:, par, h, :], wo[1][:, par, h, :],
                                       h == 0, h == GRP - 1)
                        last.then_inc(S["o_mm"], 1)
                    m = n - 2
                    if live(m, UNITS):
                        pe.wait_ge(S["pp_copied"], m + 1)
                        if past or m >= 1:
                            pe.wait_ge(S["av_lo"], m)
                        for b2 in range(2):
                            rows = slice(b2 * SEQ, (b2 + 1) * SEQ)
                            last = nc.tensor.matmul(AV[:, b2, :], V[rows, (u - 2) % 4, :], pT[rows, :], start=True, stop=True)
                        last.then_inc(S["av_mm"], 1)

                norm.several_by_tensor(pe, FIRST, rows_due(0)[2])
                pipeline(pe, step, *STEPS)

            @block.scalar
            def _(act):
                def step(n, u, g):
                    past = not isinstance(n, int)
                    rows, tiles, banks = rows_due(n)
                    for t in tiles:
                        rows.root(act, t, t % 2)
                    m = n - 2
                    if live(m, UNITS):
                        act.wait_ge(S["subbed"], m + 1)
                        s = sm[:, u % 2, :, :]
                        nc.scalar.activation(s, s, ACT.Exp).then_inc(S["exped"], 1)
                    m = n - 3
                    if live(m, UNITS):
                        act.wait_ge(S["av_mm"], m + 1)
                        for b2 in range(2):
                            last = nc.scalar.activation(aT[0][:, :, b2 * SEQ:(b2 + 1) * SEQ],
                                                        AV[:, b2, :].rearrange("p (h q) -> p h q", h=GRP), ACT.Copy)
                        last.then_inc(S["av_hi"], 1)
                    m = n - 1
                    if live(m, UNITS):
                        act.wait_ge(S["tr_mm"], m + 1)
                        if past or m >= 1:
                            act.wait_ge(S["sc_mm"], m)
                        nc.scalar.activation(kT[:], KP, ACT.Copy).then_inc(S["kT_copied"], 1)
                        nc.scalar.activation(qT[:], QT, ACT.Copy).then_inc(S["qT_copied"], 1)
                    if live(n + AHEAD, UNITS + EC):
                        if u % 8 == 0 and (past or n >= 8):
                            act.wait_ge(S["qkv_mm"], 8 * g)
                            act.wait_ge(S["o_mm"], 8 * g - 8)
                        if u % 8 == 4 and (past or n >= 8):
                            act.wait_ge(S["o_mm"], 8 * g)
                        for src, dst, loaded in split_source(n, u, g + 1):
                            act.wait_ge(*loaded)
                            last = nc.scalar.activation(dst[0], src, ACT.Copy)
                        last.then_inc(S["w_hi"], 1)
                    if live(n, UNITS):
                        act.wait_ge(S["rope_read"], n + 1)
                        if past or n >= 4:
                            act.wait_ge(S["av_mm"], n - 3)
                        nc.scalar.activation(V[:, u % 4, :], QKV[:, QC + HD:QC + KVC], ACT.Copy).then_inc(S["v_copied"], 1)
                    m = n - 2
                    if live(m, UNITS):
                        act.wait_ge(S["pp_mm"], m + 1)
                        if past or m >= 1:
                            act.wait_ge(S["av_mm"], m)
                        nc.scalar.activation(pT[:], PP, ACT.Copy).then_inc(S["pp_copied"], 1)
                    for t in tiles:
                        rows.high(act, t, banks[t % 2])

                for t in range(len(FIRST) + 1):
                    if t in FIRST:
                        norm.root(act, t, t % 2)
                    if t >= 1:
                        norm.high(act, t - 1, rows_due(0)[2][(t - 1) % 2])
                    if t < EC:
                        step(t - EC, t + 2 * TT - EC, -1)
                assert STEPS[0] == -EC
                pipeline(act, step, 0, *STEPS[1:])

            @block.vector
            def _(vec):
                norm.await_credits(vec)
                norm.several_by_vector(vec, FIRST, rows_due(0)[2])
                vec.wait_ge(cross.masked, 2)
                vec.wait_ge(cross.rot_loaded, 16 * TT)

                def step(n, u, g):
                    past = not isinstance(n, int)
                    t = u % TT
                    rows, tiles, banks = rows_due(n)
                    if tiles:
                        if rows is next_norm and n == UNITS:
                            rows.await_credits(vec)
                        if rows is next_norm:
                            vec.wait_ge(S["added"], UNITS - TT + tiles[-1] + 1)
                        rows.pair_by_vector(vec, tiles)
                    m = n - 2
                    if live(m, UNITS):
                        vec.wait_ge(S["exped"], m + 1)
                        nc.vector.reduce_sum(su[:, u % 2, :], sm[:, u % 2, :, :], AX_X).then_inc(S["summed"], 1)
                        vec.wait_ge(S["summed"], m + 1)
                        nc.vector.reciprocal(rc[:, u % 2, :], su[:, u % 2, :]).then_inc(S["recip"], 1)
                    m = n - 3
                    if live(m, UNITS):
                        vec.wait_ge(S["av_hi"], m + 1)
                        for b2 in range(2):
                            q = slice(b2 * SEQ, (b2 + 1) * SEQ)
                            last = nc.vector.tensor_tensor(aT[1][:, :, q], AV[:, b2, :].rearrange("p (h q) -> p h q", h=GRP),
                                                           aT[0][:, :, q].bitcast(F32), ALU.subtract)
                        last.then_inc(S["av_lo"], 1)
                    m = n - 4
                    if live(m, UNITS):
                        vec.wait_ge(S["o_mm"], m + 1)
                        x = sh.X[:, (t - 4) % TT, :]
                        nc.vector.tensor_tensor(x, x, O, ALU.add).then_inc(S["added"], 1)
                    if live(n, UNITS):
                        vec.wait_ge(S["qkv_mm"], n + 1)
                        if past or n >= 1:
                            vec.wait_ge(S["tr_mm"], n)
                            vec.wait_ge(S["roped"], n)
                        cs, sn_t = rot[:, t, 0:HD // 2], rot[:, t, HD // 2:HD]
                        x = QKV[:, 0:QC + HD].rearrange("p (h x c) -> p h x c", x=2, c=HD // 2)
                        y = sn.rearrange("p (h x c) -> p h x c", x=2, c=HD // 2)
                        nc.vector.tensor_tensor(qr.rearrange("p (h c) -> p h c", c=HD // 2),
                                                QKV[:, 0:QC + HD].rearrange("p (h c) -> p h c", c=HD // 2),
                                                cs.unsqueeze(1).broadcast_to([P, 2 * (GRP + 1), HD // 2]), ALU.mult)
                        s5 = sn_t.unsqueeze(1).broadcast_to([P, GRP + 1, HD // 2])
                        nc.vector.tensor_tensor(y[:, :, 1, :], x[:, :, 0, :], s5, ALU.mult)
                        nc.vector.scalar_tensor_tensor(y[:, :, 0, :], x[:, :, 1, :], -1.0, s5, ALU.mult,
                                                       ALU.mult).then_inc(S["rope_read"], 1)
                    m = n - 1
                    if live(m, UNITS):
                        vec.wait_ge(S["sc_mm"], m + 1)
                        if past or m >= 2:
                            vec.wait_ge(S["pp_mm"], m - 1)
                        s = sm[:, (u - 1) % 2, :, :]
                        nc.vector.scalar_tensor_tensor(
                            s.rearrange("p (h b) k -> p h (b k)", h=2), SC.rearrange("p (h k) -> p h k", h=2), HD ** -0.5,
                            cap[:, (t - 1) % TT, :].unsqueeze(1).broadcast_to([P, 2, P]),
                            ALU.mult, ALU.min).then_inc(S["capped"], 1)
                        vec.wait_ge(S["capped"], m + 1)
                        nc.vector.reduce_max(mx[:, (u - 1) % 2, :], s, AX_X).then_inc(S["maxed"], 1)

                    for t in tiles:
                        rows.low(vec, t, banks[t % 2])

                pipeline(vec, step, *STEPS)

            @block.gpsimd
            def _(gp):
                next_norm.give_credits(gp)

                def step(n, u, g):
                    m = n - 2
                    if live(m, UNITS):
                        gp.wait_ge(S["recip"], m + 1)
                        s = sm[:, u % 2, :, :]
                        nc.gpsimd.tensor_tensor(s, s, rc[:, u % 2, :].unsqueeze(2).broadcast_to([P, 4, SEQ]),
                                                ALU.mult).then_inc(S["probs"], 1)
                    if live(n + AHEAD, UNITS + EC):
                        gp.wait_ge(S["w_hi"], n + (AHEAD + 1))
                        for src, dst, loaded in split_source(n, u, g + 1):
                            last = nc.gpsimd.tensor_tensor(dst[1], src, dst[0].bitcast(F32), ALU.subtract)
                        last.then_inc(S["w_split"], 1)
                    if live(n, UNITS):
                        gp.wait_ge(S["rope_read"], n + 1)
                        nc.gpsimd.tensor_tensor(qr[:], qr[:], sn[:], ALU.add).then_inc(S["roped"], 1)
                    m = n - 1
                    if live(m, UNITS):
                        gp.wait_ge(S["maxed"], m + 1)
                        s = sm[:, (u - 1) % 2, :, :]
                        nc.gpsimd.tensor_tensor(s, s, mx[:, (u - 1) % 2, :].unsqueeze(2).broadcast_to([P, 4, SEQ]),
                                                ALU.subtract).then_inc(S["subbed"], 1)

                pipeline(gp, step, *STEPS)


def routed_ffn(nc, sh, d, norm, cross):
    UNITS = EXPERTS * TT
    AHEAD = TT
    STEPS = (0, 8, UNITS - AHEAD, UNITS, 16, TT)
    with ExitStack() as st:
        sb, sem = allocator(nc, st)
        iota = sh.const[:, C_IOTA:C_END]
        raw, w, gw = cross.raw, cross.wq, cross.gw
        lgT = sb("rf_lgT", [EXPERTS, TT * P])
        lg = sb("rf_lg", [P, TT, EXPERTS])
        top = sb("rf_top", [P, TT, EXPERTS])
        at = sb("rf_at", [P, TT, EXPERTS], U32)
        atf = sb("rf_atf", [P, 2, TT])
        wt = sb("rf_wt", [P, 2, TT])
        e2, s2 = sb("rf_e2", [P, TT]), sb("rf_s2", [P, TT])
        we = sb("rf_we", [P, TT, EXPERTS])
        we2 = sb("rf_we2", [P, TT, EXPERTS])

        LG = sh.PS[:, 0, 0:TT * EXPERTS]
        LGT = sh.PS[:EXPERTS, 2:4, :]
        REST = (TT - 2, TT - 1)
        D = sh.PS[:, 4:8, :]
        NT_BANKS = [sh.PS[:, 0, :], sh.PS[:, 1, :]]
        raw_loaded = [sem(f"rf_raw{p}") for p in range(EC)]
        names = ("lgT_mm lgT_copied lg_mm lg_copied top_done at_done w_hi w_split d_mm added "
                 "chain exped stored").split()
        S = {x: sem("rf_" + x) for x in names}

        with nc.Block() as block:
            @block.sync
            def _(sp):
                def load(e, p):
                    sp.dma_start(raw[:, p, :], d["experts"][bass.ds(e, 1), p * P:(p + 1) * P, :].rearrange("a p o -> (a p) o")
                                 ).then_inc(raw_loaded[p], 16)

                for p in range(EC):
                    load(1, p)
                with sp.Fori(2, EXPERTS) as e:
                    for p in range(EC):
                        sp.wait_ge(S["w_split"], 4 * e + (p - 7))
                        load(e, p)
                for t in range(TT):
                    sp.wait_ge(S["added"], UNITS - TT + t + 1)
                    sp.dma_start(d["out"][2 * t:2 * t + 2, :, :].rearrange("b s e -> (b s) e"),
                                 sh.X[:, t, :]).then_inc(S["stored"], 16)
                sp.wait_ge(S["stored"], 16 * TT)

            @block.tensor
            def _(pe):
                def logits(half):
                    tok = slice(half * TT * P // 2, (half + 1) * TT * P // 2)
                    for c in range(EC):
                        last = mm3(nc, LGT[:, half, :], gw[0][:, c, :], gw[1][:, c, :], sh.NTh[:, c, tok], sh.NTl[:, c, tok],
                                   c == 0, c == EC - 1)
                    last.then_inc(S["lgT_mm"], 1)

                logits(0)
                norm.several_by_tensor(pe, REST, NT_BANKS)
                pe.wait_ge(norm.low_done, TT + 1)
                logits(1)
                pe.wait_ge(S["lgT_copied"], 2)
                for t in range(TT):
                    last = nc.tensor.transpose(LG[:, t * EXPERTS:(t + 1) * EXPERTS], lgT[:, t * P:(t + 1) * P],
                                               sh.const[:EXPERTS, C_ID:C_ID + EXPERTS])
                last.then_inc(S["lg_mm"], 1)

                def step(n, u, e):
                    if live(n, UNITS):
                        t, par = u % TT, u // TT
                        if t == 0 and (not isinstance(n, int) or n > 0):
                            pe.wait_ge(S["w_split"], 4 * e)
                        if not isinstance(n, int) or n >= 4:
                            pe.wait_ge(S["added"], n - 3)
                        tok = slice(t * P, (t + 1) * P)
                        for c in range(EC):
                            last = mm3(nc, D[:, t % 4, :], sh.NTh[:, c, tok], sh.NTl[:, c, tok],
                                       w[0][:, par, c, :], w[1][:, par, c, :], c == 0, c == EC - 1)
                        last.then_inc(S["d_mm"], 1)

                pipeline(pe, step, *STEPS)

            @block.scalar
            def _(act):
                for t in REST:
                    norm.root(act, t, t % 2)
                for t in REST:
                    norm.high(act, t, NT_BANKS[t % 2])
                for half in range(2):
                    act.wait_ge(S["lgT_mm"], half + 1)
                    nc.scalar.activation(lgT[:, half * TT * P // 2:(half + 1) * TT * P // 2], LGT[:, half, :],
                                         ACT.Copy).then_inc(S["lgT_copied"], 1)
                act.wait_ge(S["chain"], 1)
                nc.scalar.activation(e2[:], e2[:], ACT.Exp).then_inc(S["exped"], 1)

                def step(n, u, e):
                    p, par = u % TT, (u // TT + 1) % 2
                    if live(n + AHEAD, UNITS) and p < EC:
                        act.wait_ge(raw_loaded[p], 16 * e + 16)
                        if p == 0 and (not isinstance(n, int) or n >= TT):
                            act.wait_ge(S["d_mm"], TT * e)
                        nc.scalar.activation(w[0][:, par, p, :], raw[:, p, :], ACT.Copy).then_inc(S["w_hi"], 1)

                pipeline(act, step, *STEPS)

            @block.gpsimd
            def _(gp):
                def step(n, u, e):
                    p, par = u % TT, (u // TT + 1) % 2
                    if live(n + AHEAD, UNITS) and p < EC:
                        gp.wait_ge(S["w_hi"], 4 * e + (p + 1))
                        nc.gpsimd.tensor_tensor(w[1][:, par, p, :], raw[:, p, :], w[0][:, par, p, :].bitcast(F32),
                                                ALU.subtract).then_inc(S["w_split"], 1)

                pipeline(gp, step, *STEPS)

            @block.vector
            def _(vec):
                norm.pair_by_vector(vec, REST)
                for t in REST:
                    norm.low(vec, t, NT_BANKS[t % 2])
                vec.wait_ge(S["lg_mm"], 1)
                nc.vector.tensor_copy(lg[:].rearrange("p t e -> p (t e)"), LG).then_inc(S["lg_copied"], 1)
                vec.wait_ge(S["lg_copied"], 1)
                for t in range(TT):
                    nc.vector.max(top[:, t, :], lg[:, t, :]).then_inc(S["top_done"], 1)
                for t in range(TT):
                    vec.wait_ge(S["top_done"], t + 1)
                    nc.vector.max_index(at[:, t, :], top[:, t, :], lg[:, t, :]).then_inc(S["at_done"], 1)
                nc.vector.tensor_tensor(e2[:], top[:, :, 1], top[:, :, 0], ALU.subtract).then_inc(S["chain"], 1)
                vec.wait_ge(S["exped"], 1)
                nc.vector.tensor_scalar(s2[:], e2[:], 1.0, None, ALU.add).then_inc(S["chain"], 1)
                vec.wait_ge(S["chain"], 2)
                nc.vector.reciprocal(wt[:, 0, :], s2[:]).then_inc(S["chain"], 1)
                vec.wait_ge(S["chain"], 3)
                nc.vector.tensor_tensor(wt[:, 1, :], e2[:], wt[:, 0, :], ALU.mult).then_inc(S["chain"], 1)
                vec.wait_ge(S["at_done"], TT)
                nc.vector.tensor_copy(atf[:], at[:, :, 0:2].rearrange("p t k -> p k t")).then_inc(S["chain"], 1)
                vec.wait_ge(S["chain"], 5)
                for t in range(TT):
                    for k, dst in enumerate((we, we2)):
                        nc.vector.tensor_scalar(dst[:, t, :], iota, atf[:, k, t:t + 1], wt[:, k, t:t + 1],
                                                ALU.is_equal, ALU.mult).then_inc(S["chain"], 1)
                vec.wait_ge(S["chain"], 5 + 2 * TT)
                nc.vector.tensor_tensor(we[:], we[:], we2[:], ALU.add).then_inc(S["chain"], 1)
                vec.wait_ge(S["chain"], 6 + 2 * TT)

                def step(n, u, e):
                    if live(n, UNITS):
                        t = u % TT
                        vec.wait_ge(S["d_mm"], n + 1)
                        x = sh.X[:, t, :]
                        nc.vector.scalar_tensor_tensor(x, D[:, t % 4, :], we[:, t, bass.ds(e, 1)], x,
                                                       ALU.mult, ALU.add).then_inc(S["added"], 1)

                pipeline(vec, step, *STEPS)


def two_layers_kernel(nc, d):
    with ExitStack() as st:
        sh = Shared()
        sh.X = st.enter_context(nc.sbuf_tensor("X", [P, TT, E], F32))
        sh.const = st.enter_context(nc.sbuf_tensor("const", [P, C_END], F32))
        sh.PS = st.enter_context(nc.psum_tensor("PS", [P, 8, 512], F32))
        sh.NTh, sh.NTl, sh.CTh, sh.CTl = (
            st.enter_context(nc.sbuf_tensor(x, [P, EC, TT * P], F32R)) for x in ("NTh", "NTl", "CTh", "CTl"))
        sh.norm_buffers = NormedRows.buffers(allocator(nc, st)[0])
        norm1, norm2, norm3 = (NormedRows(nc, sh, st, name) for name in ("n1", "n2", "n3"))
        sh.room = st.enter_context(nc.sbuf_tensor("room", [P, 6 * E], F32))
        ffn = GatedInputs(nc, st, sh.room, d)
        with nc.sbuf_tensor("CTX", [P, TT, E], F32) as sh.CTX:
            window_attention(nc, sh, d, norm1, ffn)
        cross = CrossInputs(nc, st, d)
        gated_ffn(nc, sh, d, norm1, ffn, norm2, cross)
        cross_attention(nc, sh, d, norm2, norm3, cross)
        routed_ffn(nc, sh, d, norm3, cross)


INPUTS = {"x": "x", "ctx_4096": "ctx", "pos_BxS2": "pos", "mask_BxSxS2_ik0": "mask",
          "L0_xattn_Wq": "L0_Wq", "L0_xattn_bq": "L0_bq", "L0_xattn_Wk": "L0_Wk", "L0_xattn_bk": "L0_bk",
          "L0_xattn_Wv": "L0_Wv", "L0_xattn_bv": "L0_bv", "L0_xattn_Wo": "L0_Wo", "L0_xattn_bo": "L0_bo",
          "L0_ffn_Wg": "L0_Wg", "L0_ffn_Wu": "L0_Wu", "L0_ffn_Wd": "L0_Wd",
          "L0_ffn_ag": "L0_ag", "L0_ffn_au": "L0_au", "L0_ffn_ad": "L0_ad",
          "L1_xattn_Wq": "L1_Wq", "L1_xattn_Wk": "L1_Wk", "L1_xattn_Wv": "L1_Wv", "L1_xattn_Wo": "L1_Wo",
          "L1_ffn_gate_w": "gate_w", "L1_ffn_expert_w": "experts"}


def kernel(**inputs):
    import concourse.bacc as bacc
    from concourse.bass_utils import run_bass_kernel_spmd

    nc = bacc.Bacc("TRN2", target_bir_lowering=False, num_devices=1)
    arrays, d = {}, {}
    for name, short in INPUTS.items():
        arrays["in_" + short] = np.ascontiguousarray(inputs[name])
    arrays["in_consts"] = shape_constants()
    arrays["in_rotary"] = rotary_table()
    for name, a in arrays.items():
        d[name[3:]] = nc.dram_tensor(name, a.shape, mybir.dt.from_np(a.dtype), kind="ExternalInput").ap()
    d["out"] = nc.dram_tensor("out", (BATCH, SEQ, E), F32, kind="ExternalOutput").ap()
    two_layers_kernel(nc, d)
    r = run_bass_kernel_spmd(nc, [arrays], core_ids=[0])
    return r.results[0]["out"]
```

```python
from contextlib import ExitStack

import concourse.bass as bass
import numpy as np
from concourse import mybir

F32 = mybir.dt.float32
F32R = mybir.dt.float32r
I32 = mybir.dt.int32
U32 = mybir.dt.uint32
ALU = mybir.AluOpType
ACT = mybir.ActivationFunctionType
AX_X = mybir.AxisListType.X

P = 128
BATCH, SEQ, E = 16, 64, 512
TT = BATCH * SEQ // P
EC = E // P
EPS = 1e-5

WARM_UP = 7
WH, WD, WIN = 8, 8, 16
BLK = 16
KEYS = 2 * BLK
PAD = WIN // 2
UNIT_T = 128
UNITS_PER_TILE = E // UNIT_T

INTER = 1376
IT = -(-INTER // P)

HEADS, KVH, HD = 32, 8, 128
GRP = HEADS // KVH
QC = GRP * HD
KVC = 2 * HD
MAX_POS, THETA = 512, 10000.0
MASKED = -1e9

EXPERTS = 8

C_ID, C_HM, C_HH, C_BAND, C_IOTA, C_END = np.cumsum([0, P, WH, WH // 2, KEYS, EXPERTS]).tolist()


def shape_constants():
    c = np.zeros((P, C_END), np.float32)
    p = np.arange(P)
    c[:, C_ID:C_HM] = np.eye(P)
    c[:, C_HM:C_HH] = (p[:, None] % SEQ) // WD == np.arange(WH)
    c[:, C_HH:C_BAND] = (p[:, None] % (SEQ // 2)) // WD == np.arange(WH // 2)
    j, t = np.arange(KEYS), p % BLK
    inside = (j[None] >= t[:, None]) & (j[None] < t[:, None] + WIN)
    c[:, C_BAND:C_IOTA] = np.where(inside, 0.0, -1e30)
    c[:, C_IOTA:C_END] = np.arange(EXPERTS)
    return c


def rotary_table():
    inv = (1.0 / np.float32(THETA) ** (np.arange(0, HD, 2, dtype=np.float32) / np.float32(HD))).astype(np.float32)
    f = np.arange(MAX_POS, dtype=np.float32)[:, None] * inv[None]
    return np.concatenate([np.cos(f), np.cos(f), np.sin(f), -np.sin(f)], -1).astype(np.float32)


def live(n, total):
    return not isinstance(n, int) or 0 <= n < total


def pipeline(eng, step, begin, loop_begin, loop_end, end, body, per):
    assert (loop_end - loop_begin) % body == 0
    for n in range(begin, loop_begin):
        step(n, n % body, n // per)
    with eng.Fori(0, (loop_end - loop_begin) // body) as i:
        for u in range(body):
            step(i * body + (loop_begin + u), (loop_begin + u) % body, i * (body // per) + (loop_begin + u) // per)
    for n in range(loop_end, end):
        step(n, n % body, n // per)


def mm3(nc, out, l_hi, l_lo, r_hi, r_lo, first, last):
    nc.tensor.matmul(out, l_hi, r_hi, start=first, stop=False)
    nc.tensor.matmul(out, l_hi, r_lo, start=False, stop=False)
    return nc.tensor.matmul(out, l_lo, r_hi, start=False, stop=last)


class Shared:
    pass


def views(room, *sizes):
    ends = np.cumsum(sizes).tolist()
    return [room[:, end - size:end] for end, size in zip(ends, sizes)]


def allocator(nc, stack):
    def sb(name, shape, dt=F32):
        return stack.enter_context(nc.sbuf_tensor(name, shape, dt))

    def sem(name):
        return stack.enter_context(nc.semaphore(name))

    return sb, sem


def norm_stats(nc, vec, src, tiles, stats, mv, veps, sem_stats, sem_aggr, sem_veps, loaded=None):
    for t in tiles:
        if loaded:
            vec.wait_ge(loaded[t], 16)
        nc.vector.bn_stats(stats[:, t, :], src[:, t, :]).then_inc(sem_stats, 1)
    for t in tiles:
        vec.wait_ge(sem_stats, t + 1)
        nc.vector.bn_aggr(mv[:, t, :], stats[:, t, :]).then_inc(sem_aggr, 1)
    vec.wait_ge(sem_aggr, tiles[-1] + 1)
    some = slice(tiles[0], tiles[-1] + 1)
    nc.vector.tensor_scalar(veps[:, some], mv[:, some, 1], EPS, None, ALU.add).then_inc(sem_veps, 1)


class NormedRows:

    @staticmethod
    def buffers(sb):
        return [sb("norm_" + name, [P, 2] + more) for name, more in
                (("stats", [6]), ("mv", [2]), ("veps", []), ("std", []), ("rstd", []), ("spare", []))]

    def __init__(self, nc, sh, st, name, xn):
        sem = allocator(nc, st)[1]
        self.nc, self.sh = nc, sh
        self.stats, self.mv, self.veps, self.std, self.rstd, self.spare = sh.norm_buffers
        self.xn = xn.rearrange("p (a e) -> p a e", a=2)
        (self.counted, self.aggregated, self.eps_added, self.rooted, self.inverted, self.normed, self.transposed,
         self.high_done, self.low_done) = (sem(name + x) for x in
                                           ("_counted", "_aggregated", "_eps_added", "_rooted", "_inverted",
                                            "_normed", "_transposed", "_high", "_low"))

    def give_credits(self, gp):
        self.nc.gpsimd.memset(self.spare[:, 0:1], 0.0).then_inc(self.transposed, 2)
        self.nc.gpsimd.memset(self.spare[:, 1:2], 0.0).then_inc(self.low_done, 1)

    def await_credits(self, vec):
        vec.wait_ge(self.transposed, 2)
        vec.wait_ge(self.low_done, 1)

    def count(self, vec, t, slot):
        self.nc.vector.bn_stats(self.stats[:, slot, :], self.sh.X[:, bass.ds(t, 1), :].rearrange("p a e -> p (a e)")
                                ).then_inc(self.counted, 1)

    def await_count(self, vec, t):
        vec.wait_ge(self.counted, t + 1)
        vec.wait_ge(self.transposed, t + 1)

    def aggregate(self, vec, t, slot):
        one = slice(slot, slot + 1)
        self.nc.vector.bn_aggr(self.mv[:, slot, :], self.stats[:, slot, :]).then_inc(self.aggregated, 1)
        vec.wait_ge(self.aggregated, t + 1)
        self.nc.vector.tensor_scalar(self.veps[:, one], self.mv[:, one, 1], EPS, None, ALU.add).then_inc(self.eps_added, 1)

    def root(self, act, t, slot):
        one = slice(slot, slot + 1)
        act.wait_ge(self.eps_added, t + 1)
        self.nc.scalar.activation(self.std[:, one], self.veps[:, one], ACT.Sqrt).then_inc(self.rooted, 1)

    def normalise(self, vec, t, slot):
        one = slice(slot, slot + 1)
        vec.wait_ge(self.rooted, t + 1)
        self.nc.vector.reciprocal(self.rstd[:, one], self.std[:, one]).then_inc(self.inverted, 1)
        vec.wait_ge(self.inverted, t + 1)
        self.nc.vector.tensor_scalar(self.xn[:, one, :], self.sh.X[:, bass.ds(t, 1), :], self.mv[:, one, 0],
                                     self.rstd[:, one], ALU.subtract, ALU.mult).then_inc(self.normed, 1)

    def transpose(self, pe, t, slot, bank):
        pe.wait_ge(self.normed, t + 1)
        for c in range(EC):
            last = self.nc.tensor.transpose(bank[:, c * P:(c + 1) * P], self.xn[:, slot, c * P:(c + 1) * P],
                                            self.sh.const[:, C_ID:C_HM])
        last.then_inc(self.transposed, 1)

    def high(self, act, t, bank):
        act.wait_ge(self.transposed, t + 3)
        self.nc.scalar.activation(self.sh.NTh[:, :, t * P:(t + 1) * P], bank.rearrange("p (c n) -> p c n", c=EC),
                                  ACT.Copy).then_inc(self.high_done, 1)

    def high_by_vector(self, vec, t, bank):
        vec.wait_ge(self.transposed, t + 3)
        self.nc.vector.tensor_copy(self.sh.NTh[:, :, bass.ds(t * P, P)], bank.rearrange("p (c n) -> p c n", c=EC)
                                   ).then_inc(self.high_done, 1)

    def low(self, vec, t, bank):
        vec.wait_ge(self.high_done, t + 1)
        tok = bass.ds(t * P, P)
        self.nc.vector.tensor_tensor(self.sh.NTl[:, :, tok], bank.rearrange("p (c n) -> p c n", c=EC),
                                     self.sh.NTh[:, :, tok].bitcast(F32), ALU.subtract).then_inc(self.low_done, 1)

    def several_by_vector(self, vec, tiles, banks):
        first, end = tiles[0], tiles[-1] + 1
        for t in range(first, end + 2):
            if t < end:
                self.count(vec, t, t % 2)
            if first < t <= end:
                self.normalise(vec, t - 1, (t - 1) % 2)
            if t < end:
                self.await_count(vec, t)
                self.aggregate(vec, t, t % 2)
            if t >= first + 2:
                self.low(vec, t - 2, banks[t % 2])

    def pair_by_vector(self, vec, tiles):
        for t in tiles:
            self.count(vec, t, t % 2)
        for t in tiles:
            self.await_count(vec, t)
            self.aggregate(vec, t, t % 2)
        for t in tiles:
            self.normalise(vec, t, t % 2)

    def several_by_tensor(self, pe, tiles, banks):
        for t in tiles:
            if t >= 2:
                pe.wait_ge(self.low_done, t)
            self.transpose(pe, t, t % 2, banks[t % 2])


def window_attention(nc, sh, d, norm, ffn):
    UNITS = TT * UNITS_PER_TILE
    STEPS = (-4, 8, 24, UNITS + 6, 8, UNITS_PER_TILE)
    HH = WH // 2
    FIRST = 2
    with ExitStack() as st:
        sb, sem = allocator(nc, st)
        ident = sh.const[:, C_ID:C_HM]
        hm = sh.const[:, C_HM:C_HH]
        hh4 = sh.const[:, C_HH:C_BAND]
        band = sh.const[:, C_BAND:C_IOTA]

        stats, mv = sb("wa_stats", [P, TT, 6]), sb("wa_mv", [P, TT, 2])
        veps, std, rstd = sb("wa_veps", [P, TT]), sb("wa_std", [P, TT]), sb("wa_rstd", [P, TT])
        wrow = sb("wa_wrow", [SEQ, 4, SEQ])
        brow = sb("wa_brow", [4, SEQ])
        wT = sb("wa_wT", [P, 4, P])
        bias = sb("wa_bias", [P, 4])
        xn = sb("wa_xn", [P, 2, E])
        qp = sb("wa_qp", [P, E])
        qx = sb("wa_qx", [P, 2, E // BLK, WH, BLK])
        kp = sb("wa_kp", [P, 2, PAD + E + PAD])
        vp = sb("wa_vp", [P, 2, PAD + E + PAD])
        sm = sb("wa_sm", [P, 4, 2 * 2 * 4, KEYS])
        mx, su, rc = (sb("wa_" + x, [P, 4, 16]) for x in ("mx", "su", "rc"))
        pt = sb("wa_pt", [P, 2, 2, 2, P])
        vt = sb("wa_vt", [P, 2, 2, P])
        oh = sb("wa_oh", [P, 2, UNIT_T])

        SC = sh.PS[:, 0:2, 0:256]
        OH = sh.PS[:, 2:6, 0:2 * HH * BLK]
        CT = [sh.PS[:, 2, :], sh.PS[:, 3, :]]
        VT = sh.PS[:, 6, 0:256]
        AO = sh.PS[:, 6, 256:256 + UNIT_T]
        PJ = sh.PS[:, 7, :]

        LOADS = ((0, FIRST), (FIRST, TT))
        x_loaded, ctx_loaded = ([part for a, b in LOADS for part in [sem(f"wa_{x}{a}")] * (b - a)] for x in ("x", "ctx"))
        names = ("const_loaded loaded zeroed padded ct_tr ct_hi ct_lo w_tr w_ready stats aggr veps std rstd normed "
                 "q_mm k_mm v_mm q_biased q_ready k_ready v_ready sc_mm keyed banded maxed subbed exped summed recip probs "
                 "rowed vt_mm vt_copied oh_mm selected oh_copied ao_mm x_added").split()
        S = {x: sem("wa_" + x) for x in names}

        with nc.Block() as block:
            @block.sync
            def _(sp):
                def load(dst, name, done, a, b):
                    sp.dma_start(dst[:, a:b, :], d[name][2 * a:2 * b, :, :].rearrange("(t b) s e -> (b s) t e", b=2)
                                 ).then_inc(done[a], 16)

                load(sh.X, "x", x_loaded, *LOADS[0])
                sp.dma_start(sh.const[:], d["consts"]).then_inc(S["const_loaded"], 16)
                for i, w in enumerate(("Wq", "Wk", "Wv", "Wo")):
                    sp.dma_start(wrow[:, i, :], d["L0_" + w]).then_inc(S["loaded"], 16)
                    sp.dma_start(brow[i:i + 1, :], d["L0_b" + w[1]].rearrange("(a c) -> a c", a=1)).then_inc(S["loaded"], 16)
                load(sh.CTX, "ctx", ctx_loaded, *LOADS[0])
                load(sh.X, "x", x_loaded, *LOADS[1])
                load(sh.CTX, "ctx", ctx_loaded, *LOADS[1])
                ffn.first_loads(sp)

            @block.tensor
            def _(pe):
                pe.wait_ge(S["zeroed"], 1)
                for _ in range(WARM_UP):
                    nc.tensor.matmul(PJ, wT[:, 0, :], wT[:].rearrange("p a b -> p (a b)"), start=True, stop=True)
                pe.wait_ge(S["const_loaded"], 16)
                pe.wait_ge(S["loaded"], 128)
                for b2 in range(2):
                    half = slice(b2 * SEQ, (b2 + 1) * SEQ)
                    for i in range(4):
                        nc.tensor.matmul(PJ[half, i * SEQ:(i + 1) * SEQ], wrow[:, i, :], ident[:SEQ, :SEQ], start=True, stop=True)
                    last = nc.tensor.matmul(PJ[half, 4 * SEQ:4 * SEQ + 4], brow[:], ident[:4, :4], start=True, stop=True)
                last.then_inc(S["w_tr"], 1)
                pe.wait_ge(S["w_ready"], 1)

                def project_context(t, which, done):
                    ctx = sh.CTX[:, bass.ds(t, 1), :].rearrange("p a e -> p (a e)")
                    nc.tensor.matmul(PJ, wT[:, which, :], ctx, start=True, stop=True).then_inc(done, 1)

                def step(n, u, t):
                    q = u % 4
                    if live(t + 1, TT):
                        if q == 0:
                            if not isinstance(t, int) or t >= 0:
                                pe.wait_ge(S["v_ready"], t + 1)
                            if not isinstance(t, int) or t >= 2:
                                pe.wait_ge(norm.low_done, t - 1)
                            pe.wait_ge(S["normed"], t + 2)
                            nc.tensor.matmul(PJ, wT[:, 0, :], xn[:, (u // 4 + 1) % 2, :],
                                             start=True, stop=True).then_inc(S["q_mm"], 1)
                        if q == 1:
                            pe.wait_ge(S["q_biased"], t + 2)
                            project_context(t + 1, 1, S["k_mm"])
                        if q == 2:
                            pe.wait_ge(S["k_ready"], t + 2)
                            project_context(t + 1, 2, S["v_mm"])
                    if q == 3 and live(t - 2, TT - 1):
                        if live(t + 1, TT):
                            pe.wait_ge(S["v_ready"], t + 2)
                        else:
                            pe.wait_ge(norm.low_done, t - 1)
                        norm.transpose(pe, t - 2, u // 4, PJ)
                    c = n + 4
                    if isinstance(n, int) and c < TT:
                        pe.wait_ge(ctx_loaded[c], 16)
                        if c >= 2:
                            pe.wait_ge(S["ct_lo"], c - 1)
                        for k in range(EC):
                            last = nc.tensor.transpose(CT[c % 2][:, k * P:(k + 1) * P], sh.CTX[:, c, k * P:(k + 1) * P], ident)
                        last.then_inc(S["ct_tr"], 1)
                    if live(n, UNITS):
                        pe.wait_ge(S["q_ready"], t + 1)
                        pe.wait_ge(S["k_ready"], t + 1)
                        if not isinstance(n, int) or n >= 1:
                            pe.wait_ge(S["keyed"], n)
                    m, w = n - 3, (u - 3) % 8
                    if live(m, UNITS):
                        slot, qm = w // 4, w % 4
                        pe.wait_ge(S["v_ready"], t + 1 if q >= 3 else t)
                        if not isinstance(n, int) or m >= 1:
                            pe.wait_ge(S["vt_copied"], m)
                        if not isinstance(n, int) or m >= 3:
                            pe.wait_ge(S["x_added"], m - 2)
                        for g in range(2):
                            t0 = qm * UNIT_T + g * BLK
                            last = nc.tensor.transpose(VT[:, g * P:(g + 1) * P], vp[:, slot, t0:t0 + P], ident)
                        last.then_inc(S["vt_mm"], 1)
                    if live(n, UNITS):
                        for g in range(2):
                            for i in range(4):
                                for b2 in range(2):
                                    rows = slice(b2 * SEQ, (b2 + 1) * SEQ)
                                    blk = 8 * q + 2 * i + g
                                    last = nc.tensor.matmul(
                                        SC[i * KEYS:(i + 1) * KEYS, b2, g * P:(g + 1) * P],
                                        kp[rows, u // 4, blk * BLK:blk * BLK + KEYS],
                                        qx[rows, u // 4, blk, :, :].rearrange("p h t -> p (h t)"),
                                        start=True, stop=True)
                        last.then_inc(S["sc_mm"], 1)
                    m = n - 4
                    if live(m, UNITS):
                        pe.wait_ge(S["rowed"], m + 1)
                        pe.wait_ge(S["vt_copied"], m + 1)
                        if not isinstance(n, int) or m >= 1:
                            pe.wait_ge(S["oh_copied"], m)
                        else:
                            pe.wait_ge(S["ct_lo"], TT)
                    m = n - 5
                    if live(m, UNITS):
                        pe.wait_ge(S["oh_copied"], m + 1)
                        pe.wait_ge(S["vt_copied"], m + 3 if live(m + 2, UNITS) else UNITS)
                        if not isinstance(n, int) or m >= 1:
                            pe.wait_ge(S["x_added"], m)
                        nc.tensor.matmul(AO, wT[:, 3, :], oh[:, (u - 5) % 2, :], start=True, stop=True).then_inc(S["ao_mm"], 1)
                    m = n - 4
                    if live(m, UNITS):
                        for g in range(2):
                            for quarter in range(4):
                                for i in range(4):
                                    rows = slice(i * KEYS, (i + 1) * KEYS)
                                    chan = slice(quarter * 32, (quarter + 1) * 32)
                                    b2, half = quarter // 2, quarter % 2
                                    out = OH[chan, i, :].rearrange("p (h g t) -> p h g t", h=HH, g=2)[:, :, g, :]
                                    last = nc.tensor.matmul(out, vt[rows, u % 2, g, chan],
                                                            pt[rows, u % 2, b2, g, half * HH * BLK:(half + 1) * HH * BLK],
                                                            start=True, stop=True)
                        last.then_inc(S["oh_mm"], 1)

                pipeline(pe, step, *STEPS)

            @block.vector
            def _(vec):
                def statistics(k, tiles):
                    norm_stats(nc, vec, sh.X, tiles, stats, mv, veps, S["stats"], S["aggr"], S["veps"], x_loaded)
                    some = slice(tiles[0], tiles[-1] + 1)
                    vec.wait_ge(S["std"], k)
                    nc.vector.reciprocal(rstd[:, some], std[:, some]).then_inc(S["rstd"], 1)
                    vec.wait_ge(S["rstd"], k)

                statistics(1, range(FIRST))
                vec.wait_ge(S["const_loaded"], 16)
                vec.wait_ge(S["w_tr"], 1)
                vec.wait_ge(S["zeroed"], 1)
                for b2 in range(2):
                    half = slice(b2 * SEQ, (b2 + 1) * SEQ)
                    nc.vector.tensor_copy(wT[half, :, half], PJ[half, 0:4 * SEQ].rearrange("p (i c) -> p i c", i=4))
                nc.vector.tensor_copy(bias[:], PJ[:, 4 * SEQ:4 * SEQ + 4]).then_inc(S["w_ready"], 1)

                def normalise(t, slot):
                    if not isinstance(t, int) or t >= 2:
                        vec.wait_ge(S["q_mm"], t - 1)
                    one = bass.ds(t, 1)
                    nc.vector.tensor_scalar(xn[:, slot:slot + 1, :], sh.X[:, one, :], mv[:, one, 0], rstd[:, one],
                                            ALU.subtract, ALU.mult).then_inc(S["normed"], 1)

                def add_bias(t, which, mm, dst, ready):
                    vec.wait_ge(S[mm], t + 1)
                    nc.vector.tensor_scalar(dst, PJ, bias[:, which:which + 1], None, ALU.add).then_inc(S[ready], 1)

                normalise(0, 0)
                vec.wait_ge(S["padded"], 4)
                vec.wait_ge(S["w_ready"], 1)

                def step(n, u, t):
                    q, slot = u % 4, u // 4
                    c = n + 4
                    if isinstance(n, int) and n == 0:
                        statistics(2, range(FIRST, TT))
                    m, w = n - 1, (u - 1) % 4
                    if q == 1 and live(t - 2, TT - 1):
                        vec.wait_ge(S["x_added"], 4 * t - 4)
                    if live(m, UNITS):
                        vec.wait_ge(S["banded"], m + 1)
                        nc.vector.reduce_max(mx[:, w, :], sm[:, w, :, :], AX_X).then_inc(S["maxed"], 1)
                    if live(t + 1, TT):
                        if q == 0:
                            if not isinstance(t, int) or t >= 0:
                                vec.wait_ge(S["q_ready"], t + 1)
                            add_bias(t + 1, 0, "q_mm", qp[:], "q_biased")
                        if q == 1:
                            add_bias(t + 1, 1, "k_mm", kp[:, 1 - slot, PAD:PAD + E], "k_ready")
                        if q == 2:
                            if not isinstance(t, int) or t >= 1:
                                vec.wait_ge(S["vt_mm"], 4 * t)
                            add_bias(t + 1, 2, "v_mm", vp[:, 1 - slot, PAD:PAD + E], "v_ready")
                    if q == 3 and live(t + 2, TT) and (not isinstance(t, int) or t >= -1):
                        normalise(t + 2, slot)
                    if q == 1 and live(t - 2, TT - 1):
                        norm.count(vec, t - 2, slot)
                        norm.await_count(vec, t - 2)
                    if q == 2 and live(t - 2, TT - 1):
                        norm.normalise(vec, t - 2, slot)
                    if q == 3 and live(t - 2, TT - 1):
                        norm.high_by_vector(vec, t - 2, PJ)
                        norm.low(vec, t - 2, PJ)
                    m, w = n - 2, (u - 2) % 4
                    if live(m, UNITS):
                        vec.wait_ge(S["exped"], m + 1)
                        nc.vector.reduce_sum(su[:, w, :], sm[:, w, :, :], AX_X).then_inc(S["summed"], 1)
                        vec.wait_ge(S["summed"], m + 1)
                        nc.vector.reciprocal(rc[:, w, :], su[:, w, :]).then_inc(S["recip"], 1)
                    if q == 1 and live(t - 2, TT - 1):
                        norm.aggregate(vec, t - 2, slot)
                    m, w = n - 3, (u - 3) % 4
                    if live(m, UNITS):
                        vec.wait_ge(S["probs"], m + 1)
                        if not isinstance(n, int) or m >= 2:
                            vec.wait_ge(S["oh_mm"], m - 1)
                        nc.vector.transpose(pt[:, w % 2, :, :, :].rearrange("p b g x -> p (b g x)"),
                                            sm[:, w, :, :].rearrange("p a k -> p (a k)")).then_inc(S["rowed"], 1)
                    if live(n, UNITS):
                        vec.wait_ge(S["sc_mm"], n + 1)
                        if not isinstance(n, int) or n >= 4:
                            vec.wait_ge(S["rowed"], n - 3)
                        nc.vector.transpose(sm[:, u % 4, :, :].rearrange("p (b x) k -> p b (x k)", b=2),
                                            SC).then_inc(S["keyed"], 1)
                    m, w = n - 5, (u - 5) % 4
                    if live(m, UNITS):
                        vec.wait_ge(S["ao_mm"], m + 1)
                        x = sh.X[:, bass.ds(t - 1 if q >= 1 else t - 2, 1),
                                 w * UNIT_T:(w + 1) * UNIT_T]
                        nc.vector.scalar_tensor_tensor(x, AO.rearrange("p (a e) -> p a e", a=1), bias[:, 3:4], x,
                                                       ALU.add, ALU.add).then_inc(S["x_added"], 1)
                    m = n - 4
                    if live(m, UNITS):
                        vec.wait_ge(S["oh_mm"], m + 1)
                        if not isinstance(n, int) or m >= 2:
                            vec.wait_ge(S["ao_mm"], m - 1)
                        own = oh[:, u % 2, :].rearrange("p (i x) -> p i x", i=4)
                        for h in range(HH):
                            part = OH[:, :, h * 2 * BLK:(h + 1) * 2 * BLK]
                            if h == 0:
                                nc.vector.tensor_scalar(own, part, hh4[:, h:h + 1], None, ALU.mult).then_inc(S["selected"], 1)
                            else:
                                vec.wait_ge(S["selected"], (HH - 1) * m + h)
                                nc.vector.scalar_tensor_tensor(own, part, hh4[:, h:h + 1], own, ALU.mult,
                                                               ALU.add).then_inc(S["selected" if h < HH - 1 else "oh_copied"], 1)
                    if isinstance(n, int) and c < TT:
                        vec.wait_ge(S["ct_hi"], c + 1)
                        tok = slice(c * P, (c + 1) * P)
                        nc.vector.tensor_tensor(sh.CTl[:, :, tok], CT[c % 2].rearrange("p (c n) -> p c n", c=EC),
                                                sh.CTh[:, :, tok].bitcast(F32), ALU.subtract).then_inc(S["ct_lo"], 1)

                pipeline(vec, step, *STEPS)

            @block.gpsimd
            def _(gp):
                nc.gpsimd.memset(wT[:], 0.0).then_inc(S["zeroed"], 1)
                nc.gpsimd.memset(ffn.agu, 0.0).then_inc(ffn.agu_zeroed, 1)
                for padded in (kp, vp):
                    nc.gpsimd.memset(padded[:, :, 0:PAD], 0.0).then_inc(S["padded"], 1)
                    nc.gpsimd.memset(padded[:, :, PAD + E:], 0.0).then_inc(S["padded"], 1)
                norm.give_credits(gp)
                gp.wait_ge(S["const_loaded"], 16)

                def step(n, u, t):
                    m, w = n - 1, (u - 1) % 4
                    if live(m, UNITS):
                        gp.wait_ge(S["maxed"], m + 1)
                        s = sm[:, w, :, :]
                        nc.gpsimd.tensor_tensor(s, s, mx[:, w, :].unsqueeze(2).broadcast_to([P, 16, KEYS]),
                                                ALU.subtract).then_inc(S["subbed"], 1)
                    m, w = n - 2, (u - 2) % 4
                    if live(m, UNITS):
                        gp.wait_ge(S["recip"], m + 1)
                        s = sm[:, w, :, :]
                        nc.gpsimd.tensor_tensor(s, s, rc[:, w, :].unsqueeze(2).broadcast_to([P, 16, KEYS]),
                                                ALU.mult).then_inc(S["probs"], 1)
                    if live(n, UNITS):
                        gp.wait_ge(S["keyed"], n + 1)
                        s = sm[:, u % 4, :, :]
                        nc.gpsimd.tensor_tensor(s, s, band.unsqueeze(1).broadcast_to([P, 16, KEYS]),
                                                ALU.add).then_inc(S["banded"], 1)

                pipeline(gp, step, *STEPS)

            @block.scalar
            def _(act):
                def deviations(k, tiles):
                    some = slice(tiles[0], tiles[-1] + 1)
                    act.wait_ge(S["veps"], k)
                    nc.scalar.activation(std[:, some], veps[:, some], ACT.Sqrt).then_inc(S["std"], 1)

                deviations(1, range(FIRST))
                act.wait_ge(S["const_loaded"], 16)

                def step(n, u, t):
                    q, slot = u % 4, u // 4
                    c = n + 4
                    if isinstance(n, int) and n == 0:
                        deviations(2, range(FIRST, TT))
                    m = n - 3
                    if live(m, UNITS):
                        act.wait_ge(S["vt_mm"], m + 1)
                        if not isinstance(n, int) or m >= 2:
                            act.wait_ge(S["oh_mm"], m - 1)
                        nc.scalar.activation(vt[:, (u - 3) % 2, :, :].rearrange("p g x -> p (g x)"), VT,
                                             ACT.Copy).then_inc(S["vt_copied"], 1)
                    m, w = n - 1, (u - 1) % 4
                    if live(m, UNITS):
                        act.wait_ge(S["subbed"], m + 1)
                        nc.scalar.activation(sm[:, w, :, :], sm[:, w, :, :], ACT.Exp, scale=WD ** -0.5).then_inc(S["exped"], 1)
                    if q == 1 and live(t - 2, TT - 1):
                        norm.root(act, t - 2, slot)
                    if q >= 1 and live(t + 1, TT):
                        if q == 1:
                            act.wait_ge(S["q_biased"], t + 2)
                            if not isinstance(t, int) or t >= 1:
                                act.wait_ge(S["sc_mm"], 4 * t)
                        for h in range(3 * q - 3, min(3 * q, WH)):
                            last = nc.scalar.activation(qx[:, 1 - slot, :, h, :], qp[:].rearrange("p (k t) -> p k t", t=BLK),
                                                        ACT.Copy, scale=hm[:, h:h + 1])
                        if q == 3:
                            last.then_inc(S["q_ready"], 1)
                    if isinstance(n, int) and c < TT:
                        act.wait_ge(S["ct_tr"], c + 1)
                        nc.scalar.activation(sh.CTh[:, :, c * P:(c + 1) * P], CT[c % 2].rearrange("p (c n) -> p c n", c=EC),
                                             ACT.Copy).then_inc(S["ct_hi"], 1)

                pipeline(act, step, *STEPS)


def width(i):
    return INTER - (IT - 1) * P if isinstance(i, int) and i == IT - 1 else P


class GatedInputs:

    SIZE = 7 * E + 2 * IT

    def __init__(self, nc, st, room, d):
        sem = allocator(nc, st)[1]
        self.d = d
        graw, uraw, draw, self.ad, agu = views(room, 2 * E, 2 * E, 2 * E, E, 2 * IT)
        self.agu = agu.rearrange("p (i a) -> p i a", a=2)
        self.graw, self.uraw = (x.rearrange("p (a e) -> p a e", a=2) for x in (graw, uraw))
        self.draw = draw.rearrange("p (a c n) -> p a c n", a=2, c=EC)
        self.loaded = [sem("ff_loaded0"), sem("ff_loaded1")]
        self.agu_zeroed, self.scales = sem("ff_agu_zeroed"), sem("ff_scales")

    def load(self, sp, i, slot):
        w, done = width(i), self.loaded[slot]
        rows = bass.ds(i * P, w)
        sp.dma_start(self.graw[:w, slot, :], self.d["L0_Wg"][rows, :]).then_inc(done, 16)
        sp.dma_start(self.uraw[:w, slot, :], self.d["L0_Wu"][rows, :]).then_inc(done, 16)
        sp.dma_start(self.draw[:, slot, :, :w],
                     self.d["L0_Wd"].rearrange("(c p) i -> p c i", p=P)[:, :, rows]).then_inc(done, 16)

    def first_loads(self, sp):
        full = IT - 1
        self.load(sp, 0, 0)
        self.load(sp, 1, 1)
        sp.wait_ge(self.agu_zeroed, 1)
        for name, dst in (("L0_ag", self.agu[:, :, 0]), ("L0_au", self.agu[:, :, 1])):
            sp.dma_start(dst[:, 0:full], self.d[name][0:full * P].rearrange("(i p) -> p i", p=P),
                         allow_slow_non_contiguous=True).then_inc(self.scales, 16)
            sp.dma_start(dst[:width(full), full:IT], self.d[name][full * P:INTER].rearrange("(p a) -> p a", a=1),
                         allow_slow_non_contiguous=True).then_inc(self.scales, 16)
        sp.dma_start(self.ad, self.d["L0_ad"].partition_broadcast(P)).then_inc(self.scales, 16)


def gated_ffn(nc, sh, norm, ffn, next_norm, cross):
    HALF = TT * P // 2
    STEPS = (0, 4, 10, IT + 2, 2, 2)
    with ExitStack() as st:
        sb, sem = allocator(nc, st)
        ident = sh.const[:, C_ID:C_HM]
        graw, uraw, draw = ffn.graw, ffn.uraw, ffn.draw
        gT, uT, dT = ([sb(f"ff_{x}T{part}", [P, 2, E], F32R) for part in ("h", "l")] for x in "gud")
        col = sb("ff_col", [P, 2, 2])
        pi = sb("ca_pi", [P, TT], I32)
        dad = sb("ff_dad", [P, E])
        sg = sb("ff_sg", [P, 2, HALF])
        hf = sb("ff_hf", [P, 2, HALF])
        hh, hl = (sb("ff_h" + x, [P, 2, 2 * HALF], F32R) for x in "hl")

        T = [sh.PS[:, 0, :], sh.PS[:, 1, :]]
        G, U = sh.PS[:, 2, :], sh.PS[:, 3, :]
        D = sh.PS[:, 4:8, :]

        names = ("columns d_scaled g_tr u_tr d_tr g_hi u_hi d_hi g_split u_split d_split "
                 "g_mm u_mm silu gated h_hi h_split d_mm added").split()
        S = {x: sem("ff_" + x) for x in names}

        with nc.Block() as block:
            @block.sync
            def _(sp):
                cross.first_loads(sp)
                with sp.Fori(0, 4) as i:
                    for u in range(2):
                        sp.wait_ge(S["d_tr"], 2 * i + u + 1)
                        ffn.load(sp, 2 * i + u + 2, u)
                sp.wait_ge(S["d_tr"], IT - 2)
                ffn.load(sp, IT - 1, (IT - 1) % 2)
                for load, p, chunk in ((cross.load_q, 2, 2), (cross.load_q, 3, 3), (cross.load_o, 0, 4), (cross.load_o, 1, 5)):
                    sp.wait_ge(cross.w_split, chunk - 1)
                    load(sp, 0, p)

            @block.tensor
            def _(pe):
                def transposes(bank, raw, slot, w, done):
                    for c in range(EC):
                        if raw is draw:
                            last = nc.tensor.transpose(bank[:w, c * P:(c + 1) * P], raw[:, slot, c, :w], ident)
                        else:
                            last = nc.tensor.transpose(bank[:, c * P:c * P + w], raw[:w, slot, c * P:(c + 1) * P],
                                                       ident[:w, :w])
                    last.then_inc(S[done], 1)

                def inner(out, wT, slot, half, w):
                    tok = slice(half * HALF, (half + 1) * HALF)
                    for c in range(EC):
                        cols = slice(c * P, c * P + w)
                        last = mm3(nc, out[:w, :], wT[0][:, slot, cols], wT[1][:, slot, cols],
                                   sh.NTh[:, c, tok], sh.NTl[:, c, tok], c == 0, c == EC - 1)
                    return last

                def down(i, slot, tiles, w):
                    for t in tiles:
                        if not isinstance(i, int) or 8 * i + t >= 4:
                            pe.wait_ge(S["added"], 8 * i + (t - 3))
                        tok = slice(t * P, (t + 1) * P)
                        mm3(nc, D[:, t % 4, :], hh[:w, slot, tok], hl[:w, slot, tok],
                            dT[0][:w, slot, :], dT[1][:w, slot, :], True, True).then_inc(S["d_mm"], 1)

                def step(s, u, j):
                    i, o = s - 1, s - 2
                    past = not isinstance(s, int)
                    if live(s, IT):
                        pe.wait_ge(ffn.loaded[u], 48 * j + 48)
                        if past or s >= 2:
                            pe.wait_ge(S["d_scaled"], s - 1)
                        elif s == 1:
                            pe.wait_ge(S["g_split"], 1)
                        transposes(T[0], graw, u, width(s), "g_tr")
                    if isinstance(i, int) and i == 0:
                        norm.transpose(pe, TT - 1, (TT - 1) % 2, D[:, 3, :])
                    if live(i, IT):
                        pe.wait_ge(S["g_split"], i + 1)
                        if past or i >= 1:
                            pe.wait_ge(S["silu"], 2 * i)
                        inner(G, gT, 1 - u, 0, width(i)).then_inc(S["g_mm"], 1)
                    if isinstance(s, int) and s == IT + 1:
                        pe.wait_ge(S["d_scaled"], IT)
                        pe.wait_ge(S["u_split"], IT)
                        for k in range(4):
                            cross.table_transposes(pe, k, T[k % 2])
                    if live(o, IT):
                        pe.wait_ge(S["h_split"], 2 * o + 2)
                        pe.wait_ge(S["d_split"], o + 1)
                        down(o, u, (0, 1), width(o))
                    if live(s, IT):
                        if past or s >= 1:
                            pe.wait_ge(S["u_split"], s)
                        transposes(T[1], uraw, u, width(s), "u_tr")
                    if live(i, IT):
                        pe.wait_ge(S["u_split"], i + 1)
                        if past or i >= 1:
                            pe.wait_ge(S["gated"], 2 * i)
                        inner(U, uT, 1 - u, 0, width(i)).then_inc(S["u_mm"], 1)
                    if live(o, IT):
                        down(o, u, (2, 3), width(o))
                    if live(i, IT):
                        pe.wait_ge(S["g_split"], min(s + 1, IT) if isinstance(s, int) else s + 1)
                        transposes(T[0], draw, 1 - u, width(i), "d_tr")
                        pe.wait_ge(S["silu"], 2 * i + 1)
                        if isinstance(i, int) and i == 0:
                            pe.wait_ge(norm.low_done, TT + 1)
                        inner(G, gT, 1 - u, 1, width(i)).then_inc(S["g_mm"], 1)
                    if live(o, IT):
                        down(o, u, (4, 5), width(o))
                    if live(i, IT):
                        pe.wait_ge(S["gated"], 2 * i + 1)
                        inner(U, uT, 1 - u, 1, width(i)).then_inc(S["u_mm"], 1)
                    if live(o, IT):
                        down(o, u, (6, 7), width(o))

                pipeline(pe, step, *STEPS)

            @block.scalar
            def _(act):
                def high(bank, wT, slot, w, tr, done, free):
                    act.wait_ge(*tr)
                    if free:
                        act.wait_ge(*free)
                    src, dst = bank.rearrange("p (c n) -> p c n", c=EC), wT[0][:, slot, :].rearrange("p (c n) -> p c n", c=EC)
                    nc.scalar.activation(dst[:, :, :w], src[:, :, :w], ACT.Copy).then_inc(S[done], 1)

                def silu(i, half, w, column):
                    act.wait_ge(S["g_mm"], 2 * i + half + 1)
                    if not isinstance(i, int) or i >= 1:
                        act.wait_ge(S["gated"], 2 * i + half - 1)
                    act.wait_ge(S["columns"], i + 1)
                    nc.scalar.activation(sg[:w, half, :], G[:w, :], ACT.Silu, scale=column).then_inc(S["silu"], 1)

                def h_high(i, slot, half, w):
                    act.wait_ge(S["gated"], 2 * i + half + 1)
                    if not isinstance(i, int) or i >= 2:
                        act.wait_ge(S["d_mm"], 8 * i - 8)
                    nc.scalar.activation(hh[:w, slot, half * HALF:(half + 1) * HALF], hf[:w, half, :],
                                         ACT.Copy).then_inc(S["h_hi"], 1)

                norm.root(act, TT - 1, (TT - 1) % 2)

                def step(s, u, j):
                    i = s - 1
                    past = not isinstance(s, int)
                    if isinstance(i, int) and i == 0:
                        norm.high(act, TT - 1, D[:, 3, :])
                    if isinstance(s, int):
                        for p in cross.SPLITS.get(s, ()):
                            cross.first_high(act, p)
                        if s == IT + 1:
                            cross.gate_high(act)
                            for k in range(4):
                                cross.table_copy(act, k, T[k % 2])
                    if live(s, IT):
                        high(T[0], gT, u, width(s), (S["g_tr"], s + 1), "g_hi",
                             (S["g_mm"], 2 * s - 2) if past or s >= 2 else None)
                    if live(i, IT):
                        a = col[:width(i), 1 - u, 0:1]
                        silu(i, 0, width(i), a)
                    if live(s, IT):
                        high(T[1], uT, u, width(s), (S["u_tr"], s + 1), "u_hi",
                             (S["u_mm"], 2 * s - 2) if past or s >= 2 else None)
                    if live(i, IT):
                        h_high(i, 1 - u, 0, width(i))
                        act.wait_ge(S["d_scaled"], i + 1)
                        if past or i >= 2:
                            act.wait_ge(S["d_mm"], 8 * i - 8)
                        nc.scalar.activation(dT[0][:width(i), 1 - u, :], dad[:width(i), :], ACT.Copy).then_inc(S["d_hi"], 1)
                        silu(i, 1, width(i), a)
                        h_high(i, 1 - u, 1, width(i))

                pipeline(act, step, *STEPS)


            @block.vector
            def _(vec):
                vec.wait_ge(ffn.scales, 80)
                norm.count(vec, TT - 1, (TT - 1) % 2)
                norm.await_count(vec, TT - 1)
                norm.aggregate(vec, TT - 1, (TT - 1) % 2)
                norm.normalise(vec, TT - 1, (TT - 1) % 2)

                def low(bank, wT, slot, w, hi, done):
                    vec.wait_ge(*hi)
                    src = bank.rearrange("p (c n) -> p c n", c=EC)[:, :, :w]
                    hi_part, dst = (x[:, slot, :].rearrange("p (c n) -> p c n", c=EC)[:, :, :w] for x in wT)
                    nc.vector.tensor_tensor(dst, src, hi_part.bitcast(F32), ALU.subtract).then_inc(S[done], 1)

                def gate(i, half, w, column):
                    vec.wait_ge(S["u_mm"], 2 * i + half + 1)
                    vec.wait_ge(S["silu"], 2 * i + half + 1)
                    if not isinstance(i, int) or i >= 1:
                        vec.wait_ge(S["h_split"], 2 * i + half - 1)
                    nc.vector.scalar_tensor_tensor(hf[:w, half, :], U[:w, :], column, sg[:w, half, :],
                                                   ALU.mult, ALU.mult).then_inc(S["gated"], 1)

                def add_down(o, tiles):
                    for t in tiles:
                        vec.wait_ge(S["d_mm"], 8 * o + t + 1)
                        nc.vector.tensor_tensor(sh.X[:, t, :], sh.X[:, t, :], D[:, t % 4, :], ALU.add).then_inc(S["added"], 1)

                def step(s, u, j):
                    i, o = s - 1, s - 2
                    past = not isinstance(s, int)
                    if isinstance(i, int) and i == 0:
                        norm.low(vec, TT - 1, D[:, 3, :])
                    if isinstance(s, int) and s == 3:
                        cross.make_cap(vec)
                    if live(s, IT):
                        low(T[0], gT, u, width(s), (S["g_hi"], s + 1), "g_split")
                    if live(o, IT):
                        add_down(o, (0, 1))
                    if live(s, IT):
                        low(T[1], uT, u, width(s), (S["u_hi"], s + 1), "u_split")
                    if live(i, IT):
                        a = col[:width(i), 1 - u, 1:2]
                        gate(i, 0, width(i), a)
                    if live(o, IT):
                        add_down(o, (2, 3))
                    if live(i, IT):
                        vec.wait_ge(S["d_tr"], i + 1)
                        if past or i >= 1:
                            vec.wait_ge(S["d_split"], i)
                        nc.vector.tensor_tensor(dad[:width(i), :], T[0][:width(i), :], ffn.ad[:width(i), :],
                                                ALU.mult).then_inc(S["d_scaled"], 1)
                    if live(o, IT):
                        add_down(o, (4, 5))
                    if live(i, IT):
                        gate(i, 1, width(i), a)
                    if live(o, IT):
                        add_down(o, (6, 7))

                pipeline(vec, step, *STEPS)
            @block.gpsimd
            def _(gp):
                next_norm.give_credits(gp)
                gp.wait_ge(ffn.scales, 80)

                def h_low(i, slot, half, w):
                    gp.wait_ge(S["h_hi"], 2 * i + half + 1)
                    tok = slice(half * HALF, (half + 1) * HALF)
                    nc.gpsimd.tensor_tensor(hl[:w, slot, tok], hf[:w, half, :], hh[:w, slot, tok].bitcast(F32),
                                            ALU.subtract).then_inc(S["h_split"], 1)

                def step(s, u, j):
                    if isinstance(s, int):
                        if s == 3:
                            cross.gather_rotary(gp, pi)
                        for p in cross.SPLITS.get(s, ()):
                            cross.first_low(gp, p)
                    if live(s, IT):
                        if not isinstance(s, int) or s >= 2:
                            gp.wait_ge(S["gated"], 2 * s - 2)
                        nc.gpsimd.tensor_copy(col[:, u, :], ffn.agu[:, bass.ds(s, 1), :].rearrange("p a b -> p (a b)")
                                              ).then_inc(S["columns"], 1)
                    if live(s - 1, IT):
                        w = width(s - 1)
                        h_low(s - 1, 1 - u, 0, w)
                        gp.wait_ge(S["d_hi"], s)
                        nc.gpsimd.tensor_tensor(dT[1][:w, 1 - u, :], dad[:w, :], dT[0][:w, 1 - u, :].bitcast(F32),
                                                ALU.subtract).then_inc(S["d_split"], 1)
                        h_low(s - 1, 1 - u, 1, w)

                pipeline(gp, step, *STEPS)
                cross.gate_low(gp)



class CrossInputs:
    SPLITS = {10: (0, 1), 11: (2,), 12: (3,)}

    def __init__(self, nc, sh, st, d):
        sb, sem = allocator(nc, st)
        self.nc, self.sh, self.d = nc, sh, d
        self.raw = sb("ca_raw", [P, 2, QC])
        self.kvraw = sb("ca_kvraw", [P, EC, KVC])
        self.wq = [sb(f"ca_wq{part}", [P, 2, EC, QC], F32R) for part in ("h", "l")]
        self.rot = sh.qT.rearrange("p (t c) -> p t c", t=TT)
        self.cosT, self.sinT = (sb("ca_" + x, [P, TT * P]) for x in ("cosT", "sinT"))
        self.cap = sb("ca_cap", [P, TT, P])
        self.mask = self.cap[:].rearrange("p t k -> p (t k)").bitcast(I32)
        self.graw = sb("rf_graw", [P, EC, EXPERTS])
        self.gw = [sb(f"rf_gw{part}", [P, EC, EXPERTS], F32R) for part in ("h", "l")]
        self.raw_loaded = [sem("ca_raw0"), sem("ca_raw1")]
        self.kv_loaded, self.mask_loaded, self.pos_loaded, self.rot_loaded, self.gate_loaded = (
            sem("ca_" + x + "_loaded") for x in ("kv", "mask", "pos", "rot", "gate"))
        self.masked, self.w_hi, self.w_split, self.gate_hi, self.table_mm, self.table_copied = (
            sem("ca_" + x) for x in ("masked", "w_hi", "w_split", "gate_hi", "table_mm", "table_copied"))

    def load_q(self, sp, g, p):
        sp.dma_start(self.raw[:, p % 2, :], self.d["L1_Wq"][p * P:(p + 1) * P, bass.ds(g * QC, QC)]
                     ).then_inc(self.raw_loaded[p % 2], 16)

    def load_o(self, sp, g, p):
        sp.dma_start(self.raw[:, p % 2, :], self.d["L1_Wo"][bass.ds(g * QC + p * P, P), :]).then_inc(self.raw_loaded[p % 2], 16)

    def load_kv(self, sp, g):
        for x, name in enumerate(("L1_Wk", "L1_Wv")):
            sp.dma_start(self.kvraw[:, :, x * HD:(x + 1) * HD],
                         self.d[name][:, bass.ds(g * HD, HD)].rearrange("(c p) n -> p c n", p=P)).then_inc(self.kv_loaded, 16)

    def first_loads(self, sp):
        self.load_q(sp, 0, 0)
        self.load_q(sp, 0, 1)
        self.load_kv(sp, 0)
        for h2 in range(2):
            sp.dma_start(self.mask[h2 * SEQ:(h2 + 1) * SEQ, :].rearrange("p (b k) -> p b k", k=SEQ),
                         self.d["mask"].rearrange("b q k -> q b k")).then_inc(self.mask_loaded, 16)
        sp.dma_start(self.graw[:], self.d["gate_w"].rearrange("(c p) e -> p c e", p=P)).then_inc(self.gate_loaded, 16)

    def gather_rotary(self, gp, pi):
        gp.dma_start(pi[:], self.d["pos"].rearrange("(t b) s -> (b s) t", b=2),
                     allow_slow_non_contiguous=True).then_inc(self.pos_loaded, 16)
        gp.wait_ge(self.pos_loaded, 16)
        for t in range(TT):
            gp.indirect_dma_start(self.rot[:, t, :], None, self.d["rotary"],
                                  bass.IndirectOffsetOnAxis(ap=pi[:, t:t + 1], axis=0)).then_inc(self.rot_loaded, 16)

    def make_cap(self, vec):
        vec.wait_ge(self.mask_loaded, 32)
        flat = self.cap[:].rearrange("p t k -> p (t k)")
        self.nc.vector.tensor_scalar(flat, self.mask, 0.0, 3e38, ALU.not_equal, ALU.mult).then_inc(self.masked, 1)
        vec.wait_ge(self.masked, 1)
        self.nc.vector.tensor_scalar(flat, flat, MASKED, None, ALU.add).then_inc(self.masked, 1)

    def table_transposes(self, pe, k, bank):
        half = slice(k // 2 * HD, (k // 2 + 1) * HD)
        if k == 0:
            pe.wait_ge(self.rot_loaded, 16 * TT)
        if k >= 2:
            pe.wait_ge(self.table_copied, k - 1)
        for i in range(4):
            last = self.nc.tensor.transpose(bank[:, i * P:(i + 1) * P], self.rot[:, 4 * (k % 2) + i, half],
                                            self.sh.const[:, C_ID:C_HM])
        last.then_inc(self.table_mm, 1)

    def table_copy(self, act, k, bank):
        act.wait_ge(self.table_mm, k + 1)
        self.nc.scalar.activation((self.cosT, self.sinT)[k // 2][:, k % 2 * 4 * P:(k % 2 + 1) * 4 * P], bank,
                                  ACT.Copy).then_inc(self.table_copied, 1)

    def first_high(self, act, p):
        act.wait_ge(self.raw_loaded[p % 2], 16 * (p // 2 + 1))
        self.nc.scalar.activation(self.wq[0][:, 0, p, :], self.raw[:, p % 2, :], ACT.Copy).then_inc(self.w_hi, 1)

    def first_low(self, gp, p):
        gp.wait_ge(self.w_hi, p + 1)
        self.nc.gpsimd.tensor_tensor(self.wq[1][:, 0, p, :], self.raw[:, p % 2, :], self.wq[0][:, 0, p, :].bitcast(F32),
                                     ALU.subtract).then_inc(self.w_split, 1)

    def gate_high(self, act):
        act.wait_ge(self.gate_loaded, 16)
        self.nc.scalar.activation(self.gw[0][:], self.graw[:], ACT.Copy).then_inc(self.gate_hi, 1)

    def gate_low(self, gp):
        gp.wait_ge(self.gate_hi, 1)
        self.nc.gpsimd.tensor_tensor(self.gw[1][:], self.graw[:], self.gw[0][:].bitcast(F32), ALU.subtract)


def cross_attention(nc, sh, d, norm, next_norm, cross):
    UNITS = KVH * TT
    AHEAD = 8
    PAIR = 2 * P
    STEPS = (-EC, 8, UNITS - AHEAD, UNITS + 5, 16, TT)
    with ExitStack() as st:
        sb, sem = allocator(nc, st)
        ident = sh.const[:, C_ID:C_HM]
        raw, kvraw, wq, cap, cosT, sinT = cross.raw, cross.kvraw, cross.wq, cross.cap, cross.cosT, cross.sinT
        wo = [sb(f"ca_wo{part}", [P, 2, EC, QC], F32R) for part in ("h", "l")]
        wkv = [sb(f"ca_wkv{part}", [P, 2, EC, KVC], F32R) for part in ("h", "l")]
        xc, xs, V, sm, kT, pT, K = views(sh.room, 3 * PAIR, 3 * PAIR, 4 * HD, 2 * 4 * SEQ, 2 * PAIR, 2 * P, HD)
        V = V.rearrange("p (a c) -> p a c", a=4)
        sm = sm.rearrange("p (a x k) -> p a x k", a=2, x=4)
        kT = kT.rearrange("p (a k) -> p a k", a=2)
        qT = sh.qT[:].rearrange("p (a h b x) -> p a h b x", a=2, h=2, b=4)
        mx, su, rc = (sb("ca_" + x, [P, 2, 4]) for x in ("mx", "su", "rc"))
        aT = [sb(f"ca_aT{part}", [P, GRP, P], F32R) for part in ("h", "l")]

        QT = sh.PS[:, 0, :]
        KT = sh.PS[:, 1, 0:PAIR]
        KV = sh.PS[:, 2, 0:KVC]
        PP = sh.PS[:, 3, 0:2 * P]
        SC = sh.PS[:, 4, 0:4 * SEQ]
        AV = sh.PS[:, 5:7, 0:2 * P]
        O = sh.PS[:, 7, :]

        names = ("kv_hi kv_split kv_mm kv_copied qk_mm rope_read roped "
                 "sc_mm capped maxed subbed exped summed recip probs pp_mm pp_copied av_mm av_hi av_lo o_mm added").split()
        S = {x: sem("ca_" + x) for x in names}
        S["w_hi"], S["w_split"] = cross.w_hi, cross.w_split
        FIRST = range(2)
        TAIL = {UNITS: 0, UNITS + 1: 2, UNITS + 3: 4}

        def rows_due(n):
            if isinstance(n, int) and n in range(3):
                return norm, (2 * n + 2, 2 * n + 3), [sh.PS[:, 5, :], sh.PS[:, 6, :]]
            if isinstance(n, int) and n in TAIL:
                return next_norm, (TAIL[n], TAIL[n] + 1), [sh.PS[:, 0, :], sh.PS[:, 1, :]]
            return None, (), None

        def gp_of(u):
            return u // 8 % 2

        with nc.Block() as block:
            @block.sync
            def _(sp):
                def load(chunk_loader, g, p, before):
                    sp.wait_ge(S["w_split"], 8 * g + (before - 1))
                    chunk_loader(sp, g, p)

                load(cross.load_o, 0, 2, 6)
                load(cross.load_o, 0, 3, 7)
                with sp.Fori(1, KVH) as g:
                    for p in range(EC):
                        load(cross.load_q, g, p, p)
                        if p == 1:
                            cross.load_kv(sp, g)
                    for p in range(EC):
                        load(cross.load_o, g, p, EC + p)
                for p in range(EC):
                    sp.wait_ge(S["w_split"], 8 * KVH - 1 + p)
                    sp.dma_start(raw[:, p % 2, :], d["experts"][0, p * P:(p + 1) * P, :]).then_inc(cross.raw_loaded[p % 2], 16)

            def split_source(u, g):
                w = (u + AHEAD) % 16
                p, par = w % 8, w // 8
                if p < EC:
                    return [(raw[:, p % 2, :], [x[:, par, p, :] for x in wq],
                             (cross.raw_loaded[p % 2], 64 * g + 16 * (p // 2 + 1)))]
                p -= EC
                return [(kvraw[:, p, :], [x[:, par, p, :] for x in wkv], (cross.kv_loaded, 32 * g + 32)),
                        (raw[:, p % 2, :], [x[:, par, p, :] for x in wo],
                         (cross.raw_loaded[p % 2], 64 * g + 32 + 16 * (p // 2 + 1)))]

            @block.tensor
            def _(pe):
                def step(n, u, g):
                    past = not isinstance(n, int)
                    t, j = u % TT, u % 2
                    if live(n, UNITS):
                        par = gp_of(u)
                        if t == 0:
                            pe.wait_ge(S["kv_split"], EC * g + EC)
                        if past or n >= 1:
                            pe.wait_ge(S["kv_copied"], n)
                        pair, tok = slice((t - j) * P, (t - j + 2) * P), slice(t * P, (t + 1) * P)
                        for c in range(EC):
                            last = mm3(nc, KV, sh.CTh[:, c, tok], sh.CTl[:, c, tok],
                                       wkv[0][:, par, c, :], wkv[1][:, par, c, :], c == 0, c == EC - 1)
                        last.then_inc(S["kv_mm"], 1)
                        if t == 0:
                            pe.wait_ge(S["w_split"], 8 * g + EC)
                        if not past and j == 0 and n < TT:
                            pe.wait_ge(norm.low_done, n + 3)
                        if past or n >= 1:
                            pe.wait_ge(S["rope_read"], n)
                        for member in range(2):
                            head = slice((2 * j + member) * HD, (2 * j + member + 1) * HD)
                            for c in range(EC):
                                mm3(nc, QT[:, member * PAIR:(member + 1) * PAIR], wq[0][:, par, c, head], wq[1][:, par, c, head],
                                    sh.NTh[:, c, pair], sh.NTl[:, c, pair], c == 0, c == EC - 1)
                        pe.wait_ge(S["kv_copied"], n + 1)
                        nc.tensor.transpose(KT[:, j * P:(j + 1) * P], K, ident).then_inc(S["qk_mm"], 1)
                    rows, tiles, banks = rows_due(n)
                    if tiles:
                        if n == UNITS:
                            pe.wait_ge(S["rope_read"], UNITS)
                        rows.several_by_tensor(pe, tiles, banks)
                    m = n - 2
                    if live(m, UNITS):
                        slot = (u - 2) // 2 % 2
                        pe.wait_ge(S["roped"], n - j)
                        if past or m >= 1:
                            pe.wait_ge(S["capped"], m)
                        for hp in range(2):
                            for b2 in range(2):
                                c0, b = 2 * hp + b2, 2 * j + b2
                                last = nc.tensor.matmul(SC[:, c0 * SEQ:(c0 + 1) * SEQ], qT[:, slot, hp, b, :],
                                                        kT[:, slot, b * SEQ:(b + 1) * SEQ], start=True, stop=True)
                        last.then_inc(S["sc_mm"], 1)
                    m = n - 3
                    if live(m, UNITS):
                        pe.wait_ge(S["probs"], m + 1)
                        if past or m >= 1:
                            pe.wait_ge(S["pp_copied"], m)
                        for hp in range(2):
                            last = nc.tensor.transpose(PP[:, hp * P:(hp + 1) * P],
                                                       sm[:, (u - 3) % 2, 2 * hp:2 * hp + 2, :].rearrange("p b k -> p (b k)"), ident)
                        last.then_inc(S["pp_mm"], 1)
                    m = n - 4
                    if live(m, UNITS):
                        par = gp_of(u - 4)
                        pe.wait_ge(S["av_lo"], m + 1)
                        if past or m >= 1:
                            pe.wait_ge(S["added"], m)
                        if t == 4:
                            pe.wait_ge(S["w_split"], 8 * g + 8)
                        for h in range(GRP):
                            last = mm3(nc, O, aT[0][:, h, :], aT[1][:, h, :], wo[0][:, par, h, :], wo[1][:, par, h, :],
                                       h == 0, h == GRP - 1)
                        last.then_inc(S["o_mm"], 1)
                    m = n - 3
                    if live(m, UNITS):
                        pe.wait_ge(S["pp_copied"], m + 1)
                        if past or m >= 1:
                            pe.wait_ge(S["av_lo"], m)
                        for b2 in range(2):
                            rows = slice(b2 * SEQ, (b2 + 1) * SEQ)
                            last = nc.tensor.matmul(AV[:, b2, :], V[rows, (u - 3) % 4, :], pT[rows, :], start=True, stop=True)
                        last.then_inc(S["av_mm"], 1)

                norm.several_by_tensor(pe, FIRST, rows_due(0)[2])
                pipeline(pe, step, *STEPS)

            @block.scalar
            def _(act):
                def high(part):
                    src, dst, loaded = part
                    act.wait_ge(*loaded)
                    return nc.scalar.activation(dst[0], src, ACT.Copy)

                def first_wo_high(chunks):
                    for p in chunks:
                        high(split_source(p - EC + 2 * TT, 0)[1]).then_inc(S["w_hi"], 1)

                def step(n, u, g):
                    past = not isinstance(n, int)
                    rows, tiles, banks = rows_due(n)
                    for t in tiles:
                        rows.root(act, t, t % 2)
                    m = n - 3
                    if live(m, UNITS):
                        act.wait_ge(S["subbed"], m + 1)
                        s = sm[:, (u - 3) % 2, :, :]
                        nc.scalar.activation(s, s, ACT.Exp).then_inc(S["exped"], 1)
                    m = n - 4
                    if live(m, UNITS):
                        act.wait_ge(S["av_mm"], m + 1)
                        for b2 in range(2):
                            last = nc.scalar.activation(aT[0][:, :, b2 * SEQ:(b2 + 1) * SEQ],
                                                        AV[:, b2, :].rearrange("p (h q) -> p h q", h=GRP), ACT.Copy)
                        last.then_inc(S["av_hi"], 1)
                    if live(n, UNITS):
                        act.wait_ge(S["kv_mm"], n + 1)
                        if past or n >= 1:
                            act.wait_ge(S["qk_mm"], n)
                        if past or n >= 4:
                            act.wait_ge(S["av_mm"], n - 3)
                        nc.scalar.activation(K, KV[:, 0:HD], ACT.Copy)
                        nc.scalar.activation(V[:, u % 4, :], KV[:, HD:], ACT.Copy).then_inc(S["kv_copied"], 1)
                    m = n - 3
                    if live(m, UNITS):
                        act.wait_ge(S["pp_mm"], m + 1)
                        if past or m >= 1:
                            act.wait_ge(S["av_mm"], m)
                        nc.scalar.activation(pT, PP, ACT.Copy).then_inc(S["pp_copied"], 1)
                    for t in tiles:
                        rows.high(act, t, banks[t % 2])
                    if not past and n == 0:
                        first_wo_high(range(2, EC))
                    if live(n + AHEAD, UNITS + EC):
                        if u % 8 == 0 and (past or n >= 8):
                            act.wait_ge(S["qk_mm"], 8 * g)
                        if u % 8 == 4 and (past or n >= 8):
                            act.wait_ge(S["o_mm"], 8 * g)
                        *kv, q_or_o = split_source(u, g + 1)
                        if kv:
                            high(kv[0]).then_inc(S["kv_hi"], 1)
                        high(q_or_o).then_inc(S["w_hi"], 1)

                for t in FIRST:
                    norm.root(act, t, t % 2)
                    for p in (2 * t, 2 * t + 1):
                        high(split_source(p - EC + 2 * TT, 0)[0]).then_inc(S["kv_hi"], 1)
                for t in FIRST:
                    norm.high(act, t, rows_due(0)[2][t % 2])
                first_wo_high(range(2))
                pipeline(act, step, 0, *STEPS[1:])

            @block.vector
            def _(vec):
                norm.await_credits(vec)
                norm.several_by_vector(vec, FIRST, rows_due(0)[2])
                vec.wait_ge(cross.masked, 2)
                vec.wait_ge(cross.table_copied, 4)

                def step(n, u, g):
                    past = not isinstance(n, int)
                    t, j = u % TT, u % 2
                    rows, tiles, banks = rows_due(n)
                    if tiles:
                        if n == UNITS:
                            rows.await_credits(vec)
                            vec.wait_ge(S["sc_mm"], UNITS - 2)
                        if n >= UNITS:
                            vec.wait_ge(S["added"], UNITS - TT + tiles[-1] + 1)
                        rows.pair_by_vector(vec, tiles)
                    m, w = n - 3, (u - 3) % 2
                    if live(m, UNITS):
                        vec.wait_ge(S["exped"], m + 1)
                        nc.vector.reduce_sum(su[:, w, :], sm[:, w, :, :], AX_X).then_inc(S["summed"], 1)
                        vec.wait_ge(S["summed"], m + 1)
                        nc.vector.reciprocal(rc[:, w, :], su[:, w, :]).then_inc(S["recip"], 1)
                    m = n - 4
                    if live(m, UNITS):
                        vec.wait_ge(S["av_hi"], m + 1)
                        for b2 in range(2):
                            q = slice(b2 * SEQ, (b2 + 1) * SEQ)
                            last = nc.vector.tensor_tensor(aT[1][:, :, q], AV[:, b2, :].rearrange("p (h q) -> p h q", h=GRP),
                                                           aT[0][:, :, q].bitcast(F32), ALU.subtract)
                        last.then_inc(S["av_lo"], 1)
                    m = n - 5
                    if live(m, UNITS):
                        vec.wait_ge(S["o_mm"], m + 1)
                        x = sh.X[:, (t - 5) % TT, :]
                        nc.vector.tensor_tensor(x, x, O, ALU.add).then_inc(S["added"], 1)
                    if live(n, UNITS):
                        vec.wait_ge(S["qk_mm"], n + 1)
                        if past or n >= 1:
                            vec.wait_ge(S["roped"], n)
                        pair = slice((t - j) * P, (t - j + 2) * P)
                        for x, count, first in ((QT, 2, 0), (KT, 1, 2 * PAIR)) if j else ((QT, 2, 0),):
                            some = slice(first, first + count * PAIR)

                            def rotate(out, out_rows, table, rows):
                                return nc.vector.tensor_tensor(
                                    out[out_rows, some].rearrange("p (m k) -> p m k", m=count),
                                    x[rows, :].rearrange("p (m k) -> p m k", m=count),
                                    table[rows, pair].unsqueeze(1).broadcast_to([rows.stop - rows.start, count, PAIR]), ALU.mult)

                            rotate(xc, slice(0, P), cosT, slice(0, P))
                            rotate(xs, slice(0, HD // 2), sinT, slice(HD // 2, HD))
                            last = rotate(xs, slice(HD // 2, HD), sinT, slice(0, HD // 2))
                        last.then_inc(S["rope_read"], 1)
                    m, w = n - 2, u % 2
                    if live(m, UNITS):
                        vec.wait_ge(S["sc_mm"], m + 1)
                        if past or m >= 2:
                            vec.wait_ge(S["pp_mm"], m - 1)
                        s = sm[:, w, :, :]
                        nc.vector.scalar_tensor_tensor(
                            s.rearrange("p (h b) k -> p h (b k)", h=2), SC.rearrange("p (h k) -> p h k", h=2), HD ** -0.5,
                            cap[:, (t - 2) % TT, :].unsqueeze(1).broadcast_to([P, 2, P]),
                            ALU.mult, ALU.min).then_inc(S["capped"], 1)
                        vec.wait_ge(S["capped"], m + 1)
                        nc.vector.reduce_max(mx[:, w, :], s, AX_X).then_inc(S["maxed"], 1)
                    for tile in tiles:
                        rows.low(vec, tile, banks[tile % 2])

                pipeline(vec, step, *STEPS)

            @block.gpsimd
            def _(gp):
                next_norm.give_credits(gp)

                def low(part):
                    src, dst, loaded = part
                    return nc.gpsimd.tensor_tensor(dst[1], src, dst[0].bitcast(F32), ALU.subtract)

                def weights_low(n, u, g):
                    if live(n + AHEAD, UNITS + EC):
                        *kv, q_or_o = split_source(u, g + 1)
                        if kv:
                            gp.wait_ge(S["kv_hi"], EC * g + (u % EC + EC + 1))
                            low(kv[0]).then_inc(S["kv_split"], 1)
                        gp.wait_ge(S["w_hi"], n + (AHEAD + 1))
                        low(q_or_o).then_inc(S["w_split"], 1)

                def first_wo_low(chunks):
                    for p in chunks:
                        gp.wait_ge(S["w_hi"], EC + p + 1)
                        low(split_source(p - EC + 2 * TT, 0)[1]).then_inc(S["w_split"], 1)

                def step(n, u, g):
                    past = not isinstance(n, int)
                    j = u % 2
                    m, w = n - 3, (u - 3) % 2
                    if live(m, UNITS):
                        gp.wait_ge(S["recip"], m + 1)
                        s = sm[:, w, :, :]
                        nc.gpsimd.tensor_tensor(s, s, rc[:, w, :].unsqueeze(2).broadcast_to([P, 4, SEQ]),
                                                ALU.mult).then_inc(S["probs"], 1)
                    if past or n != 0:
                        weights_low(n, u, g)
                    if live(n, UNITS):
                        slot = u // 2 % 2
                        gp.wait_ge(S["rope_read"], n + 1)
                        if past or n - j > 2:
                            gp.wait_ge(S["sc_mm"], n - (j + 2))
                        if not past and n == 2:
                            gp.wait_ge(norm.transposed, TT + 2)
                        parts = [x[:, 0:2 * PAIR].rearrange("p (m b q) -> p m b q", m=2, b=4) for x in (xc, xs)]
                        last = nc.gpsimd.tensor_tensor(qT[:, slot, j, :, :].rearrange("p b (m q) -> p m b q", m=2),
                                                       *parts, ALU.add)
                        if j == 1:
                            last = nc.gpsimd.tensor_tensor(kT[:, slot, :], xc[:, 2 * PAIR:], xs[:, 2 * PAIR:], ALU.add)
                        last.then_inc(S["roped"], 1)
                    m, w = n - 2, u % 2
                    if live(m, UNITS):
                        gp.wait_ge(S["maxed"], m + 1)
                        s = sm[:, w, :, :]
                        nc.gpsimd.tensor_tensor(s, s, mx[:, w, :].unsqueeze(2).broadcast_to([P, 4, SEQ]),
                                                ALU.subtract).then_inc(S["subbed"], 1)
                    if not past and n == 0:
                        first_wo_low(range(2, EC))
                        weights_low(n, u, g)

                for p in range(EC):
                    gp.wait_ge(S["kv_hi"], p + 1)
                    low(split_source(p - EC + 2 * TT, 0)[0]).then_inc(S["kv_split"], 1)
                first_wo_low(range(2))
                pipeline(gp, step, 0, *STEPS[1:])


def routed_ffn(nc, sh, d, norm, cross):
    UNITS = EXPERTS * TT
    AHEAD = TT
    STEPS = (0, 8, UNITS - AHEAD, UNITS, 16, TT)
    with ExitStack() as st:
        sb, sem = allocator(nc, st)
        iota = sh.const[:, C_IOTA:C_END]
        raw, w, gw = cross.raw, cross.wq, cross.gw
        lgT = sb("rf_lgT", [EXPERTS, TT * P])
        lg = sb("rf_lg", [P, TT, EXPERTS])
        top = sb("rf_top", [P, TT, EXPERTS])
        at = sb("rf_at", [P, TT, EXPERTS], U32)
        atf = sb("rf_atf", [P, 2, TT])
        wt = sb("rf_wt", [P, 2, TT])
        e2, s2 = sb("rf_e2", [P, TT]), sb("rf_s2", [P, TT])
        we = sb("rf_we", [P, TT, EXPERTS])
        we2 = sb("rf_we2", [P, TT, EXPERTS])

        LG = sh.PS[:, 0, 0:TT * EXPERTS]
        LGT = sh.PS[:EXPERTS, 2:4, :]
        REST = (TT - 2, TT - 1)
        D = sh.PS[:, 4:8, :]
        NT_BANKS = [sh.PS[:, 0, :], sh.PS[:, 1, :]]
        raw_loaded = [sem("rf_raw0"), sem("rf_raw1")]
        names = ("lgT_mm lgT_copied lg_mm lg_copied top_done at_done w_hi w_split d_mm added "
                 "chain exped stored").split()
        S = {x: sem("rf_" + x) for x in names}

        with nc.Block() as block:
            @block.sync
            def _(sp):
                def load(e, p):
                    sp.dma_start(raw[:, p % 2, :], d["experts"][bass.ds(e, 1), p * P:(p + 1) * P, :].rearrange("a p o -> (a p) o")
                                 ).then_inc(raw_loaded[p % 2], 16)

                for p in range(EC):
                    if p >= 2:
                        sp.wait_ge(S["w_split"], p - 1)
                    load(1, p)
                with sp.Fori(2, EXPERTS) as e:
                    for p in range(EC):
                        sp.wait_ge(S["w_split"], 4 * e + (p - 5))
                        load(e, p)
                for t in range(TT):
                    sp.wait_ge(S["added"], UNITS - TT + t + 1)
                    sp.dma_start(d["out"][2 * t:2 * t + 2, :, :].rearrange("b s e -> (b s) e"),
                                 sh.X[:, t, :]).then_inc(S["stored"], 16)
                sp.wait_ge(S["stored"], 16 * TT)

            @block.tensor
            def _(pe):
                def logits(half):
                    tok = slice(half * TT * P // 2, (half + 1) * TT * P // 2)
                    for c in range(EC):
                        last = mm3(nc, LGT[:, half, :], gw[0][:, c, :], gw[1][:, c, :], sh.NTh[:, c, tok], sh.NTl[:, c, tok],
                                   c == 0, c == EC - 1)
                    last.then_inc(S["lgT_mm"], 1)

                logits(0)
                norm.several_by_tensor(pe, REST, NT_BANKS)
                pe.wait_ge(norm.low_done, TT + 1)
                logits(1)
                pe.wait_ge(S["lgT_copied"], 2)
                for t in range(TT):
                    last = nc.tensor.transpose(LG[:, t * EXPERTS:(t + 1) * EXPERTS], lgT[:, t * P:(t + 1) * P],
                                               sh.const[:EXPERTS, C_ID:C_ID + EXPERTS])
                last.then_inc(S["lg_mm"], 1)

                def step(n, u, e):
                    if live(n, UNITS):
                        t, par = u % TT, u // TT
                        if t == 0 and (not isinstance(n, int) or n > 0):
                            pe.wait_ge(S["w_split"], 4 * e)
                        if not isinstance(n, int) or n >= 4:
                            pe.wait_ge(S["added"], n - 3)
                        tok = slice(t * P, (t + 1) * P)
                        for c in range(EC):
                            last = mm3(nc, D[:, t % 4, :], sh.NTh[:, c, tok], sh.NTl[:, c, tok],
                                       w[0][:, par, c, :], w[1][:, par, c, :], c == 0, c == EC - 1)
                        last.then_inc(S["d_mm"], 1)

                pipeline(pe, step, *STEPS)

            @block.scalar
            def _(act):
                for t in REST:
                    norm.root(act, t, t % 2)
                for t in REST:
                    norm.high(act, t, NT_BANKS[t % 2])
                for half in range(2):
                    act.wait_ge(S["lgT_mm"], half + 1)
                    nc.scalar.activation(lgT[:, half * TT * P // 2:(half + 1) * TT * P // 2], LGT[:, half, :],
                                         ACT.Copy).then_inc(S["lgT_copied"], 1)
                act.wait_ge(S["chain"], 1)
                nc.scalar.activation(e2[:], e2[:], ACT.Exp).then_inc(S["exped"], 1)

                def step(n, u, e):
                    p, par = u % TT, (u // TT + 1) % 2
                    if live(n + AHEAD, UNITS) and p < EC:
                        act.wait_ge(raw_loaded[p % 2], 32 * e + 16 * (p // 2 + 1))
                        if p == 0 and (not isinstance(n, int) or n >= TT):
                            act.wait_ge(S["d_mm"], TT * e)
                        nc.scalar.activation(w[0][:, par, p, :], raw[:, p % 2, :], ACT.Copy).then_inc(S["w_hi"], 1)

                pipeline(act, step, *STEPS)

            @block.gpsimd
            def _(gp):
                def step(n, u, e):
                    p, par = u % TT, (u // TT + 1) % 2
                    if live(n + AHEAD, UNITS) and p < EC:
                        gp.wait_ge(S["w_hi"], 4 * e + (p + 1))
                        nc.gpsimd.tensor_tensor(w[1][:, par, p, :], raw[:, p % 2, :], w[0][:, par, p, :].bitcast(F32),
                                                ALU.subtract).then_inc(S["w_split"], 1)

                pipeline(gp, step, *STEPS)

            @block.vector
            def _(vec):
                norm.pair_by_vector(vec, REST)
                for t in REST:
                    norm.low(vec, t, NT_BANKS[t % 2])
                vec.wait_ge(S["lg_mm"], 1)
                nc.vector.tensor_copy(lg[:].rearrange("p t e -> p (t e)"), LG).then_inc(S["lg_copied"], 1)
                vec.wait_ge(S["lg_copied"], 1)
                for t in range(TT):
                    nc.vector.max(top[:, t, :], lg[:, t, :]).then_inc(S["top_done"], 1)
                for t in range(TT):
                    vec.wait_ge(S["top_done"], t + 1)
                    nc.vector.max_index(at[:, t, :], top[:, t, :], lg[:, t, :]).then_inc(S["at_done"], 1)
                nc.vector.tensor_tensor(e2[:], top[:, :, 1], top[:, :, 0], ALU.subtract).then_inc(S["chain"], 1)
                vec.wait_ge(S["exped"], 1)
                nc.vector.tensor_scalar(s2[:], e2[:], 1.0, None, ALU.add).then_inc(S["chain"], 1)
                vec.wait_ge(S["chain"], 2)
                nc.vector.reciprocal(wt[:, 0, :], s2[:]).then_inc(S["chain"], 1)
                vec.wait_ge(S["chain"], 3)
                nc.vector.tensor_tensor(wt[:, 1, :], e2[:], wt[:, 0, :], ALU.mult).then_inc(S["chain"], 1)
                vec.wait_ge(S["at_done"], TT)
                nc.vector.tensor_copy(atf[:], at[:, :, 0:2].rearrange("p t k -> p k t")).then_inc(S["chain"], 1)
                vec.wait_ge(S["chain"], 5)
                for t in range(TT):
                    for k, dst in enumerate((we, we2)):
                        nc.vector.tensor_scalar(dst[:, t, :], iota, atf[:, k, t:t + 1], wt[:, k, t:t + 1],
                                                ALU.is_equal, ALU.mult).then_inc(S["chain"], 1)
                vec.wait_ge(S["chain"], 5 + 2 * TT)
                nc.vector.tensor_tensor(we[:], we[:], we2[:], ALU.add).then_inc(S["chain"], 1)
                vec.wait_ge(S["chain"], 6 + 2 * TT)

                def step(n, u, e):
                    if live(n, UNITS):
                        t = u % TT
                        vec.wait_ge(S["d_mm"], n + 1)
                        x = sh.X[:, t, :]
                        nc.vector.scalar_tensor_tensor(x, D[:, t % 4, :], we[:, t, bass.ds(e, 1)], x,
                                                       ALU.mult, ALU.add).then_inc(S["added"], 1)

                pipeline(vec, step, *STEPS)


def two_layers_kernel(nc, d):
    with ExitStack() as st:
        sh = Shared()
        sh.X = st.enter_context(nc.sbuf_tensor("X", [P, TT, E], F32))
        sh.const = st.enter_context(nc.sbuf_tensor("const", [P, C_END], F32))
        sh.PS = st.enter_context(nc.psum_tensor("PS", [P, 8, 512], F32))
        sh.NTh, sh.NTl, sh.CTh, sh.CTl = (
            st.enter_context(nc.sbuf_tensor(x, [P, EC, TT * P], F32R)) for x in ("NTh", "NTl", "CTh", "CTl"))
        sh.norm_buffers = NormedRows.buffers(allocator(nc, st)[0])
        sh.qT = st.enter_context(nc.sbuf_tensor("qT", [P, 4 * E], F32))
        norm1, norm2, norm3 = (NormedRows(nc, sh, st, name, sh.qT[:, a * E:(a + 2) * E])
                               for name, a in (("n1", 2), ("n2", 2), ("n3", 0)))
        sh.room = st.enter_context(nc.sbuf_tensor("room", [P, GatedInputs.SIZE], F32))
        ffn = GatedInputs(nc, st, sh.room, d)
        with nc.sbuf_tensor("CTX", [P, TT, E], F32) as sh.CTX:
            window_attention(nc, sh, d, norm1, ffn)
        cross = CrossInputs(nc, sh, st, d)
        gated_ffn(nc, sh, norm1, ffn, norm2, cross)
        cross_attention(nc, sh, d, norm2, norm3, cross)
        routed_ffn(nc, sh, d, norm3, cross)


INPUTS = {"x": "x", "ctx_4096": "ctx", "pos_BxS2": "pos", "mask_BxSxS2_ik0": "mask",
          "L0_xattn_Wq": "L0_Wq", "L0_xattn_bq": "L0_bq", "L0_xattn_Wk": "L0_Wk", "L0_xattn_bk": "L0_bk",
          "L0_xattn_Wv": "L0_Wv", "L0_xattn_bv": "L0_bv", "L0_xattn_Wo": "L0_Wo", "L0_xattn_bo": "L0_bo",
          "L0_ffn_Wg": "L0_Wg", "L0_ffn_Wu": "L0_Wu", "L0_ffn_Wd": "L0_Wd",
          "L0_ffn_ag": "L0_ag", "L0_ffn_au": "L0_au", "L0_ffn_ad": "L0_ad",
          "L1_xattn_Wq": "L1_Wq", "L1_xattn_Wk": "L1_Wk", "L1_xattn_Wv": "L1_Wv", "L1_xattn_Wo": "L1_Wo",
          "L1_ffn_gate_w": "gate_w", "L1_ffn_expert_w": "experts"}


def kernel(**inputs):
    import concourse.bacc as bacc
    from concourse.bass_utils import run_bass_kernel_spmd

    nc = bacc.Bacc("TRN2", target_bir_lowering=False, num_devices=1)
    arrays, d = {}, {}
    for name, short in INPUTS.items():
        arrays["in_" + short] = np.ascontiguousarray(inputs[name])
    arrays["in_consts"] = shape_constants()
    arrays["in_rotary"] = rotary_table()
    for name, a in arrays.items():
        d[name[3:]] = nc.dram_tensor(name, a.shape, mybir.dt.from_np(a.dtype), kind="ExternalInput").ap()
    d["out"] = nc.dram_tensor("out", (BATCH, SEQ, E), F32, kind="ExternalOutput").ap()
    two_layers_kernel(nc, d)
    r = run_bass_kernel_spmd(nc, [arrays], core_ids=[0])
    return r.results[0]["out"]
```
